# Optimizing a Trainium2 kernel written in Bass

```python
import numpy as np
import jax
import jax.numpy as jnp

def _softmax(x, axis=-1):
    return jax.nn.softmax(x, axis=axis)

def _gelu(x):
    return jax.nn.gelu(x, approximate=True)

def _silu(x):
    return jax.nn.silu(x)

def _sigmoid(x):
    return jax.nn.sigmoid(x)

def _layernorm(x, axis=-1, eps=1e-05):
    m = jnp.mean(x, axis=axis, keepdims=True)
    v = jnp.var(x, axis=axis, keepdims=True)
    return (x - m) / jnp.sqrt(v + eps)

def _scatter_add(tgt, idx, src, axis=0):
    return tgt.at[idx].add(src)

def _segment_sum(src, seg, n):
    return jax.ops.segment_sum(src, seg, n)
kernel_name = 'mk_gnn_ffn_d2_gnn_r32_5b02e3'

def setup_inputs(seed: int=0):
    np.random.seed(seed)
    _w = jnp.asarray

    def _rec_inputs():
        import jax
        import jax.numpy as jnp
        _gk = jax.random.key(seed)
        x = -0.0005963 + 1.001 * jax.random.normal(jax.random.fold_in(_gk, 1), (96, 1024), jnp.float32)
        src = jax.random.randint(jax.random.fold_in(_gk, 2), (3072,), 0, 96, jnp.int32)
        dst = jax.random.randint(jax.random.fold_in(_gk, 3), (3072,), 0, 96, jnp.int32)
        _o = jnp.argsort(dst, stable=True)
        src = src[_o]
        dst = dst[_o]
        edge_type_5 = jax.random.randint(jax.random.fold_in(_gk, 12), (3072,), 0, 5, jnp.int32)
        return (x, src, dst, edge_type_5)
    x, src, dst, edge_type_5 = _rec_inputs()

    def _L0_gnn_setup():
        import jax, jax.numpy as jnp
        import numpy as np
        N = 96
        E = 3072
        IN_F = 1024
        OUT_F = 1024
        H = 16
        D = OUT_F // H
        NUM_ETYPES = 4

        def _build_mask(edge_index, edge_type, edge_type_weights, dtype):
            src, dst = (edge_index[0], edge_index[1])
            w = jax.nn.softplus(edge_type_weights)
            mask = jnp.full((N, N), -jnp.inf, dtype=dtype)
            mask = mask.at[src, dst].set(w[edge_type - 1])
            diag = jnp.diagonal(mask)
            idx = jnp.arange(N)
            mask = mask.at[idx, idx].set(jnp.where(jnp.isneginf(diag), w[3], diag))
            return mask
        key = jax.random.key(seed)
        ks = jax.random.split(key, 20)
        p = lambda k, shape: jax.random.normal(k, shape, dtype=jnp.float32) * 0.02
        return {'x': jax.random.normal(ks[0], (N, IN_F), dtype=jnp.float32), 'edge_index': jax.random.randint(ks[1], (2, E), 0, N), 'edge_type': jax.random.randint(ks[2], (E,), 1, NUM_ETYPES + 1), 'edge_type_weights': jnp.ones((NUM_ETYPES,), jnp.float32) + 0.1 * jax.random.normal(ks[3], (NUM_ETYPES,), dtype=jnp.float32), 'wq': p(ks[4], (OUT_F, IN_F)), 'bq': p(ks[5], (OUT_F,)), 'wk': p(ks[6], (OUT_F, IN_F)), 'bk': p(ks[7], (OUT_F,)), 'wv': p(ks[8], (OUT_F, IN_F)), 'bv': p(ks[9], (OUT_F,)), 'wiq': p(ks[10], (OUT_F, OUT_F)), 'biq': p(ks[11], (OUT_F,)), 'wik': p(ks[12], (OUT_F, OUT_F)), 'bik': p(ks[13], (OUT_F,)), 'wiv': p(ks[14], (OUT_F, OUT_F)), 'biv': p(ks[15], (OUT_F,)), 'wo': p(ks[16], (OUT_F, OUT_F)), 'bo': p(ks[17], (OUT_F,))}
    _L0_gnn_all = _L0_gnn_setup()
    _L0_gnn_in = {k: v for k, v in _L0_gnn_all.items() if k in ('edge_type_weights', 'wq', 'bq', 'wk', 'bk', 'wv', 'bv', 'wiq', 'biq', 'wik', 'bik', 'wiv', 'biv', 'wo', 'bo')}
    del _L0_gnn_all

    def _L0_ffn_setup():
        import jax, jax.numpy as jnp
        import numpy as np
        E = 8
        K = 2
        D = 1024
        H = 2736
        B, S = (2, 64)

        def _moe_forward(x, centroid, Wg, bg, W1, b1, W2, b2):
            T = x.shape[0] * x.shape[1]
            xs = x.reshape(T, D)
            d2 = jnp.sum(xs * xs, axis=-1, keepdims=True) + jnp.sum(centroid * centroid, axis=-1)[None, :] - 2.0 * (xs @ centroid.T)
            dist = jnp.sqrt(jnp.maximum(d2, 1e-12))
            w, sel = jax.lax.top_k(dist, K)
            w = jax.nn.softmax(w.astype(jnp.float32), axis=1).astype(x.dtype)
            we = jnp.zeros((T, E), dtype=x.dtype).at[jnp.arange(T)[:, None], sel].add(w)
            out = jnp.zeros_like(xs)
            for e in range(E):
                h = jax.nn.silu(xs @ Wg[e] + bg[e]) * (xs @ W1[e] + b1[e])
                out = out + we[:, e:e + 1] * (h @ W2[e] + b2[e])
            return out.reshape(x.shape)
        key = jax.random.key(seed)
        ks = jax.random.split(key, 9)
        scale = 0.02
        return {'x': jax.random.normal(ks[0], (B, S, D), dtype=jnp.float32), 'centroid': jax.random.normal(ks[1], (E, D), dtype=jnp.float32), 'Wg': jax.random.normal(ks[2], (E, D, H), dtype=jnp.float32) * scale, 'bg': jnp.zeros((E, H), dtype=jnp.float32), 'W1': jax.random.normal(ks[3], (E, D, H), dtype=jnp.float32) * scale, 'b1': jnp.zeros((E, H), dtype=jnp.float32), 'W2': jax.random.normal(ks[4], (E, H, D), dtype=jnp.float32) * scale, 'b2': jnp.zeros((E, D), dtype=jnp.float32)}
    _L0_ffn_all = _L0_ffn_setup()
    _L0_ffn_in = {k: v for k, v in _L0_ffn_all.items() if k in ('centroid', 'Wg', 'bg', 'W1', 'b1', 'W2', 'b2')}
    del _L0_ffn_all

    def _L1_gnn_setup():
        import jax, jax.numpy as jnp
        import numpy as np
        N = 625
        E = 10000
        D_IN = 1024
        D_OUT = 1024
        key = jax.random.key(seed)
        k1, k2, k3, k4 = jax.random.split(key, 4)
        x = jax.random.normal(k1, (N, D_IN), dtype=jnp.float32)
        edge_index = jax.random.randint(k2, (2, E), 0, N, dtype=jnp.int64)
        W = jax.random.normal(k3, (D_OUT, D_IN), dtype=jnp.float32) * (1.0 / np.sqrt(D_IN))
        b = jax.random.normal(k4, (D_OUT,), dtype=jnp.float32) * 0.01
        return {'x': x, 'edge_index': edge_index, 'W': W, 'b': b}
    _L1_gnn_all = _L1_gnn_setup()
    _L1_gnn_in = {k: v for k, v in _L1_gnn_all.items() if k in ('W', 'b')}
    del _L1_gnn_all

    def _L1_ffn_setup():
        import jax, jax.numpy as jnp
        import numpy as np
        INT8_MAX = 127.0

        def _absmax_scale(x, axes):
            amax = jnp.max(jnp.abs(x), axis=axes, keepdims=True)
            return jnp.maximum(amax, 1e-12) / INT8_MAX
        key = jax.random.key(seed)
        k1, k2 = jax.random.split(key)
        lhs = jax.random.normal(k1, (4, 256, 1024), dtype=jnp.float32)
        rhs = jax.random.normal(k2, (1024, 1024), dtype=jnp.float32)
        return {'lhs': lhs, 'rhs': rhs}
    _L1_ffn_all = _L1_ffn_setup()
    _L1_ffn_in = {k: v for k, v in _L1_ffn_all.items() if k in ('rhs',)}
    del _L1_ffn_all
    return {'x': x, 'src': src, 'dst': dst, 'edge_type_5': edge_type_5, 'L0_gnn_edge_type_weights': _L0_gnn_in['edge_type_weights'], 'L0_gnn_wq': _L0_gnn_in['wq'], 'L0_gnn_bq': _L0_gnn_in['bq'], 'L0_gnn_wk': _L0_gnn_in['wk'], 'L0_gnn_bk': _L0_gnn_in['bk'], 'L0_gnn_wv': _L0_gnn_in['wv'], 'L0_gnn_bv': _L0_gnn_in['bv'], 'L0_gnn_wiq': _L0_gnn_in['wiq'], 'L0_gnn_biq': _L0_gnn_in['biq'], 'L0_gnn_wik': _L0_gnn_in['wik'], 'L0_gnn_bik': _L0_gnn_in['bik'], 'L0_gnn_wiv': _L0_gnn_in['wiv'], 'L0_gnn_biv': _L0_gnn_in['biv'], 'L0_gnn_wo': _L0_gnn_in['wo'], 'L0_gnn_bo': _L0_gnn_in['bo'], 'L0_ffn_centroid': _L0_ffn_in['centroid'], 'L0_ffn_Wg': _L0_ffn_in['Wg'], 'L0_ffn_bg': _L0_ffn_in['bg'], 'L0_ffn_W1': _L0_ffn_in['W1'], 'L0_ffn_b1': _L0_ffn_in['b1'], 'L0_ffn_W2': _L0_ffn_in['W2'], 'L0_ffn_b2': _L0_ffn_in['b2'], 'L1_gnn_W': _L1_gnn_in['W'], 'L1_gnn_b': _L1_gnn_in['b'], 'L1_ffn_rhs': _L1_ffn_in['rhs']}

def reference(x, src, dst, edge_type_5, L0_gnn_edge_type_weights, L0_gnn_wq, L0_gnn_bq, L0_gnn_wk, L0_gnn_bk, L0_gnn_wv, L0_gnn_bv, L0_gnn_wiq, L0_gnn_biq, L0_gnn_wik, L0_gnn_bik, L0_gnn_wiv, L0_gnn_biv, L0_gnn_wo, L0_gnn_bo, L0_ffn_centroid, L0_ffn_Wg, L0_ffn_bg, L0_ffn_W1, L0_ffn_b1, L0_ffn_W2, L0_ffn_b2, L1_gnn_W, L1_gnn_b, L1_ffn_rhs):
    import jax
    import jax.numpy as jnp

    def _L0_gnn_ref(x, edge_index, edge_type, edge_type_weights, wq, bq, wk, bk, wv, bv, wiq, biq, wik, bik, wiv, biv, wo, bo):
        import jax, jax.numpy as jnp
        import numpy as np
        N = 96
        E = 3072
        IN_F = 1024
        OUT_F = 1024
        H = 16
        D = OUT_F // H
        NUM_ETYPES = 4

        def _build_mask(edge_index, edge_type, edge_type_weights, dtype):
            src, dst = (edge_index[0], edge_index[1])
            w = jax.nn.softplus(edge_type_weights)
            mask = jnp.full((N, N), -jnp.inf, dtype=dtype)
            mask = mask.at[src, dst].set(w[edge_type - 1])
            diag = jnp.diagonal(mask)
            idx = jnp.arange(N)
            mask = mask.at[idx, idx].set(jnp.where(jnp.isneginf(diag), w[3], diag))
            return mask
        q = x @ wq.T + bq
        k = x @ wk.T + bk
        v = x @ wv.T + bv
        q2 = (q @ wiq.T + biq).reshape(N, H, D).transpose(1, 0, 2)
        k2 = (k @ wik.T + bik).reshape(N, H, D).transpose(1, 0, 2)
        v2 = (v @ wiv.T + biv).reshape(N, H, D).transpose(1, 0, 2)
        mask = _build_mask(edge_index, edge_type, edge_type_weights, x.dtype)
        scale = 1.0 / np.sqrt(D).astype(np.float32)
        scores = jnp.einsum('hnd,hmd->hnm', q2, k2) * scale + mask[None]
        attn = jax.nn.softmax(scores, axis=-1)
        out = jnp.einsum('hnm,hmd->hnd', attn, v2)
        out = out.transpose(1, 0, 2).reshape(N, OUT_F)
        return out @ wo.T + bo

    def _L0_ffn_ref(x, centroid, Wg, bg, W1, b1, W2, b2):
        import jax, jax.numpy as jnp
        import numpy as np
        E = 8
        K = 2
        D = 1024
        H = 2736
        B, S = (2, 64)

        def _moe_forward(x, centroid, Wg, bg, W1, b1, W2, b2):
            T = x.shape[0] * x.shape[1]
            xs = x.reshape(T, D)
            d2 = jnp.sum(xs * xs, axis=-1, keepdims=True) + jnp.sum(centroid * centroid, axis=-1)[None, :] - 2.0 * (xs @ centroid.T)
            dist = jnp.sqrt(jnp.maximum(d2, 1e-12))
            w, sel = jax.lax.top_k(dist, K)
            w = jax.nn.softmax(w.astype(jnp.float32), axis=1).astype(x.dtype)
            we = jnp.zeros((T, E), dtype=x.dtype).at[jnp.arange(T)[:, None], sel].add(w)
            out = jnp.zeros_like(xs)
            for e in range(E):
                h = jax.nn.silu(xs @ Wg[e] + bg[e]) * (xs @ W1[e] + b1[e])
                out = out + we[:, e:e + 1] * (h @ W2[e] + b2[e])
            return out.reshape(x.shape)
        return _moe_forward(x, centroid, Wg, bg, W1, b1, W2, b2)

    def _L1_gnn_ref(x, edge_index, W, b):
        import jax, jax.numpy as jnp
        import numpy as np
        N = 625
        E = 10000
        D_IN = 1024
        D_OUT = 1024
        num_nodes = x.shape[0]
        self_idx = jnp.arange(num_nodes, dtype=edge_index.dtype)
        ei = jnp.concatenate([edge_index, jnp.stack([self_idx, self_idx], axis=0)], axis=1)
        row, col = (ei[0], ei[1])
        h = jnp.einsum('nd,od->no', x, W) + b
        deg = jnp.zeros((num_nodes,), dtype=h.dtype).at[row].add(1.0)
        deg_inv_sqrt = deg ** (-0.5)
        norm = deg_inv_sqrt[row] * deg_inv_sqrt[col]
        msg = norm[:, None] * h[col]
        out = jax.ops.segment_sum(msg, row, num_segments=num_nodes)
        return out

    def _L1_ffn_ref(lhs, rhs):
        import jax, jax.numpy as jnp
        import numpy as np
        INT8_MAX = 127.0

        def _absmax_scale(x, axes):
            amax = jnp.max(jnp.abs(x), axis=axes, keepdims=True)
            return jnp.maximum(amax, 1e-12) / INT8_MAX
        lhs_scale = _absmax_scale(lhs, (2,))
        rhs_scale = _absmax_scale(rhs, (0,))
        q_lhs = jnp.clip(jnp.round(lhs / lhs_scale), -INT8_MAX, INT8_MAX).astype(jnp.int8)
        q_rhs = jnp.clip(jnp.round(rhs / rhs_scale), -INT8_MAX, INT8_MAX).astype(jnp.int8)
        acc = jax.lax.dot_general(q_lhs, q_rhs, (((2,), (0,)), ((), ())), preferred_element_type=jnp.int32)
        return acc.astype(jnp.float32) * lhs_scale * rhs_scale
    edge_index = jnp.stack([src, dst])
    x = x + _L0_gnn_ref(_layernorm(x, axis=-1), edge_index, edge_type_5, L0_gnn_edge_type_weights, L0_gnn_wq, L0_gnn_bq, L0_gnn_wk, L0_gnn_bk, L0_gnn_wv, L0_gnn_bv, L0_gnn_wiq, L0_gnn_biq, L0_gnn_wik, L0_gnn_bik, L0_gnn_wiv, L0_gnn_biv, L0_gnn_wo, L0_gnn_bo)
    x = x + _L0_ffn_ref(_layernorm(x, axis=-1)[None], L0_ffn_centroid, L0_ffn_Wg, L0_ffn_bg, L0_ffn_W1, L0_ffn_b1, L0_ffn_W2, L0_ffn_b2)[0]
    x = x + _L1_gnn_ref(_layernorm(x, axis=-1), edge_index, L1_gnn_W, L1_gnn_b)
    x = x + _L1_ffn_ref(_layernorm(x, axis=-1)[None], L1_ffn_rhs)[0]
    return x

_drawn_inputs = setup_inputs


def setup_inputs(seed=0):
    import zlib

    import numpy as np

    out = dict(_drawn_inputs(seed))
    spreads = {'L0_ffn_bg': (0.0, 0.1), 'L0_ffn_b1': (0.0, 0.268), 'L0_ffn_b2': (0.0, 0.1)}
    factors = {'L0_gnn_edge_type_weights': 10.995,
     'L0_gnn_wq': 3.145,
     'L0_gnn_bq': 8.0,
     'L0_gnn_wk': 4.884,
     'L0_gnn_bk': 64.0,
     'L0_gnn_bv': 4.238,
     'L0_gnn_wiq': 4.906,
     'L0_gnn_biq': 8.0,
     'L0_gnn_wik': 3.288,
     'L0_gnn_bik': 64.0,
     'L1_gnn_b': 4.721,
     'L0_gnn_biv': 2.873}
    for name, (base, spread) in spreads.items():
        noise = np.random.default_rng([zlib.crc32(name.encode()), seed]).standard_normal(out[name].shape)
        drawn = base * np.exp(spread * noise) if base else spread * noise
        out[name] = jnp.asarray(drawn.astype(out[name].dtype))
    for name, factor in factors.items():
        out[name] = (out[name] * factor).astype(out[name].dtype)
    return out
```

```python
import numpy as np
import concourse.bass as bass
from concourse import mybir
from contextlib import ExitStack


def gnn_moe_gcn_int8_kernel(nc, x_in, src_in, dst_in, etype_in, etw_in,
                            wq, bq, wk, bk, wv, bv, wiq, biq, wik, bik, wiv, biv, wo, bo,
                            centroid, Wg, bg, W1, b1, W2, b2, gcn_w, gcn_b, rhs_in, out):
    F32, BF16, I32 = mybir.dt.float32, mybir.dt.bfloat16, mybir.dt.int32
    ALU, ACT, AX = mybir.AluOpType, mybir.ActivationFunctionType, mybir.AxisListType

    P = 128
    N, D = x_in.shape
    KD = D // P
    HALF = D // 2
    HC = HALF // P
    NE, _, FF = Wg.shape
    FC = -(-FF // P)
    CW = [min(P, FF - P * c) for c in range(FC)]
    EDGES = src_in.shape[0]
    EC = EDGES // P
    DH = 64
    HEADS = D // DH
    NTYPES = etw_in.shape[0]
    LN_EPS, NEG, INT8_MAX = 1e-5, -1e30, 127.0
    RMAX = bass.bass_isa.ReduceOp.max
    ROUND = 1.5 * 2.0 ** 23
    SCALE = 1.0 / float(np.sqrt(np.float32(DH)))

    SLOTS, SLOT = 6, HC * D
    GROUPS = [range(0, 4), range(4, 8), range(8, 12), range(12, 16), range(16, 19), range(19, 22)]
    GATE, UP, DOWN = range(3)

    def slot_of(g, kind):
        return 3 * (g % 2) + kind

    def group_width(g):
        return sum(CW[c] for c in GROUPS[g])

    def parts(g, kind):
        return 2 if kind == DOWN and group_width(g) % P else 1

    def slot_parts(s):
        return sum(parts(g, k) for g in range(len(GROUPS)) for k in range(3) if slot_of(g, k) == s)

    def slot_parts_until(g, kind):
        return sum(parts(h, kind) for h in range(g + 1) if slot_of(h, kind) == slot_of(g, kind))

    SQUARES = [wq, wiq, wk, wik, wv, wiv, wo, gcn_w]
    LQ, LIQ, LK, LIK, LV, LIV, LO, LG = range(8)
    HALVES = 2 * len(SQUARES)

    def half_uses(s):
        return len(range(s, HALVES, SLOTS))

    TGROUPS = []

    def add_groups(name, n, first=0):
        for k in range(n):
            TGROUPS.append(((name, k), "va"[(first + k) % 2]))

    add_groups("cols", 1)
    add_groups("edges", 1, 1)
    add_groups("x0", 2)
    add_groups(("w", 0, 0), KD)
    add_groups(("w", 0, 1), KD)
    for m in range(1, LO + 1):
        add_groups(("w", m, 0), KD)
        add_groups(("w", m, 1), KD)
    add_groups("probs", 4)
    add_groups("x1", 2)
    add_groups("we", 1)
    add_groups(("w", LG, 0), KD)
    add_groups(("w", LG, 1), KD)
    add_groups("q", 2)
    TINDEX = {name: i for i, (name, _) in enumerate(TGROUPS)}
    TB = 4

    def taken(i):
        who = TGROUPS[i][1]
        return who, sum(w == who for _, w in TGROUPS[:i + 1])

    VECTORS = [bq, biq, bk, bik, bv, biv]
    C_BG = len(VECTORS) * KD
    C_B1 = C_BG + NE * FC
    C_CEN = C_B1 + NE * FC
    NCOLS = C_CEN + KD * NE

    ctx = ExitStack()
    with ctx:
        def sb(name, shape, dt=F32):
            return ctx.enter_context(nc.sbuf_tensor(name, shape, dt))

        def sem(name):
            return ctx.enter_context(nc.semaphore(name))

        ring = sb("ring", [P, SLOTS, SLOT])
        wt = sb("wt", [P, 2, KD, HALF])
        arena = sb("arena", [P, 16000])
        x = sb("x", [N, D])
        aT = sb("aT", [P, KD, N])
        cols = sb("cols", [P, NCOLS])
        we_b = sb("we_b", [P, NE, N])
        silu = sb("silu", [P, 2, N])
        hid = sb("hid", [P, 2, N])
        hT = sb("hT", [P, 2, N])
        ident = sb("ident", [P, P])
        ident_b = sb("ident_b", [P, P], BF16)
        ones_b = sb("ones_b", [P, 1], BF16)
        adjT = sb("adjT", [N, N])
        dinv = sb("dinv", [N, 1])
        ones = sb("ones", [P, P])
        stats = sb("stats", [N, 12])
        mv = sb("mv", [N, 4])
        dev = sb("dev", [N, 1])
        sc = sb("sc", [N, 8])

        at = [0]

        def carve(parts_, shape, dt=F32):
            n = int(np.prod(shape))
            words = n if dt != BF16 else -(-n // 2)
            v = arena[0:parts_, at[0]:at[0] + words]
            at[0] += words
            if dt != F32:
                v = v.bitcast(dt)
            return v[:, 0:n]

        ln = carve(N, [D])
        linT = carve(P, [KD * N]).rearrange("p (k n) -> p k n", n=N)
        q2T = carve(P, [KD * N]).rearrange("p (k n) -> p k n", n=N)
        k2T = carve(P, [KD * N]).rearrange("p (k n) -> p k n", n=N)
        v2 = carve(N, [D])
        S = carve(N, [HEADS * N]).rearrange("p (h m) -> p h m", m=N)
        PT = carve(N, [HEADS * N]).rearrange("p (h m) -> p h m", m=N)
        mask = carve(N, [N])
        b2_sb = carve(NE, [D])
        bo_row = carve(1, [D])
        src1h = carve(P, [EC * N], BF16).rearrange("p (c n) -> p c n", n=N)
        dst1h = carve(P, [EC * N], BF16).rearrange("p (c n) -> p c n", n=N)
        dcode = carve(P, [EC * N], BF16).rearrange("p (c n) -> p c n", n=N)
        e_int = carve(EC, [3 * P], I32).rearrange("p (a j) -> p a j", j=P)
        e_row = carve(EC, [4 * P]).rearrange("p (a j) -> p a j", j=P)
        eT = carve(P, [4 * EC]).rearrange("p (a c) -> p a c", c=EC)
        early_max = at[0]
        at[0] = (ln.shape[1] + KD * N)
        vec_rows = carve(C_BG, [P])
        bg_rows = carve(FC, [NE * P]).rearrange("p (e j) -> p e j", j=P)
        b1_rows = carve(FC, [NE * P]).rearrange("p (e j) -> p e j", j=P)
        cen = carve(NE, [D])
        sq = carve(NE, [D])
        at[0] = max(early_max, at[0])
        iota_n = carve(P, [N])
        code_base = carve(P, [EC])
        tri = carve(P, [P])
        junk = carve(P, [4 * P], BF16).rearrange("p (c j) -> p c j", j=P)
        dup = carve(P, [EC])
        code = carve(P, [2 * EC]).rearrange("p (a c) -> p a c", c=EC)
        best = carve(N, [7 * N]).rearrange("p (a m) -> p a m", m=N)
        best_i = carve(N, [N], I32)
        etw = carve(N, [NTYPES])
        spw = carve(N, [3 * NTYPES]).rearrange("p (a t) -> p a t", t=NTYPES)
        mx = carve(N, [3 * HEADS]).rearrange("p (a h) -> p a h", h=HEADS)
        dist = carve(N, [8 * NE]).rearrange("p (a e) -> p a e", e=NE)
        cmp = carve(N, [3 * NE * NE]).rearrange("p (a e f) -> p a e f", e=NE, f=NE)
        weT = carve(NE, [N])
        csq = carve(NE, [2])
        outT = linT
        assert at[0] <= arena.shape[1]
        at[0] = 0
        rhs = carve(P, [KD * D]).rearrange("p (k n) -> p k n", n=D)
        rhs_q = carve(P, [KD * D], BF16).rearrange("p (k n) -> p k n", n=D)
        rscale = carve(P, [D])
        gcn_row = carve(1, [D])
        rmax = carve(P, [P])
        rtmp = carve(P, [KD * P]).rearrange("p (k n) -> p k n", n=P)
        rinv = carve(P, [2 * P]).rearrange("p (a n) -> p a n", n=P)
        assert at[0] <= arena.shape[1], at[0]

        yT = ring[:, 0, 0:KD * N].rearrange("p (k n) -> p k n", n=N)
        ln_t = ring[0:N, 1, 0:D]
        zT = ring[:, 2, 0:KD * N].rearrange("p (k n) -> p k n", n=N)
        row_sum = ring[0:1, 3, 0:N]
        qf = ring[0:N, 4, 0:D]
        qb = ring[0:N, 4, D:D + D // 2].bitcast(BF16)
        qT = ring[:, 4, 2 * D:2 * D + KD * N // 2].bitcast(BF16).rearrange("p (k n) -> p k n", n=N)
        res = ring[0:N, 5, 0:D]

        bank = [ctx.enter_context(nc.psum_tensor(f"bank{i}", [P, HALF], F32)) for i in range(8)]
        tbank, obank, sbank = bank[0:4], bank[4:6], bank[6:8]
        gate_bank, up_bank, acc_bank = tbank[0:2], tbank[2:4], obank

        s_const = sem("s_const")
        s_rows0 = sem("s_rows0")
        s_x = sem("s_x")
        s_edges = sem("s_edges")
        s_rows = sem("s_rows")
        s_small = sem("s_small")
        s_late = sem("s_late")
        s_full = [sem(f"s_full{s}") for s in range(SLOTS)]
        s_t = sem("s_t")
        s_tv = sem("s_tv")
        s_ta = sem("s_ta")
        s_o = sem("s_o")
        s_od = sem("s_od")
        s_s = sem("s_s")
        s_sd = sem("s_sd")
        s_dve = sem("s_dve")
        s_pool = sem("s_pool")
        s_act = sem("s_act")
        s_var = sem("s_var")
        s_dev = sem("s_dev")
        s_ln = sem("s_ln")
        s_erow = sem("s_erow")
        s_1h = sem("s_1h")
        s_cval = sem("s_cval")
        s_dcode = sem("s_dcode")
        s_spe = sem("s_spe")
        s_spv = sem("s_spv")
        s_sub = sem("s_sub")
        s_exp = sem("s_exp")
        s_prob = sem("s_prob")
        s_adj = sem("s_adj")
        s_csq = sem("s_csq")
        s_xsq = sem("s_xsq")
        s_gd = sem("s_gd")
        s_ga = sem("s_ga")
        s_we = sem("s_we")
        s_init = sem("s_init")
        s_gate = sem("s_gate")
        s_up = sem("s_up")
        s_gfree = sem("s_gfree")
        s_ufree = sem("s_ufree")
        s_hid = sem("s_hid")
        s_h = sem("s_h")
        s_hfree = sem("s_hfree")
        s_rmax = sem("s_rmax")
        s_rall = sem("s_rall")
        s_rscale = sem("s_rscale")
        s_rinv = sem("s_rinv")
        s_rq = sem("s_rq")
        s_y = sem("s_y")
        s_z = sem("s_z")
        s_q = sem("s_q")
        s_res = sem("s_res")
        s_out = sem("s_out")

        block = ctx.enter_context(nc.Block())

        S_KEY, S_ADJ, S_CODE, S_SC, S_PV, S_DIST, S_WE, S_Y, S_Z, S_ROW = 0, 6, 7, 13, 17, 19, 20, 22, 24, 26
        O_GCN, O_INT8 = 2 * LG, 2 * LG + 2
        CHUNKS = NE * FC

        def wait_taken(eng, name):
            who, n = taken(TINDEX[name])
            eng.wait_ge(s_tv if who == "v" else s_ta, n)

        def wait_x_stage(eng, n):
            wait_taken(eng, (n, 0))
            wait_taken(eng, (n, 1))

        @block.sync
        def _(sp):
            sp.dma_start(x[:, :], x_in).then_inc(s_x, 16)
            for i in range(HALVES):
                m, hf, s = i // 2, i % 2, i % SLOTS
                if i >= SLOTS:
                    sp.wait_ge(s_t, TINDEX[(("w", (i - SLOTS) // 2, (i - SLOTS) % 2), KD - 1)] + 1)
                sp.dma_start(ring[:, s, :].rearrange("p (c i) -> p c i", i=D),
                             SQUARES[m][hf * HALF:(hf + 1) * HALF, :].rearrange("(c p) i -> p c i", p=P)
                             ).then_inc(s_full[s], 16)

            def load_group(e, g):
                c0, w = GROUPS[g][0] * P, group_width(g)
                for kind, src in ((GATE, Wg), (UP, W1)):
                    s = slot_of(g, kind)
                    release(e, g, kind)
                    sp.dma_start(ring[:, s, 0:KD * w].rearrange("p (k w) -> p k w", w=w),
                                 src[e, :, c0:c0 + w].rearrange("(k p) w -> p k w", p=P)).then_inc(s_full[s], 16)
                s = slot_of(g, DOWN)
                release(e, g, DOWN)
                whole = w // P
                dst = ring[:, s, :].rearrange("p (c d) -> p c d", d=D)
                sp.dma_start(dst[:, 0:whole, :], W2[e, c0:c0 + whole * P, :].rearrange("(c p) d -> p c d", p=P)
                             ).then_inc(s_full[s], 16)
                if w % P:
                    sp.dma_start(dst[0:w % P, whole, :], W2[e, c0 + whole * P:c0 + w, :]).then_inc(s_full[s], 16)

            def release(e, g, kind):
                if isinstance(e, int) and g < 2:
                    i = max(range(slot_of(g, kind), HALVES, SLOTS))
                    sp.wait_ge(s_t, TINDEX[(("w", i // 2, i % 2), KD - 1)] + 1)
                else:
                    before = GROUPS[g - 2][-1] + 1 - (FC if g < 2 else 0)
                    done = {GATE: s_gate, UP: s_up, DOWN: s_hfree}[kind]
                    sp.wait_ge(done, e * FC + before + (2 if kind == DOWN else 0))

            for g in range(len(GROUPS)):
                load_group(0, g)
            with sp.Fori(1, NE) as e:
                for g in range(len(GROUPS)):
                    load_group(e, g)
            for hf in range(2):
                sp.wait_ge(s_res, hf + 1)
                sp.dma_start(out[:, hf * HALF:(hf + 1) * HALF], res[:, hf * HALF:(hf + 1) * HALF]).then_inc(s_out, 16)
            sp.wait_ge(s_out, 32)

        @block.gpsimd
        def _(pool):
            chain = [0]

            def link(ins):
                chain[0] += 1
                ins.then_inc(s_pool, 1)
                pool.wait_ge(s_pool, chain[0])

            nc.gpsimd.memset(bg_rows, 0.0).then_inc(s_rows0, 1)
            nc.gpsimd.memset(b1_rows, 0.0).then_inc(s_rows0, 1)
            link(nc.gpsimd.memset(ident[:, :], 0.0))
            link(nc.gpsimd.affine_select(out=ident[:, :], in_=ident[:, :], compare_op=ALU.not_equal, fill=1.0,
                                         base=0, pattern=[[-1, P]], channel_multiplier=1))
            link(nc.gpsimd.tensor_copy(ident_b[:, :], ident[:, :]))
            nc.gpsimd.memset(ones_b[:, :], 1.0).then_inc(s_const, 1)
            nc.gpsimd.memset(ones[:, :], 1.0).then_inc(s_const, 1)
            pool.wait_ge(s_const, 2)
            nc.gpsimd.affine_select(out=tri, in_=ones[:, :], compare_op=ALU.is_gt, fill=0.0,
                                    base=0, pattern=[[1, P]], channel_multiplier=-1).then_inc(s_const, 1)
            low = cmp[:, 2, :, :]
            nc.gpsimd.affine_select(out=low, in_=ones[0:N, 0:NE * NE].rearrange("p (e f) -> p e f", f=NE),
                                    compare_op=ALU.is_gt, fill=0.0, base=0, pattern=[[1, NE], [-1, NE]],
                                    channel_multiplier=0).then_inc(s_const, 1)
            nc.gpsimd.iota(iota_n, [[1, N]], base=0, channel_multiplier=0,
                           allow_small_or_imprecise_dtypes=True).then_inc(s_const, 1)
            nc.gpsimd.iota(code_base, [[8, EC]], base=8, channel_multiplier=0,
                           allow_small_or_imprecise_dtypes=True).then_inc(s_const, 1)
            pool.wait_ge(s_const, 6)
            wait_taken(pool, ("edges", 0))
            for c in range(EC):
                nc.gpsimd.tensor_scalar(src1h[:, c, :], iota_n, eT[:, 0, c:c + 1], None, ALU.is_equal)
                last = nc.gpsimd.tensor_scalar(dst1h[:, c, :], iota_n, eT[:, 1, c:c + 1], None, ALU.is_equal)
            last.then_inc(s_1h, 1)
            pool.wait_ge(s_cval, 1)
            for c in range(EC):
                last = nc.gpsimd.tensor_scalar(dcode[:, c, :], iota_n, eT[:, 1, c:c + 1], code[:, 1, c:c + 1],
                                               ALU.is_equal, ALU.mult)
            last.then_inc(s_dcode, 1)
            pool.wait_ge(s_late, 32)
            for e in range(NE):
                blk = rhs.rearrange("p k (b n) -> p b k n", n=P)[:, e, :, :]
                blk_q = rhs_q.rearrange("p k (b n) -> p b k n", n=P)[:, e, :, :]
                pool.wait_ge(s_rmax, e + 1)
                nc.gpsimd.partition_all_reduce(rinv[:, 1, :], rmax, P, RMAX).then_inc(s_rall, 1)
                pool.wait_ge(s_rinv, e + 1)
                nc.gpsimd.tensor_tensor(rtmp, blk, rinv[:, 0:1, :].to_broadcast([P, KD, P]),
                                        ALU.mult).then_inc(s_rq, 1)
                pool.wait_ge(s_rq, 4 * e + 1)
                nc.gpsimd.tensor_scalar(rtmp, rtmp, INT8_MAX, -INT8_MAX, ALU.min, ALU.max).then_inc(s_rq, 1)
                pool.wait_ge(s_rq, 4 * e + 2)
                nc.gpsimd.tensor_scalar(rtmp, rtmp, ROUND, ROUND, ALU.add, ALU.subtract).then_inc(s_rq, 1)
                pool.wait_ge(s_rq, 4 * e + 3)
                nc.gpsimd.tensor_copy(blk_q, rtmp).then_inc(s_rq, 1)
                pool.wait_ge(s_rq, 4 * e + 4)

        @block.scalar
        def _(act):
            for k, (v, t) in enumerate(((src_in, 0), (dst_in, 1), (etype_in, 2))):
                act.dma_start(e_int[:, t, :], v.rearrange("(c j) -> c j", j=P)).then_inc(s_edges, 16)
            act.wait_ge(s_rows0, 2)
            for i, v in enumerate(VECTORS):
                act.dma_start(vec_rows[i * KD:(i + 1) * KD, :], v.rearrange("(k j) -> k j", j=P)).then_inc(s_rows, 16)
            for rows, v in ((bg_rows, bg), (b1_rows, b1)):
                act.dma_start(rows[0:FC - 1, :, :], v[:, 0:(FC - 1) * P].rearrange("e (c j) -> c e j", j=P)
                              ).then_inc(s_rows, 16)
                act.dma_start(rows[FC - 1:FC, :, 0:CW[-1]], v[:, (FC - 1) * P:FF].rearrange("e (c j) -> c e j", c=1)
                              ).then_inc(s_rows, 16)
            act.dma_start(cen, centroid).then_inc(s_rows, 16)
            act.dma_start(etw, etw_in.partition_broadcast(N)).then_inc(s_small, 16)
            act.dma_start(b2_sb, b2).then_inc(s_small, 16)
            act.dma_start(bo_row, bo.partition_broadcast(1)).then_inc(s_small, 16)

            def deviation(n):
                act.wait_ge(s_var, n + 1)
                nc.scalar.activation(dev[:, :], mv[:, 2:3], ACT.Sqrt).then_inc(s_dev, 1)

            def take(name, dst, src):
                i = TINDEX[name]
                act.wait_ge(s_t, i + 1)
                nc.scalar.copy(dst, src).then_inc(s_ta, 1)

            def take_weights(m, hf):
                for k in range(KD):
                    name = (("w", m, hf), k)
                    if taken(TINDEX[name])[0] == "a":
                        take(name, wt[:, hf, k, :], tbank[TINDEX[name] % TB][:, :])

            deviation(0)
            take(("edges", 0), eT, tbank[1][:, 0:4 * EC].rearrange("p (a c) -> p a c", c=EC))
            take(("x0", 1), aT[:, HC:KD, :], tbank[3][:, 0:HC * N].rearrange("p (k n) -> p k n", n=N))
            act.wait_ge(s_spv, 1)
            nc.scalar.activation(spw[:, 1, :], spw[:, 0, :], ACT.Exp).then_inc(s_spe, 1)
            act.wait_ge(s_spe, 1)
            nc.scalar.activation(spw[:, 2, :], spw[:, 1, :], ACT.Ln, bias=1.0).then_inc(s_spe, 1)
            take_weights(0, 0)
            take_weights(0, 1)
            for m in range(LO):
                for hf in range(2):
                    take_weights(m + 1, hf)
            act.wait_ge(s_sd, S_ADJ + 1)
            nc.scalar.activation(sc[:, 5:6], sc[:, 1:2], ACT.Sqrt).then_inc(s_adj, 1)
            act.wait_ge(s_sub, 1)
            nc.scalar.activation(S, S, ACT.Exp).then_inc(s_exp, 1)
            for j in range(4):
                name = ("probs", j)
                if taken(TINDEX[name])[0] == "a":
                    take(name, PT[:, 4 * j:4 * j + 4, :],
                         tbank[TINDEX[name] % TB][0:N, 0:4 * N].rearrange("p (h n) -> p h n", n=N))
            deviation(1)
            act.wait_ge(s_ln, 2)
            nc.scalar.activation(v2, ln, ACT.Square, accum_out=sc[:, 0:1]).then_inc(s_xsq, 1)
            name = ("x1", 1)
            take(name, aT[:, HC:KD, :], tbank[TINDEX[name] % TB][:, 0:HC * N].rearrange("p (k n) -> p k n", n=N))
            act.wait_ge(s_gd, 1)
            nc.scalar.activation(dist[:, 1, :], dist[:, 0, :], ACT.Sqrt).then_inc(s_ga, 1)
            act.wait_ge(s_gd, 2)
            nc.scalar.activation(dist[:, 3, :], dist[:, 2, :], ACT.Exp).then_inc(s_ga, 1)
            take_weights(LG, 0)
            take_weights(LG, 1)
            act.wait_ge(s_sd, S_WE + 2)
            act.wait_ge(s_init, 1)
            act.dma_start(rhs, rhs_in.rearrange("(k p) n -> p k n", p=P)).then_inc(s_late, 16)
            act.dma_start(gcn_row, gcn_b.partition_broadcast(1)).then_inc(s_late, 16)

            act.sem_inc(s_gfree, 2)
            with act.Fori(0, NE) as e:
                for c in range(FC):
                    w = CW[c]
                    act.wait_ge(s_gate, e * FC + c + 1)
                    act.wait_ge(s_ufree, e * FC + c + 1)
                    nc.scalar.activation(silu[0:w, c % 2, :], gate_bank[c % 2][0:w, 0:N], ACT.Silu,
                                         bias=cols[0:w, bass.ds(e * FC + (C_BG + c), 1)]).then_inc(s_gfree, 1)

            act.wait_ge(s_hfree, CHUNKS + 2)
            nc.scalar.copy(yT[:, HC:KD, :], acc_bank[1][:, 0:HC * N].rearrange("p (k n) -> p k n", n=N)
                           ).then_inc(s_y, 1)
            deviation(2)
            act.wait_ge(s_s, S_Z + 2)
            nc.scalar.copy(zT[:, HC:KD, :], sbank[(S_Z + 1) % 2][:, 0:HC * N].rearrange("p (k n) -> p k n", n=N)
                           ).then_inc(s_z, 1)
            deviation(3)
            name = ("q", 1)
            take(name, qT[:, HC:KD, :], tbank[TINDEX[name] % TB][:, :].bitcast(BF16)[:, 0:HC * N]
                 .rearrange("p (k n) -> p k n", n=N))

        @block.vector
        def _(dve):
            chain = [0]

            def link(ins):
                chain[0] += 1
                ins.then_inc(s_dve, 1)
                dve.wait_ge(s_dve, chain[0])

            def norm(n, dst):
                for h in range(2):
                    link(nc.vector.bn_stats(stats[:, 6 * h:6 * h + 6], x[:, h * HALF:(h + 1) * HALF]))
                link(nc.vector.bn_aggr(mv[:, 0:2], stats[:, :]))
                nc.vector.tensor_scalar(mv[:, 2:3], mv[:, 1:2], LN_EPS, None, ALU.add).then_inc(s_var, 1)
                dve.wait_ge(s_dev, n + 1)
                link(nc.vector.reciprocal(mv[:, 3:4], dev[:, :]))
                nc.vector.tensor_scalar(dst, x[:, :], mv[:, 0:1], mv[:, 3:4], ALU.subtract,
                                        ALU.mult).then_inc(s_ln, 1)

            def take(name, dst, src):
                dve.wait_ge(s_t, TINDEX[name] + 1)
                nc.vector.tensor_copy(dst, src).then_inc(s_tv, 1)

            def take_weights(m, hf):
                for k in range(KD):
                    name = (("w", m, hf), k)
                    if taken(TINDEX[name])[0] == "v":
                        take(name, wt[:, hf, k, :], tbank[TINDEX[name] % TB][:, :])

            def chunks(v, n=N):
                return v.rearrange("p (k n) -> p k n", n=n)

            dve.wait_ge(s_x, 16)
            norm(0, ln)
            dve.wait_ge(s_edges, 48)
            link(nc.vector.tensor_copy(e_row[:, 0:3, :], e_int))
            nc.vector.scalar_tensor_tensor(e_row[:, 3, :], e_row[:, 0, :], float(N), e_row[:, 1, :],
                                           ALU.mult, ALU.add).then_inc(s_erow, 1)
            take(("cols", 0), cols[:, :], tbank[0][:, 0:NCOLS])
            nc.vector.scalar_tensor_tensor(sq, cen, -0.5, cen, ALU.mult, ALU.mult, accum_out=csq[:, 0:1]).then_inc(s_csq, 1)
            dve.wait_ge(s_const, 6)
            take(("x0", 0), aT[:, 0:HC, :], chunks(tbank[2][:, 0:HC * N]))
            dve.wait_ge(s_small, 48)
            link(nc.vector.tensor_scalar(spw[:, 0, :], etw, -1.0, None, ALU.mult))
            nc.vector.tensor_tensor(spw[:, 0, :], spw[:, 0, :], etw, ALU.min).then_inc(s_spv, 1)
            wait_taken(dve, ("edges", 0))
            link(nc.vector.tensor_scalar(code[:, 0, :], eT[:, 2, :], 0.0, float(NTYPES), ALU.is_equal, ALU.mult))
            link(nc.vector.tensor_tensor(code[:, 0, :], code[:, 0, :], eT[:, 2, :], ALU.add))
            link(nc.vector.tensor_tensor(code[:, 0, :], code[:, 0, :], code_base, ALU.add))
            dve.wait_ge(s_spe, 2)
            link(nc.vector.scalar_tensor_tensor(etw, etw, 0.0, spw[:, 2, :], ALU.max, ALU.add))

            def later_same_edge(j):
                dve.wait_ge(s_s, S_KEY + j + 1)
                if j:
                    dve.wait_ge(s_sd, S_KEY + j)
                for c in range(4):
                    last = (nc.vector.scalar_tensor_tensor(
                        junk[:, c, :], sbank[(S_KEY + j) % 2][:, c * P:(c + 1) * P], eT[:, 3, 4 * j + c:4 * j + c + 1], tri,
                        ALU.is_equal, ALU.mult, accum_out=dup[:, 4 * j + c:4 * j + c + 1]))
                last.then_inc(s_sd, 1)

            def last_edges(j):
                dve.wait_ge(s_s, S_CODE + j + 1)
                nc.vector.reduce_max(best[:, j, :], sbank[(S_CODE + j) % 2][0:N, 0:4 * N]
                                     .rearrange("p (c m) -> p m c", m=N), AX.X).then_inc(s_sd, 1)

            def adjacency():
                b = sbank[S_ADJ % 2]
                dve.wait_ge(s_s, S_ADJ + 1)
                link(nc.vector.tensor_tensor(adjT[:, :], b[0:N, 0:N], ident[0:N, 0:N], ALU.add))
                nc.vector.tensor_scalar(sc[:, 1:2], b[0:N, N:N + 1], 1.0, None, ALU.add).then_inc(s_sd, 1)

            def mask_values():
                dve.wait_ge(s_sd, S_CODE + 6)
                link(nc.vector.reduce_max(best[:, 6, :], best[:, 0:6, :].rearrange("p a m -> p m a"), AX.X))
                link(nc.vector.scalar_tensor_tensor(best[:, 6, :], ident[0:N, 0:N], float(NTYPES), best[:, 6, :],
                                                    ALU.mult, ALU.max))
                link(nc.vector.tensor_copy(best_i, best[:, 6, :]))
                link(nc.vector.tensor_scalar(best_i, best_i, 7, None, ALU.bitwise_and))
                link(nc.vector.tensor_copy(best[:, 0, :], best_i))
                link(nc.vector.tensor_scalar(mask, best[:, 0, :], 0.0, NEG, ALU.is_equal, ALU.mult))
                for t in range(NTYPES):
                    link(nc.vector.tensor_scalar(best[:, 1, :], best[:, 0, :], float(t + 1), etw[:, t:t + 1],
                                                 ALU.is_equal, ALU.mult))
                    link(nc.vector.tensor_tensor(mask, mask, best[:, 1, :], ALU.add))

            def scores(r):
                for par in range(2):
                    j = S_SC + 2 * r + par
                    dve.wait_ge(s_s, j + 1)
                    nc.vector.scalar_tensor_tensor(
                        S[:, 8 * r + par:8 * r + 8:2, :], chunks(sbank[j % 2][0:N, 0:4 * N]), SCALE,
                        mask.rearrange("p (a m) -> p a m", a=1).to_broadcast([N, 4, N]),
                        ALU.mult, ALU.add).then_inc(s_sd, 1)

            def heads(v):
                return v.rearrange("p (h m) -> p h m", m=1).to_broadcast([N, HEADS, N])

            def softmax_a():
                dve.wait_ge(s_sd, S_SC + 4)
                link(nc.vector.reduce_max(mx[:, 0, :], S, AX.X))
                nc.vector.tensor_tensor(S, S, heads(mx[:, 0, :]), ALU.subtract).then_inc(s_sub, 1)

            def softmax_b():
                dve.wait_ge(s_exp, 1)
                link(nc.vector.reduce_sum(mx[:, 1, :], S, AX.X))
                link(nc.vector.reciprocal(mx[:, 2, :], mx[:, 1, :]))
                nc.vector.tensor_tensor(S, S, heads(mx[:, 2, :]), ALU.mult).then_inc(s_prob, 1)

            def side_work(f):
                if f < 3:
                    later_same_edge(2 * f)
                    later_same_edge(2 * f + 1)
                if f == 2:
                    dve.wait_ge(s_sd, S_KEY + 6)
                    nc.vector.scalar_tensor_tensor(code[:, 1, :], dup, 0.0, code[:, 0, :], ALU.is_equal,
                                                   ALU.mult).then_inc(s_cval, 1)
                if f == 3:
                    adjacency()
                if 4 <= f < 7:
                    last_edges(2 * (f - 4))
                    last_edges(2 * (f - 4) + 1)
                if f == 6:
                    mask_values()
                if f == 7:
                    scores(0)
                if f == 8:
                    scores(1)
                    softmax_a()

            LIN = {LQ: linT, LIQ: q2T, LK: linT, LIK: k2T, LV: linT}
            take_weights(0, 0)
            take_weights(0, 1)
            for m in range(LO):
                for hf in range(2):
                    dve.wait_ge(s_o, 2 * m + hf + 1)
                    if m in LIN:
                        nc.vector.tensor_tensor(
                            LIN[m][:, hf * HC:(hf + 1) * HC, :], chunks(obank[hf][:, 0:HC * N]),
                            cols[:, m * KD + hf * HC:m * KD + (hf + 1) * HC].rearrange("p (k n) -> p k n", n=1)
                            .to_broadcast([P, HC, N]), ALU.add).then_inc(s_od, 1)
                    else:
                        nc.vector.tensor_copy(v2[:, hf * HALF:(hf + 1) * HALF], obank[hf][0:N, :]).then_inc(s_od, 1)
                    take_weights(m + 1, hf)
                    side_work(2 * m + hf)
            softmax_b()
            for j in range(4):
                name = ("probs", j)
                if taken(TINDEX[name])[0] == "v":
                    take(name, PT[:, 4 * j:4 * j + 4, :], chunks(tbank[TINDEX[name] % TB][0:N, 0:4 * N]))
            for hf in range(2):
                j = S_PV + hf
                dve.wait_ge(s_s, j + 1)
                nc.vector.tensor_tensor(outT[:, hf * HC:(hf + 1) * HC, :], chunks(sbank[j % 2][:, 0:HC * N]),
                                        cols[:, LIV * KD + hf * HC:LIV * KD + (hf + 1) * HC]
                                        .rearrange("p (k n) -> p k n", n=1).to_broadcast([P, HC, N]),
                                        ALU.add).then_inc(s_sd, 1)
            for hf in range(2):
                xs = x[:, hf * HALF:(hf + 1) * HALF]
                dve.wait_ge(s_o, 2 * LO + hf + 1)
                nc.vector.tensor_tensor(xs, xs, obank[hf][0:N, :], ALU.add).then_inc(s_od, 1)
            dve.wait_ge(s_od, 2 * LO + 2)
            norm(1, ln)
            name = ("x1", 0)
            take(name, aT[:, 0:HC, :], chunks(tbank[TINDEX[name] % TB][:, 0:HC * N]))

            dve.wait_ge(s_s, S_DIST + 1)
            dve.wait_ge(s_xsq, 1)
            nc.vector.tensor_scalar(dist[:, 4, :], sbank[S_DIST % 2][0:N, 0:NE], -2.0, sc[:, 0:1],
                                    ALU.mult, ALU.add).then_inc(s_sd, 1)
            dve.wait_ge(s_sd, S_DIST + 1)
            nc.vector.tensor_scalar(dist[:, 0, :], dist[:, 4, :], 1e-12, None, ALU.max).then_inc(s_gd, 1)
            dve.wait_ge(s_ga, 1)
            link(nc.vector.reduce_max(sc[:, 2:3], dist[:, 1, :], AX.X))
            nc.vector.tensor_scalar(dist[:, 2, :], dist[:, 1, :], sc[:, 2:3], None, ALU.subtract).then_inc(s_gd, 1)
            mine = dist[:, 1, :].rearrange("p (e f) -> p e f", f=1).to_broadcast([N, NE, NE])
            other = dist[:, 1:2, :].to_broadcast([N, NE, NE])
            link(nc.vector.tensor_tensor(cmp[:, 0, :, :], other, mine, ALU.is_equal))
            link(nc.vector.tensor_tensor(cmp[:, 0, :, :], cmp[:, 0, :, :], cmp[:, 2, :, :], ALU.mult))
            link(nc.vector.tensor_tensor(cmp[:, 1, :, :], other, mine, ALU.is_gt))
            link(nc.vector.tensor_tensor(cmp[:, 1, :, :], cmp[:, 0, :, :], cmp[:, 1, :, :], ALU.add))
            link(nc.vector.reduce_sum(dist[:, 5, :], cmp[:, 1, :, :], AX.X))
            dve.wait_ge(s_ga, 2)
            link(nc.vector.scalar_tensor_tensor(dist[:, 6, :], dist[:, 5, :], 2.0, dist[:, 3, :], ALU.is_lt,
                                                ALU.mult, accum_out=sc[:, 3:4]))
            link(nc.vector.reciprocal(sc[:, 4:5], sc[:, 3:4]))
            nc.vector.tensor_scalar(dist[:, 7, :], dist[:, 6, :], sc[:, 4:5], None, ALU.mult).then_inc(s_we, 1)
            take(("we", 0), weT, tbank[TINDEX[("we", 0)] % TB][0:NE, 0:N])
            for hf in range(2):
                j = S_WE + hf
                dve.wait_ge(s_s, j + 1)
                nc.vector.tensor_copy(we_b[:, hf * 4:hf * 4 + 4, :], chunks(sbank[j % 2][:, 0:4 * N])
                                      ).then_inc(s_sd, 1)
            dve.wait_ge(s_adj, 1)
            link(nc.vector.reciprocal(dinv[:, :], sc[:, 5:6]))
            link(nc.vector.tensor_scalar(adjT[:, :], adjT[:, :], dinv[:, :], None, ALU.mult))
            take_weights(LG, 0)
            take_weights(LG, 1)

            dve.sem_inc(s_ufree, 2)
            dve.wait_ge(s_late, 32)
            with dve.Fori(0, NE) as e:
                blk = rhs.rearrange("p k (b n) -> p b n k", n=P)[:, e, :, :]
                we_e = we_b[:, e, :]
                for c in range(FC):
                    w = CW[c]
                    dve.wait_ge(s_up, e * FC + c + 1)
                    dve.wait_ge(s_gfree, e * FC + c + 3)
                    nc.vector.scalar_tensor_tensor(hid[0:w, c % 2, :], up_bank[c % 2][0:w, 0:N],
                                                   cols[0:w, bass.ds(e * FC + (C_B1 + c), 1)], silu[0:w, c % 2, :],
                                                   ALU.add, ALU.mult).then_inc(s_ufree, 1)
                    dve.wait_ge(s_ufree, e * FC + c + 3)
                    dve.wait_ge(s_hfree, e * FC + c + 1)
                    nc.vector.tensor_tensor(hT[0:w, c % 2, :], hid[0:w, c % 2, :], we_e[0:w, :],
                                            ALU.mult).then_inc(s_h, 1)
                    if c == 1:
                        nc.vector.tensor_reduce(rmax, blk, AX.X, ALU.max, apply_absolute_value=True
                                                ).then_inc(s_rmax, 1)
                    if c == 12:
                        dve.wait_ge(s_rall, e + 1)
                        nc.vector.tensor_scalar(rmax, rinv[:, 1, :], 1e-12, 1.0 / INT8_MAX,
                                                ALU.max, ALU.mult).then_inc(s_rscale, 1)
                        dve.wait_ge(s_rscale, e + 1)
                        nc.vector.reciprocal(rinv[:, 0, :], rmax).then_inc(s_rinv, 1)
                        nc.vector.tensor_copy(rscale[:, bass.ts(e, P)], rmax)

            dve.wait_ge(s_hfree, CHUNKS + 2)
            nc.vector.tensor_copy(yT[:, 0:HC, :], chunks(acc_bank[0][:, 0:HC * N])).then_inc(s_y, 1)
            for hf in range(2):
                xs = x[:, hf * HALF:(hf + 1) * HALF]
                j = S_Y + hf
                dve.wait_ge(s_s, j + 1)
                nc.vector.tensor_tensor(xs, xs, sbank[j % 2][0:N, :], ALU.add).then_inc(s_sd, 1)
            dve.wait_ge(s_sd, S_Y + 2)
            norm(2, ln_t)
            j = S_Z
            dve.wait_ge(s_s, j + 1)
            nc.vector.tensor_copy(zT[:, 0:HC, :], chunks(sbank[j % 2][:, 0:HC * N])).then_inc(s_sd, 1)
            dve.wait_ge(s_z, 1)
            dve.wait_ge(s_s, S_ROW + 1)
            nc.vector.tensor_copy(row_sum, sbank[S_ROW % 2][0:1, 0:N]).then_inc(s_sd, 1)
            for hf in range(2):
                xs = x[:, hf * HALF:(hf + 1) * HALF]
                dve.wait_ge(s_o, O_GCN + hf + 1)
                nc.vector.scalar_tensor_tensor(xs, obank[hf][0:N, :], dinv[:, :], xs, ALU.mult,
                                               ALU.add).then_inc(s_od, 1)
            dve.wait_ge(s_od, O_GCN + 2)
            norm(3, qf)
            dve.wait_ge(s_ln, 4)
            link(nc.vector.tensor_reduce(sc[:, 5:6], qf, AX.X, ALU.max, apply_absolute_value=True))
            link(nc.vector.tensor_scalar(sc[:, 6:7], sc[:, 5:6], 1e-12, 1.0 / INT8_MAX, ALU.max, ALU.mult))
            link(nc.vector.reciprocal(sc[:, 7:8], sc[:, 6:7]))
            link(nc.vector.tensor_scalar(qf, qf, sc[:, 7:8], INT8_MAX, ALU.mult, ALU.min))
            link(nc.vector.tensor_scalar(qf, qf, -INT8_MAX, ROUND, ALU.max, ALU.add))
            nc.vector.tensor_scalar(qb, qf, ROUND, None, ALU.subtract).then_inc(s_q, 1)
            name = ("q", 0)
            take(name, qT[:, 0:HC, :], chunks(tbank[TINDEX[name] % TB][:, :].bitcast(BF16)[:, 0:HC * N]))
            for hf in range(2):
                cut = slice(hf * HALF, (hf + 1) * HALF)
                dve.wait_ge(s_o, O_INT8 + hf + 1)
                link(nc.vector.scalar_tensor_tensor(res[:, cut], obank[hf][0:N, :], sc[:, 6:7], rscale[0:N, cut],
                                                    ALU.mult, ALU.mult))
                nc.vector.tensor_tensor(res[:, cut], res[:, cut], x[:, cut], ALU.add).then_inc(s_res, 1)

        @block.tensor
        def _(pe):
            def open_bank(name):
                i = TINDEX[name]
                if i >= TB:
                    who, n = taken(i - TB)
                    pe.wait_ge(s_tv if who == "v" else s_ta, n)
                return tbank[i % TB]

            def transpose_weights(m, hf):
                i = 2 * m + hf
                s = i % SLOTS
                pe.wait_ge(s_full[s], 16 * (i // SLOTS + 1))
                for k in range(KD):
                    b = open_bank((("w", m, hf), k))
                    for c in range(HC):
                        last = nc.tensor.transpose(b[:, c * P:(c + 1) * P],
                                                   ring[:, s, c * D + k * P:c * D + (k + 1) * P], ident[:, :])
                    last.then_inc(s_t, 1)

            def transpose_rows(name, src):
                for hf in range(2):
                    b = open_bank((name, hf))
                    for c in range(HC):
                        k = hf * HC + c
                        last = nc.tensor.transpose(b[:, c * N:(c + 1) * N], src[:, k * P:(k + 1) * P],
                                                   ident[0:N, 0:N])
                    last.then_inc(s_t, 1)

            def side(j):
                if j >= 2:
                    pe.wait_ge(s_sd, j - 1)
                return sbank[j % 2]

            def product(j):
                if j >= 2:
                    pe.wait_ge(s_od, j - 1)
                return obank[j % 2]

            def linear_T(m, hf, src):
                b = product(2 * m + hf)
                for c in range(HC):
                    for k in range(KD):
                        last = nc.tensor.matmul(b[:, c * N:(c + 1) * N], wt[:, hf, k, c * P:(c + 1) * P],
                                                src[:, k, :], start=(k == 0), stop=(k == KD - 1))
                last.then_inc(s_o, 1)

            def linear_rows(b, hf, src, bias_l=None, bias_r=None):
                for k in range(KD):
                    last = nc.tensor.matmul(b[0:N, :], src[:, k, :], wt[:, hf, k, :], start=(k == 0),
                                            stop=(k == KD - 1 and bias_l is None))
                if bias_l is not None:
                    last = nc.tensor.matmul(b[0:N, :], bias_l, bias_r, start=False, stop=True)
                last.then_inc(s_o, 1)

            pe.wait_ge(s_const, 1)
            pe.wait_ge(s_rows, 16 * (len(VECTORS) + 5))
            b = open_bank(("cols", 0))
            nc.tensor.transpose(b[:, 0:C_BG], vec_rows, ident[0:C_BG, 0:C_BG])
            for first, rows in ((C_BG, bg_rows), (C_B1, b1_rows)):
                for e in range(NE):
                    nc.tensor.transpose(b[:, first + e * FC:first + (e + 1) * FC], rows[:, e, :], ident[0:FC, 0:FC])
            for k in range(KD):
                last = nc.tensor.transpose(b[:, C_CEN + k * NE:C_CEN + (k + 1) * NE], cen[:, k * P:(k + 1) * P],
                                           ident[0:NE, 0:NE])
            last.then_inc(s_t, 1)
            b = open_bank(("edges", 0))
            pe.wait_ge(s_erow, 1)
            for a in range(4):
                last = nc.tensor.transpose(b[:, a * EC:(a + 1) * EC], e_row[:, a, :], ident[0:EC, 0:EC])
            last.then_inc(s_t, 1)
            pe.wait_ge(s_ln, 1)
            transpose_rows("x0", ln)

            def spread(column, n):
                return column.to_broadcast([column.shape[0], n])

            def spread_keys(j):
                b = side(S_KEY + j)
                for c in range(4):
                    last = nc.tensor.matmul(b[:, c * P:(c + 1) * P], spread(ident[0:EC, 4 * j + c:4 * j + c + 1], P), e_row[:, 3, :],
                                            start=True, stop=True)
                last.then_inc(s_s, 1)

            def count_edges():
                b = side(S_ADJ)
                for c in range(EC):
                    nc.tensor.matmul(b[0:N, 0:N], dst1h[:, c, :], src1h[:, c, :], start=(c == 0), stop=(c == EC - 1))
                for c in range(EC):
                    last = nc.tensor.matmul(b[0:N, N:N + 1], src1h[:, c, :], ones_b[:, 0:1], start=(c == 0),
                                            stop=(c == EC - 1))
                last.then_inc(s_s, 1)

            def spread_codes(j):
                b = side(S_CODE + j)
                for c in range(4):
                    last = nc.tensor.matmul(b[0:N, c * N:(c + 1) * N], src1h[:, 4 * j + c, :],
                                            dcode[:, 4 * j + c, :], start=True, stop=True)
                last.then_inc(s_s, 1)

            def scores(r):
                for par in range(2):
                    b = side(S_SC + 2 * r + par)
                    rows = slice(DH * par, DH * (par + 1))
                    for i in range(4):
                        last = nc.tensor.matmul(b[0:N, i * N:(i + 1) * N], q2T[rows, 4 * r + i, :],
                                                k2T[rows, 4 * r + i, :], start=True, stop=True)
                    last.then_inc(s_s, 1)

            def side_work(f):
                if f < 3:
                    spread_keys(2 * f)
                    spread_keys(2 * f + 1)
                if f == 3:
                    pe.wait_ge(s_1h, 1)
                    count_edges()
                if f == 4:
                    pe.wait_ge(s_dcode, 1)
                if 4 <= f < 7:
                    spread_codes(2 * (f - 4))
                    spread_codes(2 * (f - 4) + 1)
                if f == 7:
                    pe.wait_ge(s_od, 2 * LIK + 2)
                    scores(0)
                if f == 8:
                    scores(1)

            transpose_weights(0, 0)
            transpose_weights(0, 1)
            for m in range(LO):
                for hf in range(2):
                    if hf == 0:
                        if m in (LQ, LK, LV):
                            wait_x_stage(pe, "x0")
                        else:
                            pe.wait_ge(s_od, 2 * m)
                    for k in (KD - 2, KD - 1):
                        wait_taken(pe, (("w", m, hf), k))
                    if m == LIV:
                        linear_rows(product(2 * m + hf), hf, linT)
                    else:
                        linear_T(m, hf, aT if m in (LQ, LK, LV) else linT)
                    transpose_weights(m + 1, hf)
                    side_work(2 * m + hf)

            pe.wait_ge(s_prob, 1)
            for j in range(4):
                b = open_bank(("probs", j))
                for i in range(4):
                    last = nc.tensor.transpose(b[0:N, i * N:(i + 1) * N], S[:, 4 * j + i, :], ident[0:N, 0:N])
                last.then_inc(s_t, 1)
            for j in range(4):
                wait_taken(pe, ("probs", j))
            for hf in range(2):
                b = side(S_PV + hf)
                for h in range(8 * hf, 8 * hf + 8):
                    last = nc.tensor.matmul(b[DH * (h % 2):DH * (h % 2 + 1), (h // 2 % 4) * N:(h // 2 % 4 + 1) * N],
                                            v2[:, h * DH:(h + 1) * DH], PT[:, h, :], start=True, stop=True)
                last.then_inc(s_s, 1)
            pe.wait_ge(s_sd, S_PV + 2)
            for k in (KD - 2, KD - 1):
                wait_taken(pe, (("w", LO, 1), k))
            pe.wait_ge(s_small, 48)
            for hf in range(2):
                linear_rows(product(2 * LO + hf), hf, outT, ones[0:1, 0:N], bo_row[:, hf * HALF:(hf + 1) * HALF])

            pe.wait_ge(s_ln, 2)
            transpose_rows("x1", ln)
            wait_x_stage(pe, "x1")
            pe.wait_ge(s_csq, 1)
            b = side(S_DIST)
            for k in range(KD):
                nc.tensor.matmul(b[0:N, 0:NE], aT[:, k, :], cols[:, C_CEN + k * NE:C_CEN + (k + 1) * NE],
                                 start=(k == 0), stop=False)
            nc.tensor.matmul(b[0:N, 0:NE], spread(csq[:, 0:1], N), ident[0:NE, 0:NE], start=False, stop=True).then_inc(s_s, 1)
            pe.wait_ge(s_we, 1)
            b = open_bank(("we", 0))
            nc.tensor.transpose(b[0:NE, 0:N], dist[:, 7, :], ident[0:N, 0:N]).then_inc(s_t, 1)
            wait_taken(pe, ("we", 0))
            for hf in range(2):
                b = side(S_WE + hf)
                for i in range(4):
                    last = nc.tensor.matmul(b[:, i * N:(i + 1) * N], spread(ident[0:NE, 4 * hf + i:4 * hf + i + 1], P), weT, start=True, stop=True)
                last.then_inc(s_s, 1)
            for hf in range(2):
                pe.wait_ge(s_od, O_GCN)
                b = acc_bank[hf]
                for c in range(HC):
                    k = hf * HC + c
                    last = nc.tensor.matmul(b[:, c * N:(c + 1) * N], b2_sb[:, k * P:(k + 1) * P], weT,
                                            start=(c == 0), stop=False, skip_group_check=True)
            last.then_inc(s_init, 1)
            transpose_weights(LG, 0)
            transpose_weights(LG, 1)
            for k in range(KD - 4, KD):
                wait_taken(pe, (("w", LG, 1), k))

            def slot_view(g, kind):
                return ring[:, slot_of(g, kind), :]

            def wait_loaded(e, g, kind):
                s = slot_of(g, kind)
                pe.wait_ge(s_full[s], e * (16 * slot_parts(s)) + 16 * (half_uses(s) + slot_parts_until(g, kind)))

            group_of = {c: g for g, cs in enumerate(GROUPS) for c in cs}

            def expand(e, c):
                g, w = group_of[c], CW[c]
                off = (c - GROUPS[g][0]) * P
                gw = group_width(g)
                for kind, b, s_done, s_free in ((GATE, gate_bank[c % 2], s_gate, s_gfree),
                                                (UP, up_bank[c % 2], s_up, s_ufree)):
                    if c == GROUPS[g][0]:
                        wait_loaded(e, g, kind)
                    pe.wait_ge(s_free, e * FC + c + 1)
                    W = slot_view(g, kind)[:, 0:KD * gw].rearrange("p (k w) -> p k w", w=gw)
                    for k in range(KD):
                        last = nc.tensor.matmul(b[0:w, 0:N], W[:, k, off:off + w], aT[:, k, :],
                                                start=(k == 0), stop=(k == KD - 1))
                    last.then_inc(s_done, 1)

            def contract(e, c):
                g, w = group_of[c], CW[c]
                if c == GROUPS[g][0]:
                    wait_loaded(e, g, DOWN)
                pe.wait_ge(s_h, e * FC + c + 1)
                W = slot_view(g, DOWN).rearrange("p (c d) -> p c d", d=D)[0:w, c - GROUPS[g][0], :]
                for k in range(KD):
                    last = nc.tensor.matmul(acc_bank[k // HC][:, (k % HC) * N:(k % HC + 1) * N],
                                            W[:, k * P:(k + 1) * P], hT[0:w, c % 2, :],
                                            start=False, stop=False, skip_group_check=True)
                last.then_inc(s_hfree, 1)

            pe.sem_inc(s_hfree, 2)
            with pe.Fori(0, NE) as e:
                for c in range(FC):
                    expand(e, c)
                    if c >= 1:
                        contract(e, c - 1)
                contract(e, FC - 1)

            pe.wait_ge(s_y, 2)
            for hf in range(2):
                b = side(S_Y + hf)
                for c in range(HC):
                    last = nc.tensor.transpose(b[0:N, c * P:(c + 1) * P], yT[:, hf * HC + c, :], ident[:, :])
                last.then_inc(s_s, 1)
            pe.wait_ge(s_ln, 3)
            for hf in range(2):
                b = side(S_Z + hf)
                for c in range(HC):
                    k = hf * HC + c
                    last = nc.tensor.matmul(b[:, c * N:(c + 1) * N], ln_t[:, k * P:(k + 1) * P], adjT[:, :],
                                            start=True, stop=True)
                last.then_inc(s_s, 1)
            nc.tensor.matmul(side(S_ROW)[0:1, 0:N], ones[0:N, 0:1], adjT[:, :], start=True, stop=True).then_inc(s_s, 1)
            pe.wait_ge(s_z, 1)
            pe.wait_ge(s_sd, S_Z + 2)
            for hf in range(2):
                linear_rows(product(O_GCN + hf), hf, zT, row_sum, gcn_row[:, hf * HALF:(hf + 1) * HALF])
            pe.wait_ge(s_q, 1)
            for hf in range(2):
                b = open_bank(("q", hf))[:, :].bitcast(BF16)
                for c in range(HC):
                    k = hf * HC + c
                    last = nc.tensor.transpose(b[:, c * N:(c + 1) * N], qb[:, k * P:(k + 1) * P], ident_b[0:N, 0:N])
                last.then_inc(s_t, 1)
            wait_x_stage(pe, "q")
            pe.wait_ge(s_rq, 4 * NE)
            for hf in range(2):
                b = product(O_INT8 + hf)
                for k in range(KD):
                    last = nc.tensor.matmul(b[0:N, :], qT[:, k, :], rhs_q[:, k, hf * HALF:(hf + 1) * HALF],
                                            start=(k == 0), stop=(k == KD - 1))
                last.then_inc(s_o, 1)


_INS = ['x', 'src', 'dst', 'edge_type_5', 'L0_gnn_edge_type_weights', 'L0_gnn_wq', 'L0_gnn_bq', 'L0_gnn_wk',
        'L0_gnn_bk', 'L0_gnn_wv', 'L0_gnn_bv', 'L0_gnn_wiq', 'L0_gnn_biq', 'L0_gnn_wik', 'L0_gnn_bik',
        'L0_gnn_wiv', 'L0_gnn_biv', 'L0_gnn_wo', 'L0_gnn_bo', 'L0_ffn_centroid', 'L0_ffn_Wg', 'L0_ffn_bg',
        'L0_ffn_W1', 'L0_ffn_b1', 'L0_ffn_W2', 'L0_ffn_b2', 'L1_gnn_W', 'L1_gnn_b', 'L1_ffn_rhs']
_OUTS = [((96, 1024), 'float32')]


def kernel(**inputs):
    import numpy as _np
    import concourse.bacc as _bacc
    from concourse import mybir as _mybir
    from concourse.bass_utils import run_bass_kernel_spmd as _run

    nc = _bacc.Bacc("TRN2", target_bir_lowering=False, num_devices=1)
    arrays, args = {}, []
    for name in _INS:
        a = _np.ascontiguousarray(inputs[name])
        arrays[f"in_{name}_dram"] = a
        args.append(nc.dram_tensor(f"in_{name}_dram", a.shape, _mybir.dt.from_np(a.dtype), kind="ExternalInput").ap())
    for i, (shape, dtype) in enumerate(_OUTS):
        dt = _mybir.dt.from_np(_np.dtype(dtype))
        args.append(nc.dram_tensor(f"out_{i}_dram", shape, dt, kind="ExternalOutput").ap())
    gnn_moe_gcn_int8_kernel(nc, *args)
    r = _run(nc, [arrays], core_ids=[0])
    got = tuple(r.results[0][f"out_{i}_dram"] for i in range(len(_OUTS)))
    return got[0]
```

```python
import numpy as np
import concourse.bass as bass
from concourse import mybir
from contextlib import ExitStack


def gnn_moe_gcn_int8_kernel(nc, x_in, src_in, dst_in, etype_in, etw_in,
                            wq, bq, wk, bk, wv, bv, wiq, biq, wik, bik, wiv, biv, wo, bo,
                            centroid, Wg, bg, W1, b1, W2, b2, gcn_w, gcn_b, rhs_in, out):
    F32, BF16, I32 = mybir.dt.float32, mybir.dt.bfloat16, mybir.dt.int32
    ALU, ACT, AX = mybir.AluOpType, mybir.ActivationFunctionType, mybir.AxisListType

    P = 128
    N, D = x_in.shape
    KD = D // P
    HALF = D // 2
    HC = HALF // P
    NE, _, FF = Wg.shape
    FC = -(-FF // P)
    CW = [min(P, FF - P * c) for c in range(FC)]
    EDGES = src_in.shape[0]
    EC = EDGES // P
    DH = 64
    HEADS = D // DH
    NTYPES = etw_in.shape[0]
    LN_EPS, NEG, INT8_MAX = 1e-5, -1e30, 127.0
    RMAX = bass.bass_isa.ReduceOp.max
    ROUND = 1.5 * 2.0 ** 23
    SCALE = 1.0 / float(np.sqrt(np.float32(DH)))

    SLOTS, SLOT = 8, HC * D
    GROUPS = [range(0, 4), range(4, 8), range(8, 12), range(12, 16), range(16, 19), range(19, 22)]
    GATE, UP, DOWN = range(3)
    DEPTH = {GATE: 3, UP: 3, DOWN: 2}

    def slot_of(g, kind):
        return 3 * (g % DEPTH[kind]) + kind

    def group_width(g):
        return sum(CW[c] for c in GROUPS[g])

    def parts(g, kind):
        return 2 if kind == DOWN and group_width(g) % P else 1

    def slot_parts(s):
        return sum(parts(g, k) for g in range(len(GROUPS)) for k in range(3) if slot_of(g, k) == s)

    def slot_parts_until(g, kind):
        return sum(parts(h, kind) for h in range(g + 1) if slot_of(h, kind) == slot_of(g, kind))

    SQUARES = [wq, wiq, wk, wik, wv, wiv, wo, gcn_w]
    LQ, LIQ, LK, LIK, LV, LIV, LO, LG = range(8)
    HALVES = 2 * len(SQUARES)

    HSLOTS = 4
    WT2_SLOT, EARLY_SLOT = 4, 6
    LOAD_ORDER = [LQ, LIQ, LK, LIK, LV, LG, LIV, LO]
    SECOND = (LIQ, LIK, LIV, LO)
    LAST = {s: max(range(s, HALVES, HSLOTS)) for s in range(HSLOTS)}

    QUADRANT_OUT = (LQ, LK, LV)
    Q, B = 4, 32
    QF = D // Q

    TGROUPS = []

    def add_groups(name, n, first=0):
        for k in range(n):
            TGROUPS.append(((name, k), first if first == "a" else "va"[(first + k) % 2]))

    add_groups("x0", 2)
    add_groups("cols", 1, "a")
    add_groups("edges", 1, "a")
    for m in (LG, LO):
        for hf in range(2):
            add_groups(("w", m, hf), KD, "a")
    add_groups("probs", 4)
    add_groups("x1", 2)
    add_groups("we", 1)
    add_groups("q", 2)
    TINDEX = {name: i for i, (name, _) in enumerate(TGROUPS)}
    TB = 4

    def taken(i):
        who = TGROUPS[i][1]
        return who, sum(w == who for _, w in TGROUPS[:i + 1])

    VECTORS = [bq, biq, bk, bik, bv, biv]
    C_BG = len(VECTORS) * KD
    C_B1 = C_BG + NE * FC
    C_CEN = C_B1 + NE * FC
    NCOLS = C_CEN + KD * NE

    ctx = ExitStack()
    with ctx:
        def sb(name, shape, dt=F32):
            return ctx.enter_context(nc.sbuf_tensor(name, shape, dt))

        def sem(name):
            return ctx.enter_context(nc.semaphore(name))

        ring = sb("ring", [P, SLOTS, SLOT])
        wt = sb("wt", [P, KD, D])
        arena = sb("arena", [P, 8032])
        x = sb("x", [N, D])
        aT = sb("aT", [P, KD, N])
        cols = sb("cols", [P, NCOLS])
        we_b = sb("we_b", [P, NE, N])
        silu = sb("silu", [P, 2, N])
        hid = sb("hid", [P, 2, N])
        hT = sb("hT", [P, 2, N])
        ident = sb("ident", [P, P])
        ident_b = sb("ident_b", [P, P], BF16)
        ones_b = sb("ones_b", [P, 1], BF16)
        adjT = sb("adjT", [N, N])
        dinv = sb("dinv", [N, 1])
        ones = sb("ones", [P, P])
        stats = sb("stats", [N, 12])
        mv = sb("mv", [N, 4])
        dev = sb("dev", [N, 1])
        sc = sb("sc", [N, 8])

        at = {"arena": 0, "ring": 0}
        places = {"arena": arena[:, :], "ring": ring[:, EARLY_SLOT:SLOTS, :].rearrange("p s n -> p (s n)")}

        def carve(rows, n, dt=F32, place="arena"):
            words = n if dt != BF16 else -(-n // 2)
            v = places[place][0:rows, at[place]:at[place] + words]
            at[place] += words
            return v if dt == F32 else v.bitcast(dt)

        def chunked(v, n):
            return v.rearrange("p (k n) -> p k n", n=n)

        wt2 = ring[:, WT2_SLOT:EARLY_SLOT, :].rearrange("p s (k n) -> p (s k) n", n=D)

        def weights(m):
            return wt2 if m in SECOND else wt[:, :, :]

        ln = carve(N, D)
        b2_sb = carve(NE, D)
        bo_row = carve(1, D)
        mask = carve(N, N)
        start = at["arena"]
        linT = chunked(carve(P, KD * N), N)
        q2T = chunked(carve(P, KD * N), N)
        k2T = chunked(carve(P, KD * N), N)
        v2 = carve(N, D)
        outT = linT
        end = at["arena"]
        S = chunked(carve(N, HEADS * N, place="ring"), N)
        PT = chunked(carve(N, HEADS * N, place="ring"), N)
        src1h = chunked(carve(P, EC * N, BF16, "ring"), N)
        dst1h = chunked(carve(P, EC * N, BF16, "ring"), N)
        dcode = chunked(carve(P, EC * N, BF16, "ring"), N)
        best = chunked(carve(N, 7 * N, place="ring"), N)
        best_i = carve(N, N, I32, "ring")
        e_int = chunked(carve(EC, 3 * P, I32, "ring"), P)
        eT = chunked(carve(P, 4 * EC, place="ring"), EC)
        at["arena"], at["ring"] = start, 0
        bg_rows = chunked(carve(FC, NE * P), P)
        b1_rows = chunked(carve(FC, NE * P), P)
        vec_rows = carve(C_BG, P)
        sq = carve(NE, D)
        cen = carve(NE, D, place="ring")
        at["arena"] = max(end, at["arena"])
        e_row = chunked(carve(EC, 4 * P), P)
        iota_n = carve(P, N)
        code_base = carve(P, EC)
        tri = carve(P, P)
        junk = chunked(carve(P, 4 * P, BF16), P)
        dup = carve(P, EC)
        code = chunked(carve(P, 2 * EC), EC)
        etw = carve(N, NTYPES)
        spw = chunked(carve(N, 3 * NTYPES), NTYPES)
        mx = chunked(carve(N, 3 * HEADS), HEADS)
        dist = chunked(carve(N, 8 * NE), NE)
        cmp = carve(N, 3 * NE * NE).rearrange("p (a e f) -> p a e f", e=NE, f=NE)
        weT = carve(NE, N)
        csq = carve(NE, 2)
        at["arena"] = 0
        rhs_q = chunked(carve(P, KD * D, BF16), D)
        rblk = chunked(carve(P, KD * P), P)
        rscale = carve(P, D)
        gcn_row = carve(1, D)
        rmax = carve(P, P)
        rinv = chunked(carve(P, 2 * P), P)

        yT = chunked(ring[:, 0, 0:KD * N], N)
        ln_t = ring[0:N, 1, 0:D]
        zT = chunked(ring[:, 2, 0:KD * N], N)
        row_sum = ring[0:1, 3, 0:N]
        qf = ring[0:N, 4, 0:D]
        qb = ring[0:N, 4, D:D + D // 2].bitcast(BF16)
        qT = chunked(ring[:, 4, 2 * D:2 * D + KD * N // 2].bitcast(BF16), N)
        res = ring[0:N, 5, 0:D]

        bank = [ctx.enter_context(nc.psum_tensor(f"bank{i}", [P, HALF], F32)) for i in range(8)]
        tbank, obank, sbank = bank[0:4], bank[4:6], bank[6:8]
        gate_bank, up_bank, acc_bank = tbank[0:2], tbank[2:4], obank

        s_const = sem("s_const")
        s_rows0 = sem("s_rows0")
        s_x = sem("s_x")
        s_edges = sem("s_edges")
        s_rows = sem("s_rows")
        s_small = sem("s_small")
        s_gcnb = sem("s_gcnb")
        s_rblk = sem("s_rblk")
        s_wt = sem("s_wt")
        s_full = [sem(f"s_full{s}") for s in range(SLOTS)]
        s_t = sem("s_t")
        s_tv = sem("s_tv")
        s_ta = sem("s_ta")
        s_o = sem("s_o")
        s_od = sem("s_od")
        s_s = sem("s_s")
        s_sd = sem("s_sd")
        s_dve = sem("s_dve")
        s_pool = sem("s_pool")
        s_act = sem("s_act")
        s_var = sem("s_var")
        s_dev = sem("s_dev")
        s_ln = sem("s_ln")
        s_erow = sem("s_erow")
        s_1h = sem("s_1h")
        s_cval = sem("s_cval")
        s_dcode = sem("s_dcode")
        s_spe = sem("s_spe")
        s_spv = sem("s_spv")
        s_sub = sem("s_sub")
        s_exp = sem("s_exp")
        s_prob = sem("s_prob")
        s_adj = sem("s_adj")
        s_csq = sem("s_csq")
        s_xsq = sem("s_xsq")
        s_gd = sem("s_gd")
        s_ga = sem("s_ga")
        s_we = sem("s_we")
        s_init = sem("s_init")
        s_gate = sem("s_gate")
        s_up = sem("s_up")
        s_gfree = sem("s_gfree")
        s_ufree = sem("s_ufree")
        s_hid = sem("s_hid")
        s_h = sem("s_h")
        s_hfree = sem("s_hfree")
        s_rmax = sem("s_rmax")
        s_rall = sem("s_rall")
        s_rscale = sem("s_rscale")
        s_rinv = sem("s_rinv")
        s_rq = sem("s_rq")
        s_y = sem("s_y")
        s_z = sem("s_z")
        s_q = sem("s_q")
        s_res = sem("s_res")
        s_out = sem("s_out")

        block = ctx.enter_context(nc.Block())

        S_KEY, S_ADJ, S_CODE, S_SC, S_PV, S_DIST, S_WE, S_Y, S_Z, S_ROW = 0, 6, 7, 13, 17, 19, 20, 22, 24, 26
        O_GCN, O_INT8 = 2 * LG, 2 * LG + 2
        CHUNKS = NE * FC

        ROW_LOADS = 16 * (len(VECTORS) + 5)

        def half_index(m, hf):
            return 2 * LOAD_ORDER.index(m) + hf

        def half_loads(i):
            return Q if LOAD_ORDER[i // 2] <= LIV else 1

        def half_loaded(i):
            return 16 * sum(half_loads(j) for j in range(i % HSLOTS, i + 1, HSLOTS))

        def wait_taken(eng, name):
            who, n = taken(TINDEX[name])
            eng.wait_ge(s_tv if who == "v" else s_ta, n)

        def early_tenants_gone(eng):
            eng.wait_ge(s_sd, S_WE + 2)
            eng.wait_ge(s_init, 1)

        def wait_x_stage(eng, n):
            wait_taken(eng, (n, 0))
            wait_taken(eng, (n, 1))

        @block.sync
        def _(sp):
            def half_freed(i):
                m, hf = LOAD_ORDER[i // 2], i % 2
                if m <= LIV:
                    sp.wait_ge(s_wt, 2 * m + hf + 1)
                else:
                    sp.wait_ge(s_t, TINDEX[(("w", m, hf), KD - 1)] + 1)

            def small_loads():
                for k, (v, t) in enumerate(((src_in, 0), (dst_in, 1), (etype_in, 2))):
                    sp.dma_start(e_int[:, t, :], v.rearrange("(c j) -> c j", j=P)).then_inc(s_edges, 16)
                sp.wait_ge(s_rows0, 2)
                for i, v in enumerate(VECTORS):
                    rows = vec_rows[i * KD:(i + 1) * KD, :]
                    if i in QUADRANT_OUT:
                        sp.dma_start(rows.rearrange("k (q b) -> k q b", b=B), v.rearrange("(q k b) -> k q b", q=Q, b=B)
                                      ).then_inc(s_rows, 16)
                    else:
                        sp.dma_start(rows, v.rearrange("(k j) -> k j", j=P)).then_inc(s_rows, 16)
                for rows, v in ((bg_rows, bg), (b1_rows, b1)):
                    sp.dma_start(rows[0:FC - 1, :, :], v[:, 0:(FC - 1) * P].rearrange("e (c j) -> c e j", j=P)
                                  ).then_inc(s_rows, 16)
                    sp.dma_start(rows[FC - 1:FC, :, 0:CW[-1]], v[:, (FC - 1) * P:FF].rearrange("e (c j) -> c e j", c=1)
                                  ).then_inc(s_rows, 16)
                sp.dma_start(cen, centroid).then_inc(s_rows, 16)
                sp.dma_start(etw, etw_in.partition_broadcast(N)).then_inc(s_small, 16)
                sp.dma_start(b2_sb, b2).then_inc(s_small, 16)
                sp.dma_start(bo_row, bo.partition_broadcast(1)).then_inc(s_small, 16)

            sp.dma_start(x[:, :], x_in).then_inc(s_x, 16)
            for i in range(HALVES):
                m, hf, s = LOAD_ORDER[i // 2], i % 2, i % HSLOTS
                if i >= HSLOTS:
                    half_freed(i - HSLOTS)
                if i == 2:
                    small_loads()
                if m > LIV:
                    sp.dma_start(ring[:, s, :].rearrange("p (c i) -> p c i", i=D),
                                 SQUARES[m][hf * HALF:(hf + 1) * HALF, :].rearrange("(c p) i -> p c i", p=P)
                                 ).then_inc(s_full[s], 16)
                    continue
                w = SQUARES[m].rearrange("(o b) (q i) -> q b o i", b=B, q=Q)
                dst = ring[:, s, :].rearrange("p (o i) -> p o i", i=QF)
                for q in range(Q):
                    nb = HALF // B
                    sp.dma_start(dst[B * q:B * (q + 1), :, :], w[q, :, hf * nb:(hf + 1) * nb, :]
                                 ).then_inc(s_full[s], 16)

            def load_group(e, g):
                c0, w = GROUPS[g][0] * P, group_width(g)
                for kind, src in ((GATE, Wg), (UP, W1)):
                    s = slot_of(g, kind)
                    release(e, g, kind)
                    sp.dma_start(ring[:, s, 0:KD * w].rearrange("p (k w) -> p k w", w=w),
                                 src[e, :, c0:c0 + w].rearrange("(k p) w -> p k w", p=P)).then_inc(s_full[s], 16)
                s = slot_of(g, DOWN)
                release(e, g, DOWN)
                whole = w // P
                dst = ring[:, s, :].rearrange("p (c d) -> p c d", d=D)
                sp.dma_start(dst[:, 0:whole, :], W2[e, c0:c0 + whole * P, :].rearrange("(c p) d -> p c d", p=P)
                             ).then_inc(s_full[s], 16)
                if w % P:
                    sp.dma_start(dst[0:w % P, whole, :], W2[e, c0 + whole * P:c0 + w, :]).then_inc(s_full[s], 16)

            def release(e, g, kind):
                s = slot_of(g, kind)
                if isinstance(e, int) and g < DEPTH[kind]:
                    if s < HSLOTS:
                        half_freed(LAST[s])
                    elif s < EARLY_SLOT:
                        sp.wait_ge(s_o, 2 * LO + 2)
                    else:
                        early_tenants_gone(sp)
                else:
                    d = DEPTH[kind]
                    before = GROUPS[g - d][-1] + 1 - (FC if g < d else 0)
                    done = {GATE: s_gate, UP: s_up, DOWN: s_hfree}[kind]
                    sp.wait_ge(done, e * FC + before + (2 if kind == DOWN else 0))

            def load_block(e):
                if not isinstance(e, int):
                    sp.wait_ge(s_rq, 4 * e)
                sp.dma_start(rblk, rhs_in.rearrange("(k p) (b n) -> b p k n", p=P, n=P)[e]).then_inc(s_rblk, 16)

            for g in range(len(GROUPS)):
                load_group(0, g)
                if g == 2:
                    sp.dma_start(gcn_row, gcn_b.partition_broadcast(1)).then_inc(s_gcnb, 16)
                    load_block(0)
            with sp.Fori(1, NE) as e:
                for g in range(len(GROUPS)):
                    load_group(e, g)
                    if g == 2:
                        load_block(e)
            for hf in range(2):
                sp.wait_ge(s_res, hf + 1)
                sp.dma_start(out[:, hf * HALF:(hf + 1) * HALF], res[:, hf * HALF:(hf + 1) * HALF]).then_inc(s_out, 16)
            sp.wait_ge(s_out, 32)

        @block.gpsimd
        def _(pool):
            chain = [0]

            def link(ins):
                chain[0] += 1
                ins.then_inc(s_pool, 1)
                pool.wait_ge(s_pool, chain[0])

            nc.gpsimd.memset(bg_rows, 0.0).then_inc(s_rows0, 1)
            nc.gpsimd.memset(b1_rows, 0.0).then_inc(s_rows0, 1)
            link(nc.gpsimd.memset(ident[:, :], 0.0))
            link(nc.gpsimd.affine_select(out=ident[:, :], in_=ident[:, :], compare_op=ALU.not_equal, fill=1.0,
                                         base=0, pattern=[[-1, P]], channel_multiplier=1))
            link(nc.gpsimd.tensor_copy(ident_b[:, :], ident[:, :]))
            nc.gpsimd.memset(ones_b[:, :], 1.0).then_inc(s_const, 1)
            nc.gpsimd.memset(ones[:, :], 1.0).then_inc(s_const, 1)
            pool.wait_ge(s_const, 2)
            nc.gpsimd.affine_select(out=tri, in_=ones[:, :], compare_op=ALU.is_gt, fill=0.0,
                                    base=0, pattern=[[1, P]], channel_multiplier=-1).then_inc(s_const, 1)
            low = cmp[:, 2, :, :]
            nc.gpsimd.affine_select(out=low, in_=ones[0:N, 0:NE * NE].rearrange("p (e f) -> p e f", f=NE),
                                    compare_op=ALU.is_gt, fill=0.0, base=0, pattern=[[1, NE], [-1, NE]],
                                    channel_multiplier=0).then_inc(s_const, 1)
            nc.gpsimd.iota(iota_n, [[1, N]], base=0, channel_multiplier=0,
                           allow_small_or_imprecise_dtypes=True).then_inc(s_const, 1)
            nc.gpsimd.iota(code_base, [[8, EC]], base=8, channel_multiplier=0,
                           allow_small_or_imprecise_dtypes=True).then_inc(s_const, 1)
            pool.wait_ge(s_const, 6)
            wait_taken(pool, ("edges", 0))
            for c in range(EC):
                nc.gpsimd.tensor_scalar(src1h[:, c, :], iota_n, eT[:, 0, c:c + 1], None, ALU.is_equal)
                last = nc.gpsimd.tensor_scalar(dst1h[:, c, :], iota_n, eT[:, 1, c:c + 1], None, ALU.is_equal)
            last.then_inc(s_1h, 1)
            for e in range(NE):
                blk_q = rhs_q.rearrange("p k (b n) -> p b k n", n=P)[:, e, :, :]
                pool.wait_ge(s_rmax, e + 1)
                nc.gpsimd.partition_all_reduce(rinv[:, 1, :], rmax, P, RMAX).then_inc(s_rall, 1)
                pool.wait_ge(s_rinv, e + 1)
                nc.gpsimd.tensor_tensor(rblk, rblk, rinv[:, 0:1, :].to_broadcast([P, KD, P]),
                                        ALU.mult).then_inc(s_rq, 1)
                pool.wait_ge(s_rq, 4 * e + 1)
                nc.gpsimd.tensor_scalar(rblk, rblk, INT8_MAX, -INT8_MAX, ALU.min, ALU.max).then_inc(s_rq, 1)
                pool.wait_ge(s_rq, 4 * e + 2)
                nc.gpsimd.tensor_scalar(rblk, rblk, ROUND, ROUND, ALU.add, ALU.subtract).then_inc(s_rq, 1)
                pool.wait_ge(s_rq, 4 * e + 3)
                nc.gpsimd.tensor_copy(blk_q, rblk).then_inc(s_rq, 1)
                pool.wait_ge(s_rq, 4 * e + 4)

        @block.scalar
        def _(act):
            def deviation(n):
                act.wait_ge(s_var, n + 1)
                nc.scalar.activation(dev[:, :], mv[:, 2:3], ACT.Sqrt).then_inc(s_dev, 1)

            def take(name, dst, src):
                i = TINDEX[name]
                act.wait_ge(s_t, i + 1)
                nc.scalar.copy(dst, src).then_inc(s_ta, 1)

            def take_weights(m, hf):
                for k in range(KD):
                    name = (("w", m, hf), k)
                    if taken(TINDEX[name])[0] == "a":
                        take(name, weights(m)[:, k, hf * HALF:(hf + 1) * HALF], tbank[TINDEX[name] % TB][:, :])

            deviation(0)
            take(("x0", 1), aT[:, HC:KD, :], tbank[1][:, 0:HC * N].rearrange("p (k n) -> p k n", n=N))

            def take_product(m, hf):
                act.wait_ge(s_o, 2 * m + hf + 1)
                if m == LIV:
                    nc.scalar.copy(v2[:, hf * HALF:(hf + 1) * HALF], obank[hf][0:N, :]).then_inc(s_od, 1)
                    return
                dst = q2T if m == LIQ else k2T if m == LIK else linT
                for c in range(HC):
                    k = hf * HC + c
                    last = nc.scalar.activation(dst[:, k, :], obank[hf][:, c * N:(c + 1) * N], ACT.Identity,
                                                bias=cols[:, m * KD + k:m * KD + k + 1])
                last.then_inc(s_od, 1)

            take(("cols", 0), cols[:, :], tbank[2][:, 0:NCOLS])
            wait_taken(act, ("cols", 0))
            for m in range(LIV):
                take_product(m, 0)
                if m == 0:
                    take(("edges", 0), eT, tbank[3][:, 0:4 * EC].rearrange("p (a c) -> p a c", c=EC))
                take_product(m, 1)
                if m == 1:
                    act.wait_ge(s_spv, 1)
                    nc.scalar.activation(spw[:, 1, :], spw[:, 0, :], ACT.Exp).then_inc(s_spe, 1)
                    act.wait_ge(s_spe, 1)
                    nc.scalar.activation(spw[:, 2, :], spw[:, 1, :], ACT.Ln, bias=1.0).then_inc(s_spe, 1)
            take_weights(LG, 0)
            take_weights(LG, 1)
            act.wait_ge(s_sd, S_ADJ + 1)
            nc.scalar.activation(sc[:, 5:6], sc[:, 1:2], ACT.Sqrt).then_inc(s_adj, 1)
            act.wait_ge(s_sub, 1)
            nc.scalar.activation(S, S, ACT.Exp).then_inc(s_exp, 1)
            take_product(LIV, 0)
            take_product(LIV, 1)
            take_weights(LO, 0)
            take_weights(LO, 1)
            for j in range(4):
                name = ("probs", j)
                if taken(TINDEX[name])[0] == "a":
                    take(name, PT[:, 4 * j:4 * j + 4, :],
                         tbank[TINDEX[name] % TB][0:N, 0:4 * N].rearrange("p (h n) -> p h n", n=N))
            deviation(1)
            act.wait_ge(s_ln, 2)
            nc.scalar.activation(v2, ln, ACT.Square, accum_out=sc[:, 0:1]).then_inc(s_xsq, 1)
            name = ("x1", 1)
            take(name, aT[:, HC:KD, :], tbank[TINDEX[name] % TB][:, 0:HC * N].rearrange("p (k n) -> p k n", n=N))
            act.wait_ge(s_gd, 1)
            nc.scalar.activation(dist[:, 1, :], dist[:, 0, :], ACT.Sqrt).then_inc(s_ga, 1)
            act.wait_ge(s_gd, 2)
            nc.scalar.activation(dist[:, 3, :], dist[:, 2, :], ACT.Exp).then_inc(s_ga, 1)
            act.sem_inc(s_gfree, 2)
            with act.Fori(0, NE) as e:
                for c in range(FC):
                    w = CW[c]
                    act.wait_ge(s_gate, e * FC + c + 1)
                    act.wait_ge(s_ufree, e * FC + c + 1)
                    nc.scalar.activation(silu[0:w, c % 2, :], gate_bank[c % 2][0:w, 0:N], ACT.Silu,
                                         bias=cols[0:w, bass.ds(e * FC + (C_BG + c), 1)]).then_inc(s_gfree, 1)

            act.wait_ge(s_hfree, CHUNKS + 2)
            nc.scalar.copy(yT[:, HC:KD, :], acc_bank[1][:, 0:HC * N].rearrange("p (k n) -> p k n", n=N)
                           ).then_inc(s_y, 1)
            deviation(2)
            act.wait_ge(s_s, S_Z + 2)
            nc.scalar.copy(zT[:, HC:KD, :], sbank[(S_Z + 1) % 2][:, 0:HC * N].rearrange("p (k n) -> p k n", n=N)
                           ).then_inc(s_z, 1)
            deviation(3)
            name = ("q", 1)
            take(name, qT[:, HC:KD, :], tbank[TINDEX[name] % TB][:, :].bitcast(BF16)[:, 0:HC * N]
                 .rearrange("p (k n) -> p k n", n=N))

        @block.vector
        def _(dve):
            chain = [0]

            def link(ins):
                chain[0] += 1
                ins.then_inc(s_dve, 1)
                dve.wait_ge(s_dve, chain[0])

            def norm(n, dst, quadrant_order=False):
                for h in range(2):
                    link(nc.vector.bn_stats(stats[:, 6 * h:6 * h + 6], x[:, h * HALF:(h + 1) * HALF]))
                link(nc.vector.bn_aggr(mv[:, 0:2], stats[:, :]))
                nc.vector.tensor_scalar(mv[:, 2:3], mv[:, 1:2], LN_EPS, None, ALU.add).then_inc(s_var, 1)
                dve.wait_ge(s_dev, n + 1)
                link(nc.vector.reciprocal(mv[:, 3:4], dev[:, :]))
                if quadrant_order:
                    for q in range(Q):
                        last = nc.vector.tensor_scalar(
                            dst.rearrange("n (k q a) -> n q k a", q=Q, a=B)[:, q],
                            x[:, q * QF:(q + 1) * QF].rearrange("n (k a) -> n k a", a=B), mv[:, 0:1], mv[:, 3:4],
                            ALU.subtract, ALU.mult)
                else:
                    last = nc.vector.tensor_scalar(dst, x[:, :], mv[:, 0:1], mv[:, 3:4], ALU.subtract, ALU.mult)
                last.then_inc(s_ln, 1)

            def take(name, dst, src):
                dve.wait_ge(s_t, TINDEX[name] + 1)
                nc.vector.tensor_copy(dst, src).then_inc(s_tv, 1)

            def chunks(v, n=N):
                return v.rearrange("p (k n) -> p k n", n=n)

            dve.wait_ge(s_x, 16)
            norm(0, ln, True)
            take(("x0", 0), aT[:, 0:HC, :], chunks(tbank[0][:, 0:HC * N]))
            def later_same_edge(j):
                dve.wait_ge(s_s, S_KEY + j + 1)
                if j:
                    dve.wait_ge(s_sd, S_KEY + j)
                for c in range(4):
                    last = (nc.vector.scalar_tensor_tensor(
                        junk[:, c, :], sbank[(S_KEY + j) % 2][:, c * P:(c + 1) * P], eT[:, 3, 4 * j + c:4 * j + c + 1], tri,
                        ALU.is_equal, ALU.mult, accum_out=dup[:, 4 * j + c:4 * j + c + 1]))
                last.then_inc(s_sd, 1)

            def last_edges(j):
                dve.wait_ge(s_s, S_CODE + j + 1)
                nc.vector.reduce_max(best[:, j, :], sbank[(S_CODE + j) % 2][0:N, 0:4 * N]
                                     .rearrange("p (c m) -> p m c", m=N), AX.X).then_inc(s_sd, 1)

            def adjacency():
                b = sbank[S_ADJ % 2]
                dve.wait_ge(s_s, S_ADJ + 1)
                link(nc.vector.tensor_tensor(adjT[:, :], b[0:N, 0:N], ident[0:N, 0:N], ALU.add))
                nc.vector.tensor_scalar(sc[:, 1:2], b[0:N, N:N + 1], 1.0, None, ALU.add).then_inc(s_sd, 1)

            def mask_values():
                dve.wait_ge(s_spe, 2)
                link(nc.vector.scalar_tensor_tensor(etw, etw, 0.0, spw[:, 2, :], ALU.max, ALU.add))
                dve.wait_ge(s_sd, S_CODE + 6)
                link(nc.vector.reduce_max(best[:, 6, :], best[:, 0:6, :].rearrange("p a m -> p m a"), AX.X))
                link(nc.vector.scalar_tensor_tensor(best[:, 6, :], ident[0:N, 0:N], float(NTYPES), best[:, 6, :],
                                                    ALU.mult, ALU.max))
                link(nc.vector.tensor_copy(best_i, best[:, 6, :]))
                link(nc.vector.tensor_scalar(best_i, best_i, 7, None, ALU.bitwise_and))
                link(nc.vector.tensor_copy(best[:, 0, :], best_i))
                link(nc.vector.tensor_scalar(mask, best[:, 0, :], 0.0, NEG, ALU.is_equal, ALU.mult))
                for t in range(NTYPES):
                    link(nc.vector.tensor_scalar(best[:, 1, :], best[:, 0, :], float(t + 1), etw[:, t:t + 1],
                                                 ALU.is_equal, ALU.mult))
                    link(nc.vector.tensor_tensor(mask, mask, best[:, 1, :], ALU.add))

            def scores(r):
                for par in range(2):
                    j = S_SC + 2 * r + par
                    dve.wait_ge(s_s, j + 1)
                    nc.vector.scalar_tensor_tensor(
                        S[:, 8 * r + par:8 * r + 8:2, :], chunks(sbank[j % 2][0:N, 0:4 * N]), SCALE,
                        mask.rearrange("p (a m) -> p a m", a=1).to_broadcast([N, 4, N]),
                        ALU.mult, ALU.add).then_inc(s_sd, 1)

            def heads(v):
                return v.rearrange("p (h m) -> p h m", m=1).to_broadcast([N, HEADS, N])

            def softmax_a():
                dve.wait_ge(s_sd, S_SC + 4)
                link(nc.vector.reduce_max(mx[:, 0, :], S, AX.X))
                nc.vector.tensor_tensor(S, S, heads(mx[:, 0, :]), ALU.subtract).then_inc(s_sub, 1)

            def softmax_b():
                dve.wait_ge(s_exp, 1)
                link(nc.vector.reduce_sum(mx[:, 1, :], S, AX.X))
                link(nc.vector.reciprocal(mx[:, 2, :], mx[:, 1, :]))
                nc.vector.tensor_tensor(S, S, heads(mx[:, 2, :]), ALU.mult).then_inc(s_prob, 1)

            def side_work(f):
                if f < 3:
                    later_same_edge(2 * f)
                    later_same_edge(2 * f + 1)
                if f == 2:
                    dve.wait_ge(s_sd, S_KEY + 6)
                    nc.vector.scalar_tensor_tensor(code[:, 1, :], dup, 0.0, code[:, 0, :], ALU.is_equal,
                                                   ALU.mult).then_inc(s_cval, 1)
                    dve.wait_ge(s_cval, 1)
                    dve.wait_ge(s_1h, 1)
                    nc.vector.tensor_tensor(dcode, dst1h, code[:, 1, :].rearrange("p (c n) -> p c n", n=1)
                                            .to_broadcast([P, EC, N]), ALU.mult).then_inc(s_dcode, 1)
                if f == 3:
                    adjacency()
                if 4 <= f < 7:
                    last_edges(2 * (f - 4))
                    last_edges(2 * (f - 4) + 1)
                if f == 6:
                    mask_values()
                if f == 7:
                    scores(0)
                if f == 8:
                    scores(1)

            def transpose_weights(i):
                m, hf = i // 2, i % 2
                i = half_index(m, hf)
                s = i % HSLOTS
                dve.wait_ge(s_full[s], half_loaded(i))
                if m >= 2:
                    dve.wait_ge(s_o, 2 * (m - 2) + 2)
                nb = HALF // B
                src = ring[:, s, :].rearrange("p (o k a) -> p k o a", k=KD, a=B)
                for k in range(KD):
                    row = weights(m)[:, k, :]
                    if m in QUADRANT_OUT:
                        dst = row.rearrange("p (j r b) -> p r j b", r=Q, b=B)[:, 2 * hf:2 * hf + 2]
                        last = nc.vector.transpose(dst, src[:, k].rearrange("p (r j) a -> p r j a", r=2))
                    else:
                        dst = row[:, hf * HALF:(hf + 1) * HALF].rearrange("p (o b) -> p o b", b=B)
                        last = nc.vector.transpose(dst, src[:, k])
                last.then_inc(s_wt, 1)

            def edge_rows():
                dve.wait_ge(s_edges, 48)
                link(nc.vector.tensor_copy(e_row[:, 0:3, :], e_int))
                nc.vector.scalar_tensor_tensor(e_row[:, 3, :], e_row[:, 0, :], float(N), e_row[:, 1, :],
                                               ALU.mult, ALU.add).then_inc(s_erow, 1)
                dve.wait_ge(s_rows, ROW_LOADS)
                nc.vector.scalar_tensor_tensor(sq, cen, -0.5, cen, ALU.mult, ALU.mult,
                                               accum_out=csq[:, 0:1]).then_inc(s_csq, 1)
                dve.wait_ge(s_small, 48)
                link(nc.vector.tensor_scalar(spw[:, 0, :], etw, -1.0, None, ALU.mult))
                nc.vector.tensor_tensor(spw[:, 0, :], spw[:, 0, :], etw, ALU.min).then_inc(s_spv, 1)

            def edge_codes():
                dve.wait_ge(s_const, 6)
                wait_taken(dve, ("edges", 0))
                link(nc.vector.tensor_scalar(code[:, 0, :], eT[:, 2, :], 0.0, float(NTYPES), ALU.is_equal, ALU.mult))
                link(nc.vector.tensor_tensor(code[:, 0, :], code[:, 0, :], eT[:, 2, :], ALU.add))
                link(nc.vector.tensor_tensor(code[:, 0, :], code[:, 0, :], code_base, ALU.add))

            for i in range(4):
                transpose_weights(i)
                if i == 1:
                    edge_rows()
            edge_codes()
            for i in range(4, 2 * LIV):
                side_work(i - 4)
                transpose_weights(i)
            for f in range(2 * LIV - 4, 9):
                side_work(f)
            softmax_a()
            transpose_weights(2 * LIV)
            transpose_weights(2 * LIV + 1)
            softmax_b()
            for j in range(4):
                name = ("probs", j)
                if taken(TINDEX[name])[0] == "v":
                    take(name, PT[:, 4 * j:4 * j + 4, :], chunks(tbank[TINDEX[name] % TB][0:N, 0:4 * N]))
            for hf in range(2):
                j = S_PV + hf
                dve.wait_ge(s_s, j + 1)
                nc.vector.tensor_tensor(outT[:, hf * HC:(hf + 1) * HC, :], chunks(sbank[j % 2][:, 0:HC * N]),
                                        cols[:, LIV * KD + hf * HC:LIV * KD + (hf + 1) * HC]
                                        .rearrange("p (k n) -> p k n", n=1).to_broadcast([P, HC, N]),
                                        ALU.add).then_inc(s_sd, 1)
            for hf in range(2):
                xs = x[:, hf * HALF:(hf + 1) * HALF]
                dve.wait_ge(s_o, 2 * LO + hf + 1)
                nc.vector.tensor_tensor(xs, xs, obank[hf][0:N, :], ALU.add).then_inc(s_od, 1)
            dve.wait_ge(s_od, 2 * LO + 2)
            norm(1, ln)
            name = ("x1", 0)
            take(name, aT[:, 0:HC, :], chunks(tbank[TINDEX[name] % TB][:, 0:HC * N]))

            dve.wait_ge(s_s, S_DIST + 1)
            dve.wait_ge(s_xsq, 1)
            nc.vector.tensor_scalar(dist[:, 4, :], sbank[S_DIST % 2][0:N, 0:NE], -2.0, sc[:, 0:1],
                                    ALU.mult, ALU.add).then_inc(s_sd, 1)
            dve.wait_ge(s_sd, S_DIST + 1)
            nc.vector.tensor_scalar(dist[:, 0, :], dist[:, 4, :], 1e-12, None, ALU.max).then_inc(s_gd, 1)
            dve.wait_ge(s_ga, 1)
            link(nc.vector.reduce_max(sc[:, 2:3], dist[:, 1, :], AX.X))
            nc.vector.tensor_scalar(dist[:, 2, :], dist[:, 1, :], sc[:, 2:3], None, ALU.subtract).then_inc(s_gd, 1)
            mine = dist[:, 1, :].rearrange("p (e f) -> p e f", f=1).to_broadcast([N, NE, NE])
            other = dist[:, 1:2, :].to_broadcast([N, NE, NE])
            link(nc.vector.tensor_tensor(cmp[:, 0, :, :], other, mine, ALU.is_equal))
            link(nc.vector.tensor_tensor(cmp[:, 0, :, :], cmp[:, 0, :, :], cmp[:, 2, :, :], ALU.mult))
            link(nc.vector.tensor_tensor(cmp[:, 1, :, :], other, mine, ALU.is_gt))
            link(nc.vector.tensor_tensor(cmp[:, 1, :, :], cmp[:, 0, :, :], cmp[:, 1, :, :], ALU.add))
            link(nc.vector.reduce_sum(dist[:, 5, :], cmp[:, 1, :, :], AX.X))
            dve.wait_ge(s_ga, 2)
            link(nc.vector.scalar_tensor_tensor(dist[:, 6, :], dist[:, 5, :], 2.0, dist[:, 3, :], ALU.is_lt,
                                                ALU.mult, accum_out=sc[:, 3:4]))
            link(nc.vector.reciprocal(sc[:, 4:5], sc[:, 3:4]))
            nc.vector.tensor_scalar(dist[:, 7, :], dist[:, 6, :], sc[:, 4:5], None, ALU.mult).then_inc(s_we, 1)
            take(("we", 0), weT, tbank[TINDEX[("we", 0)] % TB][0:NE, 0:N])
            for hf in range(2):
                j = S_WE + hf
                dve.wait_ge(s_s, j + 1)
                nc.vector.tensor_copy(we_b[:, hf * 4:hf * 4 + 4, :], chunks(sbank[j % 2][:, 0:4 * N])
                                      ).then_inc(s_sd, 1)
            dve.wait_ge(s_adj, 1)
            link(nc.vector.reciprocal(dinv[:, :], sc[:, 5:6]))
            link(nc.vector.tensor_scalar(adjT[:, :], adjT[:, :], dinv[:, :], None, ALU.mult))
            dve.sem_inc(s_ufree, 2)
            with dve.Fori(0, NE) as e:
                blk = rblk.rearrange("p k n -> p n k")
                we_e = we_b[:, e, :]
                for c in range(FC):
                    w = CW[c]
                    dve.wait_ge(s_up, e * FC + c + 1)
                    dve.wait_ge(s_gfree, e * FC + c + 3)
                    nc.vector.scalar_tensor_tensor(hid[0:w, c % 2, :], up_bank[c % 2][0:w, 0:N],
                                                   cols[0:w, bass.ds(e * FC + (C_B1 + c), 1)], silu[0:w, c % 2, :],
                                                   ALU.add, ALU.mult).then_inc(s_ufree, 1)
                    dve.wait_ge(s_ufree, e * FC + c + 3)
                    dve.wait_ge(s_hfree, e * FC + c + 1)
                    nc.vector.tensor_tensor(hT[0:w, c % 2, :], hid[0:w, c % 2, :], we_e[0:w, :],
                                            ALU.mult).then_inc(s_h, 1)
                    if c == FC // 2:
                        dve.wait_ge(s_rblk, 16 * e + 16)
                        nc.vector.tensor_reduce(rmax, blk, AX.X, ALU.max, apply_absolute_value=True
                                                ).then_inc(s_rmax, 1)
                    if c == 16:
                        dve.wait_ge(s_rall, e + 1)
                        nc.vector.tensor_scalar(rmax, rinv[:, 1, :], 1e-12, 1.0 / INT8_MAX,
                                                ALU.max, ALU.mult).then_inc(s_rscale, 1)
                        dve.wait_ge(s_rscale, e + 1)
                        nc.vector.reciprocal(rinv[:, 0, :], rmax).then_inc(s_rinv, 1)
                        nc.vector.tensor_copy(rscale[:, bass.ts(e, P)], rmax)

            dve.wait_ge(s_hfree, CHUNKS + 2)
            nc.vector.tensor_copy(yT[:, 0:HC, :], chunks(acc_bank[0][:, 0:HC * N])).then_inc(s_y, 1)
            for hf in range(2):
                xs = x[:, hf * HALF:(hf + 1) * HALF]
                j = S_Y + hf
                dve.wait_ge(s_s, j + 1)
                nc.vector.tensor_tensor(xs, xs, sbank[j % 2][0:N, :], ALU.add).then_inc(s_sd, 1)
            dve.wait_ge(s_sd, S_Y + 2)
            norm(2, ln_t)
            j = S_Z
            dve.wait_ge(s_s, j + 1)
            nc.vector.tensor_copy(zT[:, 0:HC, :], chunks(sbank[j % 2][:, 0:HC * N])).then_inc(s_sd, 1)
            dve.wait_ge(s_z, 1)
            dve.wait_ge(s_s, S_ROW + 1)
            nc.vector.tensor_copy(row_sum, sbank[S_ROW % 2][0:1, 0:N]).then_inc(s_sd, 1)
            for hf in range(2):
                xs = x[:, hf * HALF:(hf + 1) * HALF]
                dve.wait_ge(s_o, O_GCN + hf + 1)
                nc.vector.scalar_tensor_tensor(xs, obank[hf][0:N, :], dinv[:, :], xs, ALU.mult,
                                               ALU.add).then_inc(s_od, 1)
            dve.wait_ge(s_od, O_GCN + 2)
            norm(3, qf)
            dve.wait_ge(s_ln, 4)
            link(nc.vector.tensor_reduce(sc[:, 5:6], qf, AX.X, ALU.max, apply_absolute_value=True))
            link(nc.vector.tensor_scalar(sc[:, 6:7], sc[:, 5:6], 1e-12, 1.0 / INT8_MAX, ALU.max, ALU.mult))
            link(nc.vector.reciprocal(sc[:, 7:8], sc[:, 6:7]))
            link(nc.vector.tensor_scalar(qf, qf, sc[:, 7:8], INT8_MAX, ALU.mult, ALU.min))
            link(nc.vector.tensor_scalar(qf, qf, -INT8_MAX, ROUND, ALU.max, ALU.add))
            nc.vector.tensor_scalar(qb, qf, ROUND, None, ALU.subtract).then_inc(s_q, 1)
            name = ("q", 0)
            take(name, qT[:, 0:HC, :], chunks(tbank[TINDEX[name] % TB][:, :].bitcast(BF16)[:, 0:HC * N]))
            for hf in range(2):
                cut = slice(hf * HALF, (hf + 1) * HALF)
                dve.wait_ge(s_o, O_INT8 + hf + 1)
                link(nc.vector.scalar_tensor_tensor(res[:, cut], obank[hf][0:N, :], sc[:, 6:7], rscale[0:N, cut],
                                                    ALU.mult, ALU.mult))
                nc.vector.tensor_tensor(res[:, cut], res[:, cut], x[:, cut], ALU.add).then_inc(s_res, 1)

        @block.tensor
        def _(pe):
            def open_bank(name):
                i = TINDEX[name]
                if i >= TB:
                    who, n = taken(i - TB)
                    pe.wait_ge(s_tv if who == "v" else s_ta, n)
                return tbank[i % TB]

            def transpose_weights(m, hf):
                i = half_index(m, hf)
                s = i % HSLOTS
                pe.wait_ge(s_full[s], half_loaded(i))
                for k in range(KD):
                    b = open_bank((("w", m, hf), k))
                    for c in range(HC):
                        last = nc.tensor.transpose(b[:, c * P:(c + 1) * P],
                                                   ring[:, s, c * D + k * P:c * D + (k + 1) * P], ident[:, :])
                    last.then_inc(s_t, 1)

            def transpose_rows(name, src):
                for hf in range(2):
                    b = open_bank((name, hf))
                    for c in range(HC):
                        k = hf * HC + c
                        last = nc.tensor.transpose(b[:, c * N:(c + 1) * N], src[:, k * P:(k + 1) * P],
                                                   ident[0:N, 0:N])
                    last.then_inc(s_t, 1)

            def side(j):
                if j >= 2:
                    pe.wait_ge(s_sd, j - 1)
                return sbank[j % 2]

            def product(j):
                if j >= 2:
                    pe.wait_ge(s_od, j - 1)
                return obank[j % 2]

            def linear_T(m, hf, src):
                b = product(2 * m + hf)
                w = weights(m)
                for c in range(HC):
                    col = hf * HALF + c * P
                    for k in range(KD):
                        last = nc.tensor.matmul(b[:, c * N:(c + 1) * N], w[:, k, col:col + P],
                                                src[:, k, :], start=(k == 0), stop=(k == KD - 1))
                last.then_inc(s_o, 1)

            def linear_rows(b, hf, w, src, bias_l=None, bias_r=None):
                for k in range(KD):
                    last = nc.tensor.matmul(b[0:N, :], src[:, k, :], w[:, k, hf * HALF:(hf + 1) * HALF], start=(k == 0),
                                            stop=(k == KD - 1 and bias_l is None))
                if bias_l is not None:
                    last = nc.tensor.matmul(b[0:N, :], bias_l, bias_r, start=False, stop=True)
                last.then_inc(s_o, 1)

            pe.wait_ge(s_const, 1)
            pe.wait_ge(s_ln, 1)
            transpose_rows("x0", ln)
            pe.wait_ge(s_rows, ROW_LOADS)
            b = open_bank(("cols", 0))
            nc.tensor.transpose(b[:, 0:C_BG], vec_rows, ident[0:C_BG, 0:C_BG])
            for first, rows in ((C_BG, bg_rows), (C_B1, b1_rows)):
                for e in range(NE):
                    nc.tensor.transpose(b[:, first + e * FC:first + (e + 1) * FC], rows[:, e, :], ident[0:FC, 0:FC])
            for k in range(KD):
                last = nc.tensor.transpose(b[:, C_CEN + k * NE:C_CEN + (k + 1) * NE], cen[:, k * P:(k + 1) * P],
                                           ident[0:NE, 0:NE])
            last.then_inc(s_t, 1)

            def spread(column, n):
                return column.to_broadcast([column.shape[0], n])

            def spread_keys(j):
                b = side(S_KEY + j)
                for c in range(4):
                    last = nc.tensor.matmul(b[:, c * P:(c + 1) * P], spread(ident[0:EC, 4 * j + c:4 * j + c + 1], P), e_row[:, 3, :],
                                            start=True, stop=True)
                last.then_inc(s_s, 1)

            def count_edges():
                b = side(S_ADJ)
                for c in range(EC):
                    nc.tensor.matmul(b[0:N, 0:N], dst1h[:, c, :], src1h[:, c, :], start=(c == 0), stop=(c == EC - 1))
                for c in range(EC):
                    last = nc.tensor.matmul(b[0:N, N:N + 1], src1h[:, c, :], ones_b[:, 0:1], start=(c == 0),
                                            stop=(c == EC - 1))
                last.then_inc(s_s, 1)

            def spread_codes(j):
                b = side(S_CODE + j)
                for c in range(4):
                    last = nc.tensor.matmul(b[0:N, c * N:(c + 1) * N], src1h[:, 4 * j + c, :],
                                            dcode[:, 4 * j + c, :], start=True, stop=True)
                last.then_inc(s_s, 1)

            def scores(r):
                for par in range(2):
                    b = side(S_SC + 2 * r + par)
                    rows = slice(DH * par, DH * (par + 1))
                    for i in range(4):
                        last = nc.tensor.matmul(b[0:N, i * N:(i + 1) * N], q2T[rows, 4 * r + i, :],
                                                k2T[rows, 4 * r + i, :], start=True, stop=True)
                    last.then_inc(s_s, 1)

            def side_work(f):
                if f == 0:
                    b = open_bank(("edges", 0))
                    pe.wait_ge(s_erow, 1)
                    for a in range(4):
                        last = nc.tensor.transpose(b[:, a * EC:(a + 1) * EC], e_row[:, a, :], ident[0:EC, 0:EC])
                    last.then_inc(s_t, 1)
                if f < 3:
                    spread_keys(2 * f)
                    spread_keys(2 * f + 1)
                if f == 3:
                    pe.wait_ge(s_1h, 1)
                    count_edges()
                if f == 4:
                    pe.wait_ge(s_dcode, 1)
                if 4 <= f < 7:
                    spread_codes(2 * (f - 4))
                    spread_codes(2 * (f - 4) + 1)
                if f == 7:
                    pe.wait_ge(s_od, 2 * LIK + 2)
                    scores(0)
                if f == 8:
                    scores(1)

            for m in range(LO):
                if m == LIV:
                    transpose_weights(LG, 0)
                    transpose_weights(LG, 1)
                if m in QUADRANT_OUT:
                    wait_x_stage(pe, "x0")
                else:
                    pe.wait_ge(s_od, 2 * m)
                for hf in range(2):
                    pe.wait_ge(s_wt, 2 * m + 2 if m in QUADRANT_OUT else 2 * m + hf + 1)
                    if m == LIV:
                        linear_rows(product(2 * m + hf), hf, weights(m), linT)
                    else:
                        linear_T(m, hf, aT if m in QUADRANT_OUT else linT)
                    side_work(2 * m + hf)
            transpose_weights(LO, 0)
            transpose_weights(LO, 1)

            pe.wait_ge(s_prob, 1)
            for j in range(4):
                b = open_bank(("probs", j))
                for i in range(4):
                    last = nc.tensor.transpose(b[0:N, i * N:(i + 1) * N], S[:, 4 * j + i, :], ident[0:N, 0:N])
                last.then_inc(s_t, 1)
            for j in range(4):
                wait_taken(pe, ("probs", j))
            for hf in range(2):
                b = side(S_PV + hf)
                for h in range(8 * hf, 8 * hf + 8):
                    last = nc.tensor.matmul(b[DH * (h % 2):DH * (h % 2 + 1), (h // 2 % 4) * N:(h // 2 % 4 + 1) * N],
                                            v2[:, h * DH:(h + 1) * DH], PT[:, h, :], start=True, stop=True)
                last.then_inc(s_s, 1)
            pe.wait_ge(s_sd, S_PV + 2)
            for k in (KD - 2, KD - 1):
                wait_taken(pe, (("w", LO, 1), k))
            pe.wait_ge(s_small, 48)
            for hf in range(2):
                linear_rows(product(2 * LO + hf), hf, weights(LO), outT, ones[0:1, 0:N], bo_row[:, hf * HALF:(hf + 1) * HALF])

            pe.wait_ge(s_ln, 2)
            transpose_rows("x1", ln)
            wait_x_stage(pe, "x1")
            pe.wait_ge(s_csq, 1)
            b = side(S_DIST)
            for k in range(KD):
                nc.tensor.matmul(b[0:N, 0:NE], aT[:, k, :], cols[:, C_CEN + k * NE:C_CEN + (k + 1) * NE],
                                 start=(k == 0), stop=False)
            nc.tensor.matmul(b[0:N, 0:NE], spread(csq[:, 0:1], N), ident[0:NE, 0:NE], start=False, stop=True).then_inc(s_s, 1)
            pe.wait_ge(s_we, 1)
            b = open_bank(("we", 0))
            nc.tensor.transpose(b[0:NE, 0:N], dist[:, 7, :], ident[0:N, 0:N]).then_inc(s_t, 1)
            wait_taken(pe, ("we", 0))
            for hf in range(2):
                b = side(S_WE + hf)
                for i in range(4):
                    last = nc.tensor.matmul(b[:, i * N:(i + 1) * N], spread(ident[0:NE, 4 * hf + i:4 * hf + i + 1], P), weT, start=True, stop=True)
                last.then_inc(s_s, 1)
            for hf in range(2):
                pe.wait_ge(s_od, O_GCN)
                b = acc_bank[hf]
                for c in range(HC):
                    k = hf * HC + c
                    last = nc.tensor.matmul(b[:, c * N:(c + 1) * N], b2_sb[:, k * P:(k + 1) * P], weT,
                                            start=(c == 0), stop=False, skip_group_check=True)
            last.then_inc(s_init, 1)
            for i in range(TINDEX[("q", 0)] - TB, TINDEX[("q", 0)]):
                wait_taken(pe, TGROUPS[i][0])

            def slot_view(g, kind):
                return ring[:, slot_of(g, kind), :]

            def wait_loaded(e, g, kind):
                s = slot_of(g, kind)
                pe.wait_ge(s_full[s], e * (16 * slot_parts(s)) + (half_loaded(LAST[s]) if s < HSLOTS else 0)
                           + 16 * slot_parts_until(g, kind))

            group_of = {c: g for g, cs in enumerate(GROUPS) for c in cs}

            def expand(e, c):
                g, w = group_of[c], CW[c]
                off = (c - GROUPS[g][0]) * P
                gw = group_width(g)
                for kind, b, s_done, s_free in ((GATE, gate_bank[c % 2], s_gate, s_gfree),
                                                (UP, up_bank[c % 2], s_up, s_ufree)):
                    if c == GROUPS[g][0]:
                        wait_loaded(e, g, kind)
                    pe.wait_ge(s_free, e * FC + c + 1)
                    W = slot_view(g, kind)[:, 0:KD * gw].rearrange("p (k w) -> p k w", w=gw)
                    for k in range(KD):
                        last = nc.tensor.matmul(b[0:w, 0:N], W[:, k, off:off + w], aT[:, k, :],
                                                start=(k == 0), stop=(k == KD - 1))
                    last.then_inc(s_done, 1)

            def contract(e, c):
                g, w = group_of[c], CW[c]
                if c == GROUPS[g][0]:
                    wait_loaded(e, g, DOWN)
                pe.wait_ge(s_h, e * FC + c + 1)
                W = slot_view(g, DOWN).rearrange("p (c d) -> p c d", d=D)[0:w, c - GROUPS[g][0], :]
                for k in range(KD):
                    last = nc.tensor.matmul(acc_bank[k // HC][:, (k % HC) * N:(k % HC + 1) * N],
                                            W[:, k * P:(k + 1) * P], hT[0:w, c % 2, :],
                                            start=False, stop=False, skip_group_check=True)
                last.then_inc(s_hfree, 1)

            pe.sem_inc(s_hfree, 2)
            with pe.Fori(0, NE) as e:
                for c in range(FC):
                    expand(e, c)
                    if c >= 1:
                        contract(e, c - 1)
                contract(e, FC - 1)

            pe.wait_ge(s_y, 2)
            for hf in range(2):
                b = side(S_Y + hf)
                for c in range(HC):
                    last = nc.tensor.transpose(b[0:N, c * P:(c + 1) * P], yT[:, hf * HC + c, :], ident[:, :])
                last.then_inc(s_s, 1)
            pe.wait_ge(s_ln, 3)
            for hf in range(2):
                b = side(S_Z + hf)
                for c in range(HC):
                    k = hf * HC + c
                    last = nc.tensor.matmul(b[:, c * N:(c + 1) * N], ln_t[:, k * P:(k + 1) * P], adjT[:, :],
                                            start=True, stop=True)
                last.then_inc(s_s, 1)
            nc.tensor.matmul(side(S_ROW)[0:1, 0:N], ones[0:N, 0:1], adjT[:, :], start=True, stop=True).then_inc(s_s, 1)
            pe.wait_ge(s_z, 1)
            pe.wait_ge(s_gcnb, 16)
            pe.wait_ge(s_sd, S_Z + 2)
            for hf in range(2):
                linear_rows(product(O_GCN + hf), hf, weights(LG), zT, row_sum, gcn_row[:, hf * HALF:(hf + 1) * HALF])
            pe.wait_ge(s_q, 1)
            for hf in range(2):
                b = open_bank(("q", hf))[:, :].bitcast(BF16)
                for c in range(HC):
                    k = hf * HC + c
                    last = nc.tensor.transpose(b[:, c * N:(c + 1) * N], qb[:, k * P:(k + 1) * P], ident_b[0:N, 0:N])
                last.then_inc(s_t, 1)
            wait_x_stage(pe, "q")
            pe.wait_ge(s_rq, 4 * NE)
            for hf in range(2):
                b = product(O_INT8 + hf)
                for k in range(KD):
                    last = nc.tensor.matmul(b[0:N, :], qT[:, k, :], rhs_q[:, k, hf * HALF:(hf + 1) * HALF],
                                            start=(k == 0), stop=(k == KD - 1))
                last.then_inc(s_o, 1)


_INS = ['x', 'src', 'dst', 'edge_type_5', 'L0_gnn_edge_type_weights', 'L0_gnn_wq', 'L0_gnn_bq', 'L0_gnn_wk',
        'L0_gnn_bk', 'L0_gnn_wv', 'L0_gnn_bv', 'L0_gnn_wiq', 'L0_gnn_biq', 'L0_gnn_wik', 'L0_gnn_bik',
        'L0_gnn_wiv', 'L0_gnn_biv', 'L0_gnn_wo', 'L0_gnn_bo', 'L0_ffn_centroid', 'L0_ffn_Wg', 'L0_ffn_bg',
        'L0_ffn_W1', 'L0_ffn_b1', 'L0_ffn_W2', 'L0_ffn_b2', 'L1_gnn_W', 'L1_gnn_b', 'L1_ffn_rhs']
_OUTS = [((96, 1024), 'float32')]


def kernel(**inputs):
    import numpy as _np
    import concourse.bacc as _bacc
    from concourse import mybir as _mybir
    from concourse.bass_utils import run_bass_kernel_spmd as _run

    nc = _bacc.Bacc("TRN2", target_bir_lowering=False, num_devices=1)
    arrays, args = {}, []
    for name in _INS:
        a = _np.ascontiguousarray(inputs[name])
        arrays[f"in_{name}_dram"] = a
        args.append(nc.dram_tensor(f"in_{name}_dram", a.shape, _mybir.dt.from_np(a.dtype), kind="ExternalInput").ap())
    for i, (shape, dtype) in enumerate(_OUTS):
        dt = _mybir.dt.from_np(_np.dtype(dtype))
        args.append(nc.dram_tensor(f"out_{i}_dram", shape, dt, kind="ExternalOutput").ap())
    gnn_moe_gcn_int8_kernel(nc, *args)
    r = _run(nc, [arrays], core_ids=[0])
    got = tuple(r.results[0][f"out_{i}_dram"] for i in range(len(_OUTS)))
    return got[0]
```

```python
import numpy as np
import concourse.bass as bass
from concourse import mybir
from contextlib import ExitStack


def gnn_moe_gcn_int8_kernel(nc, x_in, src_in, dst_in, etype_in, etw_in,
                            wq, bq, wk, bk, wv, bv, wiq, biq, wik, bik, wiv, biv, wo, bo,
                            centroid, Wg, bg, W1, b1, W2, b2, gcn_w, gcn_b, rhs_in, out):
    F32, BF16, I32 = mybir.dt.float32, mybir.dt.bfloat16, mybir.dt.int32
    ALU, ACT, AX = mybir.AluOpType, mybir.ActivationFunctionType, mybir.AxisListType

    P = 128
    N, D = x_in.shape
    KD = D // P
    HALF = D // 2
    HC = HALF // P
    NE, _, FF = Wg.shape
    FC = -(-FF // P)
    CW = [min(P, FF - P * c) for c in range(FC)]
    EDGES = src_in.shape[0]
    EC = EDGES // P
    DH = 64
    HEADS = D // DH
    NTYPES = etw_in.shape[0]
    LN_EPS, NEG, INT8_MAX = 1e-5, -1e30, 127.0
    RMAX = bass.bass_isa.ReduceOp.max
    ROUND = 1.5 * 2.0 ** 23
    SCALE = 1.0 / float(np.sqrt(np.float32(DH)))

    SLOTS, SLOT, RAW = 8, HC * D, 3
    UNIT, UNITS = SLOT // 2, 4
    GROUPS = [range(0, 4), range(4, 8), range(8, 12), range(12, 15), range(15, 19), range(19, 22)]
    NG = len(GROUPS)
    GATE, UP, DOWN = range(3)

    def group_width(g):
        return sum(CW[c] for c in GROUPS[g])

    LAST_STEP = NG * NE - 1

    def first_unit(t):
        return 0 if isinstance(t, int) and t == 0 else 6 * t - 2

    SQUARES = [wq, wiq, wk, wik, wv, wiv, wo, gcn_w]
    LQ, LIQ, LK, LIK, LV, LIV, LO, LG = range(8)
    HALVES = 2 * len(SQUARES)

    HSLOTS = 4
    WT2_SLOT, EARLY_SLOT = 4, 6
    LOAD_ORDER = [LQ, LIQ, LK, LIK, LV, LIV, LG, LO]
    SECOND = (LIQ, LIK, LIV, LO)
    LAST = {s: max(range(s, HALVES, HSLOTS)) for s in range(HSLOTS)}

    QUADRANT_OUT = (LQ, LK, LV)
    Q, B = 4, 32
    QF = D // Q

    TGROUPS = []

    def add_groups(name, n, first=0):
        for k in range(n):
            TGROUPS.append(((name, k), first if first == "a" else "va"[(first + k) % 2]))

    add_groups("x0", 2)
    add_groups("cols", 1, "a")
    add_groups("edges", 1, "a")
    add_groups("probs", 4)
    for hf in range(2):
        add_groups(("w", LO, hf), KD, "a")
    add_groups("x1", 2)
    add_groups("we", 1)
    add_groups("q", 2)
    TINDEX = {name: i for i, (name, _) in enumerate(TGROUPS)}
    TB = 4

    def taken(i):
        who = TGROUPS[i][1]
        return who, sum(w == who for _, w in TGROUPS[:i + 1])

    VECTORS = [bq, biq, bk, bik, bv, biv]
    C_BG = len(VECTORS) * KD
    C_B1 = C_BG + NE * FC
    C_CEN = C_B1 + NE * FC
    NCOLS = C_CEN + KD * NE

    ctx = ExitStack()
    with ctx:
        def sb(name, shape, dt=F32):
            return ctx.enter_context(nc.sbuf_tensor(name, shape, dt))

        def sem(name):
            return ctx.enter_context(nc.semaphore(name))

        ring_at = -(-nc.sbuf_base // 32) * 32
        ring = sb("ring", [P, SLOTS, SLOT])
        assert nc.sbuf_base == ring_at + SLOTS * SLOT * 4
        wt = sb("wt", [P, KD, D])
        arena = sb("arena", [P, 8032])
        x = sb("x", [N, D])
        aT = sb("aT", [P, KD, N])
        cols = sb("cols", [P, NCOLS])
        we_b = sb("we_b", [P, NE, N])
        ident = sb("ident", [P, P])
        ident_b = sb("ident_b", [P, P], BF16)
        ones_b = sb("ones_b", [P, 1], BF16)
        adjT = sb("adjT", [N, N])
        dinv = sb("dinv", [N, 1])
        ones = sb("ones", [P, P])
        stats = sb("stats", [N, 12])
        mv = sb("mv", [N, 4])
        dev = sb("dev", [N, 1])
        sc = sb("sc", [N, 8])

        at = {"arena": 0, "ring": 0}
        places = {"arena": arena[:, :], "ring": ring[:, EARLY_SLOT:SLOTS, :].rearrange("p s n -> p (s n)")}

        def carve(rows, n, dt=F32, place="arena"):
            words = n if dt != BF16 else -(-n // 2)
            v = places[place][0:rows, at[place]:at[place] + words]
            at[place] += words
            return v if dt == F32 else v.bitcast(dt)

        def chunked(v, n):
            return v.rearrange("p (k n) -> p k n", n=n)

        wt2 = ring[:, WT2_SLOT:EARLY_SLOT, :].rearrange("p s (k n) -> p (s k) n", n=D)

        def weights(m):
            return wt2 if m in SECOND else wt[:, :, :]

        ln = carve(N, D)
        b2_sb = carve(NE, D)
        mask = carve(N, N)
        start = at["arena"]
        linT = chunked(carve(P, KD * N), N)
        q2T = chunked(carve(P, KD * N), N)
        k2T = chunked(carve(P, KD * N), N)
        v2 = carve(N, D)
        outT = linT
        end = at["arena"]
        S = chunked(carve(N, HEADS * N, place="ring"), N)
        PT = chunked(carve(N, HEADS * N, place="ring"), N)
        src1h = chunked(carve(P, EC * N, BF16, "ring"), N)
        dst1h = chunked(carve(P, EC * N, BF16, "ring"), N)
        dcode = chunked(carve(P, EC * N, BF16, "ring"), N)
        best = chunked(carve(N, 7 * N, place="ring"), N)
        best_i = carve(N, N, I32, "ring")
        e_int = chunked(carve(EC, 3 * P, I32, "ring"), P)
        eT = chunked(carve(P, 4 * EC, place="ring"), EC)
        at["arena"], at["ring"] = start, 0
        bg_rows = chunked(carve(FC, NE * P), P)
        b1_rows = chunked(carve(FC, NE * P), P)
        vec_rows = carve(C_BG, P)
        sq = carve(NE, D)
        cen = carve(NE, D, place="ring")
        at["arena"] = max(end, at["arena"])
        e_row = chunked(carve(EC, 4 * P), P)
        iota_n = carve(P, N)
        code_base = carve(P, EC)
        tri = carve(P, P)
        junk = chunked(carve(P, 4 * P, BF16), P)
        dup = carve(P, EC)
        code = chunked(carve(P, 2 * EC), EC)
        etw = carve(N, NTYPES)
        spw = chunked(carve(N, 3 * NTYPES), NTYPES)
        mx = chunked(carve(N, 3 * HEADS), HEADS)
        dist = chunked(carve(N, 8 * NE), NE)
        cmp = carve(N, 3 * NE * NE).rearrange("p (a e f) -> p a e f", e=NE, f=NE)
        weT = carve(NE, N)
        csq = carve(NE, 2)
        at["arena"] = 0
        rhs_q = chunked(carve(P, KD * D, BF16), D)
        rblk = chunked(carve(P, KD * P), P)
        rscale = carve(P, D)
        gcn_row = carve(1, D)
        rmax = carve(P, P)
        rinv = chunked(carve(P, 2 * P), P)

        ex_at = [0]

        def expert_buffer(name, shape, dt):
            v = nc.alloc_sbuf_tensor_at(name, [P] + shape, dt, offset=ring_at + ex_at[0])
            ex_at[0] += int(np.prod(shape)) * 4
            assert ex_at[0] <= SLOTS * SLOT * 4
            return v

        F32R = mybir.dt.float32r
        w_hi, w_lo = [], []
        for u, slot in enumerate((EARLY_SLOT, EARLY_SLOT + 1, HSLOTS - 1, WT2_SLOT)):
            ex_at[0] = slot * SLOT * 4
            w_hi.append(expert_buffer(f"w_hi{u}", [UNIT], F32R))
            w_lo.append(expert_buffer(f"w_lo{u}", [UNIT], F32R))
        ex_at[0] = (WT2_SLOT + 1) * SLOT * 4
        x_hi = expert_buffer("x_hi", [KD, N], F32R)
        x_lo = expert_buffer("x_lo", [KD, N], F32R)
        h_hi = expert_buffer("h_hi", [HC, N], F32R)
        h_lo = expert_buffer("h_lo", [HC, N], F32R)
        gate_row = expert_buffer("gate_row", [HALF], F32)
        up_row = expert_buffer("up_row", [HALF], F32)
        silu = expert_buffer("silu", [HC, N], F32)
        hid = expert_buffer("hid", [HC, N], F32)
        assert ex_at[0] <= EARLY_SLOT * SLOT * 4

        ln_t = ring[0:N, 1, 0:D]
        row_sum = ring[0:1, 0, 0:N]
        qf = ring[0:N, 4, 0:D]
        qb = ring[0:N, 4, D:D + D // 2].bitcast(BF16)
        qT = chunked(ring[:, 4, 2 * D:2 * D + KD * N // 2].bitcast(BF16), N)
        res = ring[0:N, 5, 0:D]

        bank = [ctx.enter_context(nc.psum_tensor(f"bank{i}", [P, HALF], F32)) for i in range(8)]
        tbank, obank, sbank = bank[0:4], bank[4:6], bank[6:8]
        gate_bank, up_bank, gateT_bank, upT_bank = tbank
        acc_bank = obank

        s_const = sem("s_const")
        s_rows0 = sem("s_rows0")
        s_x = sem("s_x")
        s_edges = sem("s_edges")
        s_rows = sem("s_rows")
        s_small = sem("s_small")
        s_bo = sem("s_bo")
        s_gcnb = sem("s_gcnb")
        s_rblk = sem("s_rblk")
        s_wt = sem("s_wt")
        s_full = [sem(f"s_full{s}") for s in range(SLOTS)]
        s_t = sem("s_t")
        s_tv = sem("s_tv")
        s_ta = sem("s_ta")
        s_o = sem("s_o")
        s_od = sem("s_od")
        s_s = sem("s_s")
        s_sd = sem("s_sd")
        s_dve = sem("s_dve")
        s_pool = sem("s_pool")
        s_var = sem("s_var")
        s_dev = sem("s_dev")
        s_ln = sem("s_ln")
        s_erow = sem("s_erow")
        s_1h = sem("s_1h")
        s_cval = sem("s_cval")
        s_dcode = sem("s_dcode")
        s_spe = sem("s_spe")
        s_spv = sem("s_spv")
        s_sub = sem("s_sub")
        s_exp = sem("s_exp")
        s_prob = sem("s_prob")
        s_adj = sem("s_adj")
        s_csq = sem("s_csq")
        s_xsq = sem("s_xsq")
        s_gd = sem("s_gd")
        s_ga = sem("s_ga")
        s_we = sem("s_we")
        s_init = sem("s_init")
        s_split_x = sem("s_split_x")
        s_hi = sem("s_hi")
        s_lo = sem("s_lo")
        s_unit = sem("s_unit")
        s_rowsT = sem("s_rowsT")
        s_tr = sem("s_tr")
        s_silu = sem("s_silu")
        s_hid = sem("s_hid")
        s_hf = sem("s_hf")
        s_hh = sem("s_hh")
        s_hl = sem("s_hl")
        s_acc = sem("s_acc")
        s_rmax = sem("s_rmax")
        s_rall = sem("s_rall")
        s_rscale = sem("s_rscale")
        s_rinv = sem("s_rinv")
        s_rq = sem("s_rq")
        s_z = sem("s_z")
        s_q = sem("s_q")
        s_res = sem("s_res")
        s_out = sem("s_out")

        block = ctx.enter_context(nc.Block())

        S_KEY, S_ADJ, S_CODE, S_SC, S_PV, S_DIST, S_WE, S_ROW, S_Z = 0, 6, 7, 13, 17, 19, 20, 22, 23
        O_GCN, O_INT8 = 2 * LG, 2 * LG + 2

        ROW_LOADS = 16 * (len(VECTORS) + 5)

        def half_index(m, hf):
            return 2 * LOAD_ORDER.index(m) + hf

        def half_loads(i):
            return 1 if LOAD_ORDER[i // 2] == LO else Q

        def half_loaded(i):
            return 16 * sum(half_loads(j) for j in range(i % HSLOTS, i + 1, HSLOTS))

        def wait_taken(eng, name):
            who, n = taken(TINDEX[name])
            eng.wait_ge(s_tv if who == "v" else s_ta, n)

        def early_tenants_gone(eng):
            eng.wait_ge(s_sd, S_WE + 2)
            eng.wait_ge(s_init, 1)

        rhs_blocks = rhs_in.rearrange("(k p) (b n) -> b p k n", p=P, n=P)

        RAW_HALVES = {s: half_loaded(LAST[s]) // 16 for s in range(RAW)}

        def raw_slot(t, kind):
            if isinstance(t, int):
                n = kind if t == 0 else 2 + 3 * (t - 1) + kind
                return (n if t <= LAST_STEP else 3 * t - 1) % RAW
            return (2 + kind) % RAW

        def raw_loads(e, s, kind):
            t = NG * e + s
            if isinstance(t, int) and t == 0:
                n = 1
            elif isinstance(t, int) and t > LAST_STEP:
                n = LAST_STEP + 2
            elif kind == GATE:
                n = t
            elif kind == UP:
                n = t + 1
            else:
                n = (NG + 1) * e + s + 1 + s // NG
            slot = raw_slot(t, kind)
            return 16 * (n + RAW_HALVES[slot])

        def down_chunks(g, h):
            chunks, first = GROUPS[g], -(-len(GROUPS[g]) // 2)
            return chunks[first:] if h else chunks[:first]

        def unit_views(t, j, g):
            if isinstance(t, int) and t == 0:
                u = j
            elif isinstance(t, int) and t > LAST_STEP:
                u = first_unit(t) + j - 4
            else:
                s = g + 1 if j >= 4 else g
                u = first_unit(s + NG) + j
            kind, h = j // 2, j % 2
            if isinstance(t, int) and t > LAST_STEP:
                slot = raw_slot(t, GATE)
            else:
                slot = raw_slot(t, kind)
            if kind == DOWN:
                n, w = len(down_chunks(g, h)), D
            else:
                n, w = KD // 2, group_width(g)
            at = h * (len(down_chunks(g, 0)) * D if kind == DOWN else n * w)
            cut = lambda v: v.rearrange("p (k w) -> p k w", w=w)
            assert first_unit(NG + 1) % UNITS == first_unit(1) % UNITS
            u %= UNITS
            return cut(ring[:, slot, at:at + n * w]), cut(w_hi[u][:, 0:n * w]), cut(w_lo[u][:, 0:n * w])

        GCN_UNIT = first_unit(LAST_STEP + 1) + 2
        assert GCN_UNIT % UNITS == 0 and UNITS * UNIT == KD * D

        def gcn_views(u):
            cut = lambda v: v.rearrange("p (k w) -> p k w", w=D)
            return wt[:, 2 * u:2 * u + 2, :], cut(w_hi[u][:, :]), cut(w_lo[u][:, :])

        def wait_x_stage(eng, n):
            wait_taken(eng, (n, 0))
            wait_taken(eng, (n, 1))

        @block.sync
        def _(sp):
            def half_freed(i):
                m, hf = LOAD_ORDER[i // 2], i % 2
                if m != LO:
                    sp.wait_ge(s_wt, i + 1)
                else:
                    sp.wait_ge(s_t, TINDEX[(("w", m, hf), KD - 1)] + 1)

            def small_loads():
                for k, (v, t) in enumerate(((src_in, 0), (dst_in, 1), (etype_in, 2))):
                    sp.dma_start(e_int[:, t, :], v.rearrange("(c j) -> c j", j=P)).then_inc(s_edges, 16)
                sp.wait_ge(s_rows0, 2)
                for i, v in enumerate(VECTORS):
                    rows = vec_rows[i * KD:(i + 1) * KD, :]
                    if i in QUADRANT_OUT:
                        sp.dma_start(rows.rearrange("k (q b) -> k q b", b=B), v.rearrange("(q k b) -> k q b", q=Q, b=B)
                                      ).then_inc(s_rows, 16)
                    else:
                        sp.dma_start(rows, v.rearrange("(k j) -> k j", j=P)).then_inc(s_rows, 16)
                for rows, v in ((bg_rows, bg), (b1_rows, b1)):
                    sp.dma_start(rows[0:FC - 1, :, :], v[:, 0:(FC - 1) * P].rearrange("e (c j) -> c e j", j=P)
                                  ).then_inc(s_rows, 16)
                    sp.dma_start(rows[FC - 1:FC, :, 0:CW[-1]], v[:, (FC - 1) * P:FF].rearrange("e (c j) -> c e j", c=1)
                                  ).then_inc(s_rows, 16)
                sp.dma_start(cen, centroid).then_inc(s_rows, 16)
                sp.dma_start(etw, etw_in.partition_broadcast(N)).then_inc(s_small, 16)
                sp.dma_start(b2_sb, b2).then_inc(s_small, 16)

            sp.dma_start(x[:, :], x_in).then_inc(s_x, 16)
            for i in range(HALVES):
                m, hf, s = LOAD_ORDER[i // 2], i % 2, i % HSLOTS
                if i >= HSLOTS:
                    half_freed(i - HSLOTS)
                if i == 2:
                    small_loads()
                if i == 8:
                    sp.wait_ge(s_t, TINDEX[("x0", 1)] + 1)
                    sp.dma_start(ln, bo.partition_broadcast(N)).then_inc(s_bo, 16)
                if m == LO:
                    sp.dma_start(ring[:, s, :].rearrange("p (c i) -> p c i", i=D),
                                 SQUARES[m][hf * HALF:(hf + 1) * HALF, :].rearrange("(c p) i -> p c i", p=P)
                                 ).then_inc(s_full[s], 16)
                    continue
                w = SQUARES[m].rearrange("(o b) (q i) -> q b o i", b=B, q=Q)
                dst = ring[:, s, :].rearrange("p (o i) -> p o i", i=QF)
                for q in range(Q):
                    nb = HALF // B
                    sp.dma_start(dst[B * q:B * (q + 1), :, :], w[q, :, hf * nb:(hf + 1) * nb, :]
                                 ).then_inc(s_full[s], 16)

            def load_up_like(e, g, slot, src):
                c0, w = GROUPS[g][0] * P, group_width(g)
                sp.dma_start(ring[:, slot, 0:KD * w].rearrange("p (k w) -> p k w", w=w),
                             src[e, :, c0:c0 + w].rearrange("(k p) w -> p k w", p=P)).then_inc(s_full[slot], 16)

            def load_down(e, g, slot):
                w = group_width(g)
                whole, row = w // P, e * FF + GROUPS[g][0] * P
                rows = W2.rearrange("e f d -> (e f) d")
                dst = ring[:, slot, :].rearrange("p (c d) -> p c d", d=D)
                sp.dma_start(dst[:, 0:whole, :], rows[bass.ds(row, whole * P), :].rearrange("(c p) d -> p c d", p=P)
                             ).then_inc(s_full[slot], 16)
                if w % P:
                    sp.dma_start(dst[0:w % P, whole, :], rows[bass.ds(row + whole * P, w % P), :]).then_inc(s_full[slot], 16)

            def raw_free(n):
                sp.wait_ge(s_lo, 2 * n - 2 * RAW + 2)

            def load_step(e, s):
                t = NG * e + s
                n = 3 * t - 1
                raw_free(n + UP)
                load_up_like(e, s % NG, raw_slot(t, UP), W1[s // NG:NE])
                raw_free(n + DOWN)
                load_down(e, s - 1, raw_slot(t, DOWN))
                if not isinstance(t, int) or t < LAST_STEP:
                    raw_free(n + 3)
                    load_up_like(e, (s + 1) % NG, raw_slot(t + 1, GATE), Wg[(s + 1) // NG:NE])
                if s == 2:
                    sp.wait_ge(s_rq, 4 * e + 1)
                    sp.dma_start(rblk, rhs_blocks[e]).then_inc(s_rblk, 16)

            half_freed(LAST[0])
            load_up_like(0, 0, 0, Wg)
            half_freed(LAST[1])
            load_up_like(0, 0, 1, W1)
            half_freed(LAST[2])
            load_up_like(0, 1, 2, Wg)
            with sp.Fori(0, NE - 1) as e:
                for s_ in range(1, NG + 1):
                    load_step(e, s_)
            sp.dma_start(gcn_row, gcn_b.partition_broadcast(1)).then_inc(s_gcnb, 16)
            for s_ in range(1, NG):
                load_step(NE - 1, s_)
            raw_free(3 * (LAST_STEP + 1) - 1)
            load_down(NE - 1, NG - 1, raw_slot(LAST_STEP + 1, GATE))
            for hf in range(2):
                sp.wait_ge(s_res, hf + 1)
                sp.dma_start(out[:, hf * HALF:(hf + 1) * HALF], res[:, hf * HALF:(hf + 1) * HALF]).then_inc(s_out, 16)
            sp.wait_ge(s_out, 32)

        @block.gpsimd
        def _(pool):
            chain = [0]

            def link(ins):
                chain[0] += 1
                ins.then_inc(s_pool, 1)
                pool.wait_ge(s_pool, chain[0])

            nc.gpsimd.memset(bg_rows, 0.0).then_inc(s_rows0, 1)
            nc.gpsimd.memset(b1_rows, 0.0).then_inc(s_rows0, 1)
            link(nc.gpsimd.memset(ident[:, :], 0.0))
            link(nc.gpsimd.affine_select(out=ident[:, :], in_=ident[:, :], compare_op=ALU.not_equal, fill=1.0,
                                         base=0, pattern=[[-1, P]], channel_multiplier=1))
            link(nc.gpsimd.tensor_copy(ident_b[:, :], ident[:, :]))
            nc.gpsimd.memset(ones_b[:, :], 1.0).then_inc(s_const, 1)
            nc.gpsimd.memset(ones[:, :], 1.0).then_inc(s_const, 1)
            pool.wait_ge(s_const, 2)
            nc.gpsimd.affine_select(out=tri, in_=ones[:, :], compare_op=ALU.is_gt, fill=0.0,
                                    base=0, pattern=[[1, P]], channel_multiplier=-1).then_inc(s_const, 1)
            low = cmp[:, 2, :, :]
            nc.gpsimd.affine_select(out=low, in_=ones[0:N, 0:NE * NE].rearrange("p (e f) -> p e f", f=NE),
                                    compare_op=ALU.is_gt, fill=0.0, base=0, pattern=[[1, NE], [-1, NE]],
                                    channel_multiplier=0).then_inc(s_const, 1)
            nc.gpsimd.iota(iota_n, [[1, N]], base=0, channel_multiplier=0,
                           allow_small_or_imprecise_dtypes=True).then_inc(s_const, 1)
            nc.gpsimd.iota(code_base, [[8, EC]], base=8, channel_multiplier=0,
                           allow_small_or_imprecise_dtypes=True).then_inc(s_const, 1)
            pool.wait_ge(s_const, 6)
            wait_taken(pool, ("edges", 0))
            for c in range(EC):
                nc.gpsimd.tensor_scalar(src1h[:, c, :], iota_n, eT[:, 0, c:c + 1], None, ALU.is_equal)
                last = nc.gpsimd.tensor_scalar(dst1h[:, c, :], iota_n, eT[:, 1, c:c + 1], None, ALU.is_equal)
            last.then_inc(s_1h, 1)
            early_tenants_gone(pool)
            pool.sem_inc(s_rq, 1)
            for e in range(NE):
                blk_q = rhs_q.rearrange("p k (b n) -> p b k n", n=P)[:, e, :, :]
                pool.wait_ge(s_rmax, e + 1)
                nc.gpsimd.partition_all_reduce(rinv[:, 1, :], rmax, P, RMAX).then_inc(s_rall, 1)
                pool.wait_ge(s_rinv, e + 1)
                nc.gpsimd.tensor_tensor(rblk, rblk, rinv[:, 0:1, :].to_broadcast([P, KD, P]),
                                        ALU.mult).then_inc(s_rq, 1)
                pool.wait_ge(s_rq, 4 * e + 2)
                nc.gpsimd.tensor_scalar(rblk, rblk, INT8_MAX, -INT8_MAX, ALU.min, ALU.max).then_inc(s_rq, 1)
                pool.wait_ge(s_rq, 4 * e + 3)
                nc.gpsimd.tensor_scalar(rblk, rblk, ROUND, ROUND, ALU.add, ALU.subtract).then_inc(s_rq, 1)
                pool.wait_ge(s_rq, 4 * e + 4)
                nc.gpsimd.tensor_copy(blk_q, rblk).then_inc(s_rq, 1)
                pool.wait_ge(s_rq, 4 * e + 5)

        @block.scalar
        def _(act):
            def deviation(n):
                act.wait_ge(s_var, n + 1)
                nc.scalar.activation(dev[:, :], mv[:, 2:3], ACT.Sqrt).then_inc(s_dev, 1)

            def take(name, dst, src):
                i = TINDEX[name]
                act.wait_ge(s_t, i + 1)
                nc.scalar.copy(dst, src).then_inc(s_ta, 1)

            def take_weights(m, hf):
                for k in range(KD):
                    name = (("w", m, hf), k)
                    if taken(TINDEX[name])[0] == "a":
                        take(name, weights(m)[:, k, hf * HALF:(hf + 1) * HALF], tbank[TINDEX[name] % TB][:, :])

            deviation(0)
            take(("x0", 1), aT[:, HC:KD, :], tbank[1][:, 0:HC * N].rearrange("p (k n) -> p k n", n=N))

            def take_product(m, hf):
                act.wait_ge(s_o, 2 * m + hf + 1)
                if m == LIV:
                    nc.scalar.copy(v2[:, hf * HALF:(hf + 1) * HALF], obank[hf][0:N, :]).then_inc(s_od, 1)
                    return
                dst = q2T if m == LIQ else k2T if m == LIK else linT
                for c in range(HC):
                    k = hf * HC + c
                    last = nc.scalar.activation(dst[:, k, :], obank[hf][:, c * N:(c + 1) * N], ACT.Identity,
                                                bias=cols[:, m * KD + k:m * KD + k + 1])
                last.then_inc(s_od, 1)

            take(("cols", 0), cols[:, :], tbank[2][:, 0:NCOLS])
            wait_taken(act, ("cols", 0))
            for m in range(LIV):
                take_product(m, 0)
                if m == 0:
                    take(("edges", 0), eT, tbank[3][:, 0:4 * EC].rearrange("p (a c) -> p a c", c=EC))
                take_product(m, 1)
                if m == 1:
                    act.wait_ge(s_spv, 1)
                    nc.scalar.activation(spw[:, 1, :], spw[:, 0, :], ACT.Exp).then_inc(s_spe, 1)
                    act.wait_ge(s_spe, 1)
                    nc.scalar.activation(spw[:, 2, :], spw[:, 1, :], ACT.Ln, bias=1.0).then_inc(s_spe, 1)
            act.wait_ge(s_sd, S_ADJ + 1)
            nc.scalar.activation(sc[:, 5:6], sc[:, 1:2], ACT.Sqrt).then_inc(s_adj, 1)
            act.wait_ge(s_sub, 1)
            nc.scalar.activation(S, S, ACT.Exp).then_inc(s_exp, 1)
            take_product(LIV, 0)
            take_product(LIV, 1)
            for j in range(4):
                name = ("probs", j)
                if taken(TINDEX[name])[0] == "a":
                    take(name, PT[:, 4 * j:4 * j + 4, :],
                         tbank[TINDEX[name] % TB][0:N, 0:4 * N].rearrange("p (h n) -> p h n", n=N))
            take_weights(LO, 0)
            take_weights(LO, 1)

            def split(t, j, g, loaded=None):
                if loaded is not None:
                    act.wait_ge(s_full[loaded[0]], loaded[1])
                u = first_unit(t) + j if not (isinstance(t, int) and t > LAST_STEP) else first_unit(t) + j - 4
                if not isinstance(u, int) or u >= UNITS:
                    act.wait_ge(s_unit, u - UNITS + 1)
                raw, hi, _ = unit_views(t, j, g)
                nc.scalar.copy(hi, raw).then_inc(s_hi, 1)

            def step_units(e, s, kind, g):
                t = NG * e + s
                split(t, 2 * kind, g, (raw_slot(t, kind), raw_loads(e, s, kind)))
                split(t, 2 * kind + 1, g)

            act.wait_ge(s_s, S_PV + 2)
            step_units(0, 0, GATE, 0)
            split(0, 2, 0, (raw_slot(0, UP), raw_loads(0, 0, UP)))
            act.wait_ge(s_o, 2 * LO + 2)
            split(0, 3, 0)
            deviation(1)
            act.wait_ge(s_ln, 2)
            nc.scalar.activation(v2, ln, ACT.Square, accum_out=sc[:, 0:1]).then_inc(s_xsq, 1)
            name = ("x1", 1)
            take(name, aT[:, HC:KD, :], tbank[TINDEX[name] % TB][:, 0:HC * N].rearrange("p (k n) -> p k n", n=N))
            wait_x_stage(act, "x1")
            nc.scalar.copy(x_hi[:, :, :], aT[:, :, :]).then_inc(s_split_x, 1)
            act.wait_ge(s_gd, 1)
            nc.scalar.activation(dist[:, 1, :], dist[:, 0, :], ACT.Sqrt).then_inc(s_ga, 1)
            act.wait_ge(s_gd, 2)
            nc.scalar.activation(dist[:, 3, :], dist[:, 2, :], ACT.Exp).then_inc(s_ga, 1)
            def take_row(t, kind, g):
                first = first_unit(t)
                act.wait_ge(s_unit, first + 2 * kind + 2)
                dst, src = ((gate_row, gate_bank), (up_row, up_bank))[kind]
                w = group_width(g)
                nc.scalar.copy(dst[0:N, 0:w], src[0:N, 0:w]).then_inc(s_rowsT, 1)

            def silu_step(e, g):
                act.wait_ge(s_tr, NG * e + g + 1)
                for i, c in enumerate(GROUPS[g]):
                    w = CW[c]
                    last = nc.scalar.activation(silu[0:w, i, :], gateT_bank[0:w, i * N:(i + 1) * N], ACT.Silu,
                                                bias=cols[0:w, bass.ds(e * FC + (C_BG + c), 1)])
                last.then_inc(s_silu, 1)

            def h_high(e, g):
                act.wait_ge(s_hf, NG * e + g + 1)
                n = len(GROUPS[g])
                nc.scalar.copy(h_hi[:, 0:n, :], hid[:, 0:n, :]).then_inc(s_hh, 1)

            def gate_unit(e, s, h):
                t = NG * e + s
                split(t, h, s % NG, None if h else (raw_slot(t, GATE), raw_loads(e, s, GATE)))

            def act_step(e, s):
                t, g = NG * e + s, s % NG
                silu_step(e, s - 1)
                step_units(e, s, UP, g)
                h_high(e, s - 1)
                split(t, 4, s - 1, (raw_slot(t, DOWN), raw_loads(e, s, DOWN)))
                take_row(t, GATE, g)
                split(t, 5, s - 1)
                more = not isinstance(t, int) or t < LAST_STEP
                if more:
                    gate_unit(e, s + 1, 0)
                take_row(t, UP, g)
                if more:
                    gate_unit(e, s + 1, 1)

            gate_unit(0, 1, 0)
            take_row(0, GATE, 0)
            gate_unit(0, 1, 1)
            take_row(0, UP, 0)
            with act.Fori(0, NE - 1) as e:
                for s_ in range(1, NG + 1):
                    act_step(e, s_)
            for s_ in range(1, NG):
                act_step(NE - 1, s_)
            t = LAST_STEP + 1
            split(t, 4, NG - 1, (raw_slot(t, GATE), raw_loads(NE, 0, GATE)))
            split(t, 5, NG - 1)
            silu_step(NE - 1, NG - 1)
            act.wait_ge(s_unit, first_unit(t))
            h_high(NE - 1, NG - 1)


            def split_gcn(u):
                act.wait_ge(s_unit, GCN_UNIT + u - UNITS + 1)
                raw, hi, _ = gcn_views(u)
                nc.scalar.copy(hi, raw).then_inc(s_hi, 1)

            for u in range(3):
                split_gcn(u)
            deviation(2)
            split_gcn(3)
            for hf in range(2):
                act.wait_ge(s_s, S_Z + hf + 1)
                nc.scalar.copy(x_hi[:, hf * HC:(hf + 1) * HC, :], sbank[(S_Z + hf) % 2][:, 0:HC * N]
                               .rearrange("p (k n) -> p k n", n=N)).then_inc(s_z, 1)
            deviation(3)
            name = ("q", 1)
            take(name, qT[:, HC:KD, :], tbank[TINDEX[name] % TB][:, :].bitcast(BF16)[:, 0:HC * N]
                 .rearrange("p (k n) -> p k n", n=N))

        @block.vector
        def _(dve):
            chain = [0]

            def link(ins):
                chain[0] += 1
                ins.then_inc(s_dve, 1)
                dve.wait_ge(s_dve, chain[0])

            def half_stats(h):
                link(nc.vector.bn_stats(stats[:, 6 * h:6 * h + 6], x[:, h * HALF:(h + 1) * HALF]))

            def norm(n, dst, quadrant_order=False):
                link(nc.vector.bn_aggr(mv[:, 0:2], stats[:, :]))
                nc.vector.tensor_scalar(mv[:, 2:3], mv[:, 1:2], LN_EPS, None, ALU.add).then_inc(s_var, 1)
                dve.wait_ge(s_dev, n + 1)
                link(nc.vector.reciprocal(mv[:, 3:4], dev[:, :]))
                if quadrant_order:
                    for q in range(Q):
                        last = nc.vector.tensor_scalar(
                            dst.rearrange("n (k q a) -> n q k a", q=Q, a=B)[:, q],
                            x[:, q * QF:(q + 1) * QF].rearrange("n (k a) -> n k a", a=B), mv[:, 0:1], mv[:, 3:4],
                            ALU.subtract, ALU.mult)
                else:
                    last = nc.vector.tensor_scalar(dst, x[:, :], mv[:, 0:1], mv[:, 3:4], ALU.subtract, ALU.mult)
                last.then_inc(s_ln, 1)

            def take(name, dst, src):
                dve.wait_ge(s_t, TINDEX[name] + 1)
                nc.vector.tensor_copy(dst, src).then_inc(s_tv, 1)

            def chunks(v, n=N):
                return v.rearrange("p (k n) -> p k n", n=n)

            dve.wait_ge(s_x, 16)
            half_stats(0)
            half_stats(1)
            norm(0, ln, True)
            take(("x0", 0), aT[:, 0:HC, :], chunks(tbank[0][:, 0:HC * N]))
            def later_same_edge(j):
                dve.wait_ge(s_s, S_KEY + j + 1)
                if j:
                    dve.wait_ge(s_sd, S_KEY + j)
                for c in range(4):
                    last = (nc.vector.scalar_tensor_tensor(
                        junk[:, c, :], sbank[(S_KEY + j) % 2][:, c * P:(c + 1) * P], eT[:, 3, 4 * j + c:4 * j + c + 1], tri,
                        ALU.is_equal, ALU.mult, accum_out=dup[:, 4 * j + c:4 * j + c + 1]))
                last.then_inc(s_sd, 1)

            def last_edges(j):
                dve.wait_ge(s_s, S_CODE + j + 1)
                nc.vector.reduce_max(best[:, j, :], sbank[(S_CODE + j) % 2][0:N, 0:4 * N]
                                     .rearrange("p (c m) -> p m c", m=N), AX.X).then_inc(s_sd, 1)

            def adjacency():
                b = sbank[S_ADJ % 2]
                dve.wait_ge(s_s, S_ADJ + 1)
                link(nc.vector.tensor_tensor(adjT[:, :], b[0:N, 0:N], ident[0:N, 0:N], ALU.add))
                nc.vector.tensor_scalar(sc[:, 1:2], b[0:N, N:N + 1], 1.0, None, ALU.add).then_inc(s_sd, 1)

            def mask_values():
                dve.wait_ge(s_spe, 2)
                link(nc.vector.scalar_tensor_tensor(etw, etw, 0.0, spw[:, 2, :], ALU.max, ALU.add))
                dve.wait_ge(s_sd, S_CODE + 6)
                link(nc.vector.reduce_max(best[:, 6, :], best[:, 0:6, :].rearrange("p a m -> p m a"), AX.X))
                link(nc.vector.scalar_tensor_tensor(best[:, 6, :], ident[0:N, 0:N], float(NTYPES), best[:, 6, :],
                                                    ALU.mult, ALU.max))
                link(nc.vector.tensor_copy(best_i, best[:, 6, :]))
                link(nc.vector.tensor_scalar(best_i, best_i, 7, None, ALU.bitwise_and))
                link(nc.vector.tensor_copy(best[:, 0, :], best_i))
                link(nc.vector.tensor_scalar(mask, best[:, 0, :], 0.0, NEG, ALU.is_equal, ALU.mult))
                for t in range(NTYPES):
                    link(nc.vector.tensor_scalar(best[:, 1, :], best[:, 0, :], float(t + 1), etw[:, t:t + 1],
                                                 ALU.is_equal, ALU.mult))
                    link(nc.vector.tensor_tensor(mask, mask, best[:, 1, :], ALU.add))

            def scores(r):
                for par in range(2):
                    j = S_SC + 2 * r + par
                    dve.wait_ge(s_s, j + 1)
                    nc.vector.scalar_tensor_tensor(
                        S[:, 8 * r + par:8 * r + 8:2, :], chunks(sbank[j % 2][0:N, 0:4 * N]), SCALE,
                        mask.rearrange("p (a m) -> p a m", a=1).to_broadcast([N, 4, N]),
                        ALU.mult, ALU.add).then_inc(s_sd, 1)

            def heads(v):
                return v.rearrange("p (h m) -> p h m", m=1).to_broadcast([N, HEADS, N])

            def softmax_a():
                dve.wait_ge(s_sd, S_SC + 4)
                link(nc.vector.reduce_max(mx[:, 0, :], S, AX.X))
                nc.vector.tensor_tensor(S, S, heads(mx[:, 0, :]), ALU.subtract).then_inc(s_sub, 1)

            def softmax_b():
                dve.wait_ge(s_exp, 1)
                link(nc.vector.reduce_sum(mx[:, 1, :], S, AX.X))
                link(nc.vector.reciprocal(mx[:, 2, :], mx[:, 1, :]))
                nc.vector.tensor_tensor(S, S, heads(mx[:, 2, :]), ALU.mult).then_inc(s_prob, 1)

            def side_work(f):
                if f < 3:
                    later_same_edge(2 * f)
                    later_same_edge(2 * f + 1)
                if f == 2:
                    dve.wait_ge(s_sd, S_KEY + 6)
                    nc.vector.scalar_tensor_tensor(code[:, 1, :], dup, 0.0, code[:, 0, :], ALU.is_equal,
                                                   ALU.mult).then_inc(s_cval, 1)
                    dve.wait_ge(s_cval, 1)
                    dve.wait_ge(s_1h, 1)
                    nc.vector.tensor_tensor(dcode, dst1h, code[:, 1, :].rearrange("p (c n) -> p c n", n=1)
                                            .to_broadcast([P, EC, N]), ALU.mult).then_inc(s_dcode, 1)
                if f == 3:
                    adjacency()
                if 4 <= f < 7:
                    last_edges(2 * (f - 4))
                    last_edges(2 * (f - 4) + 1)
                if f == 6:
                    mask_values()
                if f == 7:
                    scores(0)
                if f == 8:
                    scores(1)

            def transpose_weights(i):
                m, hf = LOAD_ORDER[i // 2], i % 2
                s = i % HSLOTS
                dve.wait_ge(s_full[s], half_loaded(i))
                if i >= 4:
                    dve.wait_ge(s_o, 2 * (i // 2 - 2) + 2)
                nb = HALF // B
                src = ring[:, s, :].rearrange("p (o k a) -> p k o a", k=KD, a=B)
                for k in range(KD):
                    row = weights(m)[:, k, :]
                    if m in QUADRANT_OUT:
                        dst = row.rearrange("p (j r b) -> p r j b", r=Q, b=B)[:, 2 * hf:2 * hf + 2]
                        last = nc.vector.transpose(dst, src[:, k].rearrange("p (r j) a -> p r j a", r=2))
                    else:
                        dst = row[:, hf * HALF:(hf + 1) * HALF].rearrange("p (o b) -> p o b", b=B)
                        last = nc.vector.transpose(dst, src[:, k])
                last.then_inc(s_wt, 1)

            def edge_rows():
                dve.wait_ge(s_edges, 48)
                link(nc.vector.tensor_copy(e_row[:, 0:3, :], e_int))
                nc.vector.scalar_tensor_tensor(e_row[:, 3, :], e_row[:, 0, :], float(N), e_row[:, 1, :],
                                               ALU.mult, ALU.add).then_inc(s_erow, 1)
                dve.wait_ge(s_rows, ROW_LOADS)
                nc.vector.scalar_tensor_tensor(sq, cen, -0.5, cen, ALU.mult, ALU.mult,
                                               accum_out=csq[:, 0:1]).then_inc(s_csq, 1)
                dve.wait_ge(s_small, 32)
                link(nc.vector.tensor_scalar(spw[:, 0, :], etw, -1.0, None, ALU.mult))
                nc.vector.tensor_tensor(spw[:, 0, :], spw[:, 0, :], etw, ALU.min).then_inc(s_spv, 1)

            def edge_codes():
                dve.wait_ge(s_const, 6)
                wait_taken(dve, ("edges", 0))
                link(nc.vector.tensor_scalar(code[:, 0, :], eT[:, 2, :], 0.0, float(NTYPES), ALU.is_equal, ALU.mult))
                link(nc.vector.tensor_tensor(code[:, 0, :], code[:, 0, :], eT[:, 2, :], ALU.add))
                link(nc.vector.tensor_tensor(code[:, 0, :], code[:, 0, :], code_base, ALU.add))

            for i in range(4):
                transpose_weights(i)
                if i == 1:
                    edge_rows()
            edge_codes()
            for i in range(4, 2 * LIV):
                side_work(i - 4)
                transpose_weights(i)
            side_work(2 * LIV - 4)
            transpose_weights(2 * LIV)
            side_work(7)
            transpose_weights(2 * LIV + 1)
            side_work(8)
            softmax_a()
            dve.wait_ge(s_bo, 16)
            link(nc.vector.tensor_tensor(x[:, :], x[:, :], ln, ALU.add))
            transpose_weights(half_index(LG, 0))
            softmax_b()
            transpose_weights(half_index(LG, 1))
            for j in range(4):
                name = ("probs", j)
                if taken(TINDEX[name])[0] == "v":
                    take(name, PT[:, 4 * j:4 * j + 4, :], chunks(tbank[TINDEX[name] % TB][0:N, 0:4 * N]))
            for hf in range(2):
                j = S_PV + hf
                dve.wait_ge(s_s, j + 1)
                nc.vector.tensor_tensor(outT[:, hf * HC:(hf + 1) * HC, :], chunks(sbank[j % 2][:, 0:HC * N]),
                                        cols[:, LIV * KD + hf * HC:LIV * KD + (hf + 1) * HC]
                                        .rearrange("p (k n) -> p k n", n=1).to_broadcast([P, HC, N]),
                                        ALU.add).then_inc(s_sd, 1)
            def split(t, j, g):
                u = first_unit(t) + j if not (isinstance(t, int) and t > LAST_STEP) else first_unit(t) + j - 4
                dve.wait_ge(s_hi, u + 1)
                raw, hi, lo = unit_views(t, j, g)
                nc.vector.tensor_tensor(lo, raw, hi.bitcast(F32), ALU.subtract).then_inc(s_lo, 1)

            for j in range(3):
                split(0, j, 0)
            for hf in range(2):
                xs = x[:, hf * HALF:(hf + 1) * HALF]
                dve.wait_ge(s_o, 2 * LO + hf + 1)
                nc.vector.tensor_tensor(xs, xs, obank[hf][0:N, :], ALU.add).then_inc(s_od, 1)
                dve.wait_ge(s_od, 2 * LO + hf + 1)
                half_stats(hf)
            norm(1, ln)
            name = ("x1", 0)
            take(name, aT[:, 0:HC, :], chunks(tbank[TINDEX[name] % TB][:, 0:HC * N]))

            split(0, 3, 0)

            dve.wait_ge(s_s, S_DIST + 1)
            dve.wait_ge(s_xsq, 1)
            nc.vector.tensor_scalar(dist[:, 4, :], sbank[S_DIST % 2][0:N, 0:NE], -2.0, sc[:, 0:1],
                                    ALU.mult, ALU.add).then_inc(s_sd, 1)
            dve.wait_ge(s_sd, S_DIST + 1)
            nc.vector.tensor_scalar(dist[:, 0, :], dist[:, 4, :], 1e-12, None, ALU.max).then_inc(s_gd, 1)
            dve.wait_ge(s_split_x, 1)
            nc.vector.tensor_tensor(x_lo[:, :, :], aT[:, :, :], x_hi[:, :, :].bitcast(F32), ALU.subtract
                                    ).then_inc(s_split_x, 1)
            dve.wait_ge(s_ga, 1)
            link(nc.vector.reduce_max(sc[:, 2:3], dist[:, 1, :], AX.X))
            nc.vector.tensor_scalar(dist[:, 2, :], dist[:, 1, :], sc[:, 2:3], None, ALU.subtract).then_inc(s_gd, 1)
            mine = dist[:, 1, :].rearrange("p (e f) -> p e f", f=1).to_broadcast([N, NE, NE])
            other = dist[:, 1:2, :].to_broadcast([N, NE, NE])
            link(nc.vector.tensor_tensor(cmp[:, 0, :, :], other, mine, ALU.is_equal))
            link(nc.vector.tensor_tensor(cmp[:, 0, :, :], cmp[:, 0, :, :], cmp[:, 2, :, :], ALU.mult))
            link(nc.vector.tensor_tensor(cmp[:, 1, :, :], other, mine, ALU.is_gt))
            link(nc.vector.tensor_tensor(cmp[:, 1, :, :], cmp[:, 0, :, :], cmp[:, 1, :, :], ALU.add))
            link(nc.vector.reduce_sum(dist[:, 5, :], cmp[:, 1, :, :], AX.X))
            dve.wait_ge(s_ga, 2)
            link(nc.vector.scalar_tensor_tensor(dist[:, 6, :], dist[:, 5, :], 2.0, dist[:, 3, :], ALU.is_lt,
                                                ALU.mult, accum_out=sc[:, 3:4]))
            link(nc.vector.reciprocal(sc[:, 4:5], sc[:, 3:4]))
            nc.vector.tensor_scalar(dist[:, 7, :], dist[:, 6, :], sc[:, 4:5], None, ALU.mult).then_inc(s_we, 1)
            split(1, 0, 1)
            split(1, 1, 1)
            take(("we", 0), weT, tbank[TINDEX[("we", 0)] % TB][0:NE, 0:N])
            for hf in range(2):
                j = S_WE + hf
                dve.wait_ge(s_s, j + 1)
                nc.vector.tensor_copy(we_b[:, hf * 4:hf * 4 + 4, :], chunks(sbank[j % 2][:, 0:4 * N])
                                      ).then_inc(s_sd, 1)
            dve.wait_ge(s_adj, 1)
            link(nc.vector.reciprocal(dinv[:, :], sc[:, 5:6]))
            link(nc.vector.tensor_scalar(adjT[:, :], adjT[:, :], dinv[:, :], None, ALU.mult))

            def gated(e, g):
                t = NG * e + g
                dve.wait_ge(s_silu, t + 1)
                for i, c in enumerate(GROUPS[g]):
                    w = CW[c]
                    last = nc.vector.scalar_tensor_tensor(hid[0:w, i, :], upT_bank[0:w, i * N:(i + 1) * N],
                                                          cols[0:w, bass.ds(e * FC + (C_B1 + c), 1)],
                                                          silu[0:w, i, :], ALU.add, ALU.mult)
                last.then_inc(s_hid, 1)
                dve.wait_ge(s_hid, t + 1)
                n = len(GROUPS[g])
                nc.vector.tensor_tensor(hid[:, 0:n, :], hid[:, 0:n, :],
                                        we_b[:, bass.ds(e, 1), :].to_broadcast([P, n, N]), ALU.mult).then_inc(s_hf, 1)

            def h_low(e, g):
                dve.wait_ge(s_hh, NG * e + g + 1)
                n = len(GROUPS[g])
                nc.vector.tensor_tensor(h_lo[:, 0:n, :], hid[:, 0:n, :], h_hi[:, 0:n, :].bitcast(F32),
                                        ALU.subtract).then_inc(s_hl, 1)

            def rhs_maxima(e):
                dve.wait_ge(s_rblk, 16 * e + 16)
                nc.vector.tensor_reduce(rmax, rblk.rearrange("p k n -> p n k"), AX.X, ALU.max,
                                        apply_absolute_value=True).then_inc(s_rmax, 1)

            def rhs_scales(e):
                dve.wait_ge(s_rall, e + 1)
                nc.vector.tensor_scalar(rmax, rinv[:, 1, :], 1e-12, 1.0 / INT8_MAX,
                                        ALU.max, ALU.mult).then_inc(s_rscale, 1)
                dve.wait_ge(s_rscale, e + 1)
                nc.vector.reciprocal(rinv[:, 0, :], rmax).then_inc(s_rinv, 1)
                nc.vector.tensor_copy(rscale[:, bass.ts(e, P)], rmax)

            def dve_step(e, s):
                t, g = NG * e + s, s % NG
                gated(e, s - 1)
                split(t, 2, g)
                split(t, 3, g)
                h_low(e, s - 1)
                split(t, 4, s - 1)
                if s == 3:
                    rhs_maxima(e)
                if s == 4:
                    rhs_scales(e)
                split(t, 5, s - 1)
                if not isinstance(t, int) or t < LAST_STEP:
                    split(t + 1, 0, (s + 1) % NG)
                    split(t + 1, 1, (s + 1) % NG)

            with dve.Fori(0, NE - 1) as e:
                for s_ in range(1, NG + 1):
                    dve_step(e, s_)
            for s_ in range(1, NG):
                dve_step(NE - 1, s_)
            split(LAST_STEP + 1, 4, NG - 1)
            gated(NE - 1, NG - 1)
            h_low(NE - 1, NG - 1)
            split(LAST_STEP + 1, 5, NG - 1)

            def split_gcn(u):
                dve.wait_ge(s_hi, GCN_UNIT + u + 1)
                raw, hi, lo = gcn_views(u)
                nc.vector.tensor_tensor(lo, raw, hi.bitcast(F32), ALU.subtract).then_inc(s_lo, 1)

            dve.wait_ge(s_s, S_ROW + 1)
            nc.vector.tensor_copy(row_sum, sbank[S_ROW % 2][0:1, 0:N]).then_inc(s_sd, 1)
            split_gcn(0)
            for hf in range(2):
                xs = x[:, hf * HALF:(hf + 1) * HALF]
                dve.wait_ge(s_unit, GCN_UNIT)
                nc.vector.tensor_tensor(xs, xs, acc_bank[hf][0:N, :], ALU.add).then_inc(s_acc, 1)
                dve.wait_ge(s_acc, hf + 1)
                half_stats(hf)
            norm(2, ln_t, quadrant_order=True)
            split_gcn(1)
            for hf in range(2):
                half = slice(hf * HC, (hf + 1) * HC)
                dve.wait_ge(s_z, hf + 1)
                nc.vector.tensor_tensor(x_lo[:, half, :], chunks(sbank[(S_Z + hf) % 2][:, 0:HC * N]),
                                        x_hi[:, half, :].bitcast(F32), ALU.subtract).then_inc(s_sd, 1)
            split_gcn(2)
            split_gcn(3)
            for hf in range(2):
                xs = x[:, hf * HALF:(hf + 1) * HALF]
                dve.wait_ge(s_o, O_GCN + hf + 1)
                nc.vector.scalar_tensor_tensor(xs, obank[hf][0:N, :], dinv[:, :], xs, ALU.mult,
                                               ALU.add).then_inc(s_od, 1)
                dve.wait_ge(s_od, O_GCN + hf + 1)
                half_stats(hf)
            norm(3, qf)
            dve.wait_ge(s_ln, 4)
            link(nc.vector.tensor_reduce(sc[:, 5:6], qf, AX.X, ALU.max, apply_absolute_value=True))
            link(nc.vector.tensor_scalar(sc[:, 6:7], sc[:, 5:6], 1e-12, 1.0 / INT8_MAX, ALU.max, ALU.mult))
            link(nc.vector.reciprocal(sc[:, 7:8], sc[:, 6:7]))
            link(nc.vector.tensor_scalar(qf, qf, sc[:, 7:8], INT8_MAX, ALU.mult, ALU.min))
            link(nc.vector.tensor_scalar(qf, qf, -INT8_MAX, ROUND, ALU.max, ALU.add))
            nc.vector.tensor_scalar(qb, qf, ROUND, None, ALU.subtract).then_inc(s_q, 1)
            name = ("q", 0)
            take(name, qT[:, 0:HC, :], chunks(tbank[TINDEX[name] % TB][:, :].bitcast(BF16)[:, 0:HC * N]))
            for hf in range(2):
                cut = slice(hf * HALF, (hf + 1) * HALF)
                dve.wait_ge(s_o, O_INT8 + hf + 1)
                link(nc.vector.scalar_tensor_tensor(res[:, cut], obank[hf][0:N, :], sc[:, 6:7], rscale[0:N, cut],
                                                    ALU.mult, ALU.mult))
                nc.vector.tensor_tensor(res[:, cut], res[:, cut], x[:, cut], ALU.add).then_inc(s_res, 1)

        @block.tensor
        def _(pe):
            def open_bank(name):
                i = TINDEX[name]
                if i >= TB:
                    who, n = taken(i - TB)
                    pe.wait_ge(s_tv if who == "v" else s_ta, n)
                return tbank[i % TB]

            def transpose_weights(m, hf):
                i = half_index(m, hf)
                s = i % HSLOTS
                pe.wait_ge(s_full[s], half_loaded(i))
                for k in range(KD):
                    b = open_bank((("w", m, hf), k))
                    for c in range(HC):
                        last = nc.tensor.transpose(b[:, c * P:(c + 1) * P],
                                                   ring[:, s, c * D + k * P:c * D + (k + 1) * P], ident[:, :])
                    last.then_inc(s_t, 1)

            def transpose_rows(name, src):
                for hf in range(2):
                    b = open_bank((name, hf))
                    for c in range(HC):
                        k = hf * HC + c
                        last = nc.tensor.transpose(b[:, c * N:(c + 1) * N], src[:, k * P:(k + 1) * P],
                                                   ident[0:N, 0:N])
                    last.then_inc(s_t, 1)

            def side(j):
                if j >= 2:
                    pe.wait_ge(s_sd, j - 1)
                return sbank[j % 2]

            def product(j):
                if j >= 2:
                    pe.wait_ge(s_od, j - 1)
                return obank[j % 2]

            def linear_T(m, hf, src):
                b = product(2 * m + hf)
                w = weights(m)
                for c in range(HC):
                    col = hf * HALF + c * P
                    for k in range(KD):
                        last = nc.tensor.matmul(b[:, c * N:(c + 1) * N], w[:, k, col:col + P],
                                                src[:, k, :], start=(k == 0), stop=(k == KD - 1))
                last.then_inc(s_o, 1)

            def linear_rows(b, hf, w, src):
                for k in range(KD):
                    last = nc.tensor.matmul(b[0:N, :], src[:, k, :], w[:, k, hf * HALF:(hf + 1) * HALF],
                                            start=(k == 0), stop=(k == KD - 1))
                last.then_inc(s_o, 1)


            pe.wait_ge(s_const, 1)
            pe.wait_ge(s_ln, 1)
            transpose_rows("x0", ln)
            pe.wait_ge(s_rows, ROW_LOADS)
            b = open_bank(("cols", 0))
            nc.tensor.transpose(b[:, 0:C_BG], vec_rows, ident[0:C_BG, 0:C_BG])
            for first, rows in ((C_BG, bg_rows), (C_B1, b1_rows)):
                for e in range(NE):
                    nc.tensor.transpose(b[:, first + e * FC:first + (e + 1) * FC], rows[:, e, :], ident[0:FC, 0:FC])
            for k in range(KD):
                last = nc.tensor.transpose(b[:, C_CEN + k * NE:C_CEN + (k + 1) * NE], cen[:, k * P:(k + 1) * P],
                                           ident[0:NE, 0:NE])
            last.then_inc(s_t, 1)

            def spread(column, n):
                return column.to_broadcast([column.shape[0], n])

            def spread_keys(j):
                b = side(S_KEY + j)
                for c in range(4):
                    last = nc.tensor.matmul(b[:, c * P:(c + 1) * P], spread(ident[0:EC, 4 * j + c:4 * j + c + 1], P), e_row[:, 3, :],
                                            start=True, stop=True)
                last.then_inc(s_s, 1)

            def count_edges():
                b = side(S_ADJ)
                for c in range(EC):
                    nc.tensor.matmul(b[0:N, 0:N], dst1h[:, c, :], src1h[:, c, :], start=(c == 0), stop=(c == EC - 1))
                for c in range(EC):
                    last = nc.tensor.matmul(b[0:N, N:N + 1], src1h[:, c, :], ones_b[:, 0:1], start=(c == 0),
                                            stop=(c == EC - 1))
                last.then_inc(s_s, 1)

            def spread_codes(j):
                b = side(S_CODE + j)
                for c in range(4):
                    last = nc.tensor.matmul(b[0:N, c * N:(c + 1) * N], src1h[:, 4 * j + c, :],
                                            dcode[:, 4 * j + c, :], start=True, stop=True)
                last.then_inc(s_s, 1)

            def scores(r):
                for par in range(2):
                    b = side(S_SC + 2 * r + par)
                    rows = slice(DH * par, DH * (par + 1))
                    for i in range(4):
                        last = nc.tensor.matmul(b[0:N, i * N:(i + 1) * N], q2T[rows, 4 * r + i, :],
                                                k2T[rows, 4 * r + i, :], start=True, stop=True)
                    last.then_inc(s_s, 1)

            def side_work(f):
                if f == 0:
                    b = open_bank(("edges", 0))
                    pe.wait_ge(s_erow, 1)
                    for a in range(4):
                        last = nc.tensor.transpose(b[:, a * EC:(a + 1) * EC], e_row[:, a, :], ident[0:EC, 0:EC])
                    last.then_inc(s_t, 1)
                if f < 3:
                    spread_keys(2 * f)
                    spread_keys(2 * f + 1)
                if f == 3:
                    pe.wait_ge(s_1h, 1)
                    count_edges()
                if f == 4:
                    pe.wait_ge(s_dcode, 1)
                if 4 <= f < 7:
                    spread_codes(2 * (f - 4))
                    spread_codes(2 * (f - 4) + 1)
                if f == 7:
                    pe.wait_ge(s_od, 2 * LIK + 2)
                    scores(0)
                if f == 8:
                    scores(1)

            for m in range(LO):
                if m in QUADRANT_OUT:
                    wait_x_stage(pe, "x0")
                else:
                    pe.wait_ge(s_od, 2 * m)
                for hf in range(2):
                    pe.wait_ge(s_wt, 2 * m + 2 if m in QUADRANT_OUT else 2 * m + hf + 1)
                    if m == LIV:
                        linear_rows(product(2 * m + hf), hf, weights(m), linT)
                    else:
                        linear_T(m, hf, aT if m in QUADRANT_OUT else linT)
                    side_work(2 * m + hf)
            pe.wait_ge(s_prob, 1)
            for j in range(4):
                b = open_bank(("probs", j))
                for i in range(4):
                    last = nc.tensor.transpose(b[0:N, i * N:(i + 1) * N], S[:, 4 * j + i, :], ident[0:N, 0:N])
                last.then_inc(s_t, 1)
            transpose_weights(LO, 0)
            for j in range(4):
                wait_taken(pe, ("probs", j))
            pe.wait_ge(s_od, 2 * LIV + 2)
            for hf in range(2):
                b = side(S_PV + hf)
                for h in range(8 * hf, 8 * hf + 8):
                    last = nc.tensor.matmul(b[DH * (h % 2):DH * (h % 2 + 1), (h // 2 % 4) * N:(h // 2 % 4 + 1) * N],
                                            v2[:, h * DH:(h + 1) * DH], PT[:, h, :], start=True, stop=True)
                last.then_inc(s_s, 1)
            transpose_weights(LO, 1)
            pe.wait_ge(s_sd, S_PV + 2)
            for k in (KD - 2, KD - 1):
                wait_taken(pe, (("w", LO, 1), k))
            for hf in range(2):
                linear_rows(product(2 * LO + hf), hf, weights(LO), outT)

            def multiply(b, x_parts, w_parts, start, stop):
                for i, (xp, wp) in enumerate(((0, 0), (1, 0), (0, 1))):
                    last = nc.tensor.matmul(b, x_parts[xp], w_parts[wp], start=(start and i == 0),
                                            stop=(stop and i == 2))
                return last

            def wide(t, kind, g, first):
                b = (gate_bank, up_bank)[kind]
                w = group_width(g)
                for h in range(2):
                    pe.wait_ge(s_lo, first + 2 * kind + h + 1)
                    _, hi, lo = unit_views(t, 2 * kind + h, g)
                    for i in range(KD // 2):
                        k = h * (KD // 2) + i
                        last = multiply(b[0:N, 0:w], (x_hi[:, k, :], x_lo[:, k, :]), (hi[:, i, :], lo[:, i, :]),
                                        k == 0, k == KD - 1)
                    last.then_inc(s_unit, 1)

            def down(t, h, g, u, end=False):
                pe.wait_ge(s_lo, u + 1)
                _, hi, lo = unit_views(t, 4 + h, g)
                chunks_ = down_chunks(g, h)
                for i, c in enumerate(chunks_):
                    at = c - GROUPS[g][0]
                    rows = slice(0, CW[c])
                    for hf in range(2):
                        cut = slice(hf * HALF, (hf + 1) * HALF)
                        last = multiply(acc_bank[hf][0:N, :], (h_hi[rows, at, :], h_lo[rows, at, :]),
                                        (hi[rows, i, cut], lo[rows, i, cut]), False, end and i == len(chunks_) - 1)
                last.then_inc(s_unit, 1)

            def to_columns(t, g):
                pe.wait_ge(s_rowsT, 2 * t + 2)
                for row, b in ((gate_row, gateT_bank), (up_row, upT_bank)):
                    for i, c in enumerate(GROUPS[g]):
                        last = nc.tensor.transpose(b[0:CW[c], i * N:(i + 1) * N], row[0:N, i * P:i * P + CW[c]],
                                                   ident[0:N, 0:N])
                last.then_inc(s_tr, 1)

            def pe_step(e, s):
                t, g = NG * e + s, s % NG
                first = first_unit(t)
                wide(t, GATE, g, first)
                wide(t, UP, g, first)
                pe.wait_ge(s_hl, t)
                down(t, 0, s - 1, first + 4)
                to_columns(t, g)
                down(t, 1, s - 1, first + 5)

            pe.wait_ge(s_ln, 2)
            transpose_rows("x1", ln)
            wait_x_stage(pe, "x1")
            pe.wait_ge(s_csq, 1)
            b = side(S_DIST)
            for k in range(KD):
                nc.tensor.matmul(b[0:N, 0:NE], aT[:, k, :], cols[:, C_CEN + k * NE:C_CEN + (k + 1) * NE],
                                 start=(k == 0), stop=False)
            nc.tensor.matmul(b[0:N, 0:NE], spread(csq[:, 0:1], N), ident[0:NE, 0:NE], start=False, stop=True).then_inc(s_s, 1)

            pe.wait_ge(s_split_x, 2)
            wide(0, GATE, 0, 0)
            wide(0, UP, 0, 0)
            pe.wait_ge(s_we, 1)
            b = open_bank(("we", 0))
            nc.tensor.transpose(b[0:NE, 0:N], dist[:, 7, :], ident[0:N, 0:N]).then_inc(s_t, 1)
            wait_taken(pe, ("we", 0))
            for i in range(TINDEX[("q", 0)] - TB, TINDEX[("q", 0)]):
                wait_taken(pe, TGROUPS[i][0])
            to_columns(0, 0)
            for hf in range(2):
                b = side(S_WE + hf)
                for i in range(4):
                    last = nc.tensor.matmul(b[:, i * N:(i + 1) * N], spread(ident[0:NE, 4 * hf + i:4 * hf + i + 1], P), weT, start=True, stop=True)
                last.then_inc(s_s, 1)
            pe.wait_ge(s_od, O_GCN)
            for hf in range(2):
                last = nc.tensor.matmul(acc_bank[hf][0:N, :], weT, b2_sb[:, hf * HALF:(hf + 1) * HALF],
                                        start=True, stop=False)
            last.then_inc(s_init, 1)
            with pe.Fori(0, NE - 1) as e:
                for s_ in range(1, NG + 1):
                    pe_step(e, s_)
            for s_ in range(1, NG):
                pe_step(NE - 1, s_)
            nc.tensor.matmul(side(S_ROW)[0:1, 0:N], ones[0:N, 0:1], adjT[:, :], start=True, stop=True).then_inc(s_s, 1)
            t = LAST_STEP + 1
            pe.wait_ge(s_hl, t)
            down(t, 0, NG - 1, first_unit(t))
            down(t, 1, NG - 1, first_unit(t) + 1, end=True)

            pe.wait_ge(s_gcnb, 16)
            pe.wait_ge(s_sd, S_ROW + 1)
            for hf in range(2):
                pe.wait_ge(s_acc, hf + 1)
                nc.tensor.matmul(obank[hf][0:N, :], row_sum, gcn_row[:, hf * HALF:(hf + 1) * HALF],
                                 start=True, stop=False)
            pe.wait_ge(s_ln, 3)
            for hf in range(2):
                b = side(S_Z + hf)
                for c in range(HC):
                    k = hf * HC + c
                    last = nc.tensor.matmul(b[:, c * N:(c + 1) * N], ln_t[:, k * P:(k + 1) * P], adjT[:, :],
                                            start=True, stop=True)
                last.then_inc(s_s, 1)
            for hf in range(2):
                for u in range(UNITS):
                    if hf == 0 and u % 2 == 0:
                        pe.wait_ge(s_sd, S_Z + u // 2 + 1)
                    pe.wait_ge(s_lo, GCN_UNIT + u + 1)
                    _, hi, lo = gcn_views(u)
                    cut = slice(hf * HALF, (hf + 1) * HALF)
                    for i in range(2):
                        k = 2 * u + i
                        last = multiply(obank[hf][0:N, :], (x_hi[:, k, :], x_lo[:, k, :]),
                                        (hi[:, i, cut], lo[:, i, cut]), False, k == KD - 1)
                last.then_inc(s_o, 1)
            pe.wait_ge(s_q, 1)
            for hf in range(2):
                b = open_bank(("q", hf))[:, :].bitcast(BF16)
                for c in range(HC):
                    k = hf * HC + c
                    last = nc.tensor.transpose(b[:, c * N:(c + 1) * N], qb[:, k * P:(k + 1) * P], ident_b[0:N, 0:N])
                last.then_inc(s_t, 1)
            wait_x_stage(pe, "q")
            pe.wait_ge(s_rq, 4 * NE + 1)
            for hf in range(2):
                b = product(O_INT8 + hf)
                for k in range(KD):
                    last = nc.tensor.matmul(b[0:N, :], qT[:, k, :], rhs_q[:, k, hf * HALF:(hf + 1) * HALF],
                                            start=(k == 0), stop=(k == KD - 1))
                last.then_inc(s_o, 1)


_INS = ['x', 'src', 'dst', 'edge_type_5', 'L0_gnn_edge_type_weights', 'L0_gnn_wq', 'L0_gnn_bq', 'L0_gnn_wk',
        'L0_gnn_bk', 'L0_gnn_wv', 'L0_gnn_bv', 'L0_gnn_wiq', 'L0_gnn_biq', 'L0_gnn_wik', 'L0_gnn_bik',
        'L0_gnn_wiv', 'L0_gnn_biv', 'L0_gnn_wo', 'L0_gnn_bo', 'L0_ffn_centroid', 'L0_ffn_Wg', 'L0_ffn_bg',
        'L0_ffn_W1', 'L0_ffn_b1', 'L0_ffn_W2', 'L0_ffn_b2', 'L1_gnn_W', 'L1_gnn_b', 'L1_ffn_rhs']
_OUTS = [((96, 1024), 'float32')]


def kernel(**inputs):
    import numpy as _np
    import concourse.bacc as _bacc
    from concourse import mybir as _mybir
    from concourse.bass_utils import run_bass_kernel_spmd as _run

    nc = _bacc.Bacc("TRN2", target_bir_lowering=False, num_devices=1)
    arrays, args = {}, []
    for name in _INS:
        a = _np.ascontiguousarray(inputs[name])
        arrays[f"in_{name}_dram"] = a
        args.append(nc.dram_tensor(f"in_{name}_dram", a.shape, _mybir.dt.from_np(a.dtype), kind="ExternalInput").ap())
    for i, (shape, dtype) in enumerate(_OUTS):
        dt = _mybir.dt.from_np(_np.dtype(dtype))
        args.append(nc.dram_tensor(f"out_{i}_dram", shape, dt, kind="ExternalOutput").ap())
    gnn_moe_gcn_int8_kernel(nc, *args)
    r = _run(nc, [arrays], core_ids=[0])
    got = tuple(r.results[0][f"out_{i}_dram"] for i in range(len(_OUTS)))
    return got[0]
```
